# Optimizing a Trainium2 kernel written in Bass

```python
import numpy as np
import jax
import jax.numpy as jnp

def _softmax(x, axis=-1):
    return jax.nn.softmax(x, axis=axis)

def _gelu(x):
    return jax.nn.gelu(x, approximate=True)

def _silu(x):
    return jax.nn.silu(x)

def _sigmoid(x):
    return jax.nn.sigmoid(x)

def _layernorm(x, axis=-1, eps=1e-05):
    m = jnp.mean(x, axis=axis, keepdims=True)
    v = jnp.var(x, axis=axis, keepdims=True)
    return (x - m) / jnp.sqrt(v + eps)

def _scatter_add(tgt, idx, src, axis=0):
    return tgt.at[idx].add(src)

def _segment_sum(src, seg, n):
    return jax.ops.segment_sum(src, seg, n)
kernel_name = 'mk_xattn_ffn_d1_seqx_r4_6e8ebe'

def setup_inputs(seed: int=0):
    np.random.seed(seed)
    _w = jnp.asarray

    def _rec_inputs():
        import jax
        import jax.numpy as jnp
        _rk = jax.random.key(seed)
        x = -0.0002928 + 1 * jax.random.normal(jax.random.fold_in(_rk, 1), (32, 128, 256), jnp.float32)
        _lenS = 128 - jax.random.randint(jax.random.fold_in(_rk, 7), (32,), 0, max(1, 128 // 4) + 1, jnp.int32)
        _lenS2 = 128 - jax.random.randint(jax.random.fold_in(_rk, 8), (32,), 0, max(1, 128 // 4) + 1, jnp.int32)
        _ctx_1024P = jax.random.normal(jax.random.fold_in(_rk, 11), (32, 16, 256), jnp.float32)
        _ctx_1024c = jax.random.dirichlet(jax.random.fold_in(_rk, 511), 0.3 * jnp.ones((16,), jnp.float32), (32, 128))
        _ctx_1024t = jnp.einsum('bsk,bkd->bsd', _ctx_1024c, _ctx_1024P)
        _ctx_1024t = _ctx_1024t * jax.lax.rsqrt(jnp.mean(jnp.square(_ctx_1024t)) + 1e-12) * 0.953939
        ctx_1024 = -1.39393e-06 + 0.999914 * (_ctx_1024t + 0.3 * jax.random.normal(jax.random.fold_in(_rk, 611), (32, 128, 256), jnp.float32))
        return (x, ctx_1024)
    x, ctx_1024 = _rec_inputs()

    def _L0_xattn_setup():
        import jax, jax.numpy as jnp
        import numpy as np
        import math
        EMBED_DIM = 256
        NUM_HEADS = 16
        HEAD_DIM = EMBED_DIM // NUM_HEADS
        BLOCK = 64
        SPARSITY = 0.05
        BATCH = 2
        SEQ = 512

        def _block_pattern(seq_len, block_size, sparsity_ratio, is_causal):
            nb = seq_len // block_size
            total = nb * nb
            keep = int(total * (1.0 - sparsity_ratio))
            idx = [(i, i) for i in range(nb)]
            band = max(1, int(math.sqrt(keep - nb) / 2))
            for i in range(nb):
                for o in range(1, band + 1):
                    if i + o < nb:
                        idx.append((i, i + o))
                        if not is_causal:
                            idx.append((i + o, i))
                    if not is_causal and i - o >= 0:
                        idx.append((i, i - o))
            for skip in (2, 4, 8, 16):
                if len(idx) >= keep:
                    break
                for i in range(0, nb - skip, skip):
                    if len(idx) < keep:
                        idx.append((i, i + skip))
                        if not is_causal and len(idx) < keep:
                            idx.append((i + skip, i))
            uniq = sorted(set(idx))
            if is_causal:
                uniq = [(r, c) for r, c in uniq if r >= c]
            uniq = uniq[:keep]
            rows = np.array([r for r, c in uniq], dtype=np.int32)
            cols = np.array([c for r, c in uniq], dtype=np.int32)
            return (rows, cols)
        ROWS, COLS = _block_pattern(SEQ, BLOCK, SPARSITY, is_causal=False)
        rng = jax.random.key(seed)
        ks = jax.random.split(rng, 7)
        wscale = EMBED_DIM ** (-0.5)
        return {'query': jax.random.normal(ks[0], (BATCH, SEQ, EMBED_DIM), jnp.float32), 'key': jax.random.normal(ks[1], (BATCH, SEQ, EMBED_DIM), jnp.float32), 'value': jax.random.normal(ks[2], (BATCH, SEQ, EMBED_DIM), jnp.float32), 'Wq': jax.random.normal(ks[3], (EMBED_DIM, EMBED_DIM), jnp.float32) * wscale, 'Wk': jax.random.normal(ks[4], (EMBED_DIM, EMBED_DIM), jnp.float32) * wscale, 'Wv': jax.random.normal(ks[5], (EMBED_DIM, EMBED_DIM), jnp.float32) * wscale, 'Wo': jax.random.normal(ks[6], (EMBED_DIM, EMBED_DIM), jnp.float32) * wscale}
    _L0_xattn_all = _L0_xattn_setup()
    _L0_xattn_in = {k: v for k, v in _L0_xattn_all.items() if k in ('Wq', 'Wk', 'Wv', 'Wo')}
    del _L0_xattn_all

    def _L0_ffn_setup():
        import jax, jax.numpy as jnp
        import numpy as np
        TOP_K = 2
        key = jax.random.key(seed)
        k0, k1, k2, k3 = jax.random.split(key, 4)
        B, T, C, E, F = (4, 512, 256, 8, 1024)
        x = jax.random.normal(k0, (B, T, C), dtype=jnp.float32)
        gate_w = jax.random.normal(k1, (C, E), dtype=jnp.float32) * 0.02
        w1 = jax.random.normal(k2, (E, C, F), dtype=jnp.float32) * 0.02
        w2 = jax.random.normal(k3, (E, F, C), dtype=jnp.float32) * 0.02
        return {'x': x, 'gate_w': gate_w, 'w1': w1, 'w2': w2}
    _L0_ffn_all = _L0_ffn_setup()
    _L0_ffn_in = {k: v for k, v in _L0_ffn_all.items() if k in ('gate_w', 'w1', 'w2')}
    del _L0_ffn_all
    return {'x': x, 'ctx_1024': ctx_1024, 'L0_xattn_Wq': _L0_xattn_in['Wq'], 'L0_xattn_Wk': _L0_xattn_in['Wk'], 'L0_xattn_Wv': _L0_xattn_in['Wv'], 'L0_xattn_Wo': _L0_xattn_in['Wo'], 'L0_ffn_gate_w': _L0_ffn_in['gate_w'], 'L0_ffn_w1': _L0_ffn_in['w1'], 'L0_ffn_w2': _L0_ffn_in['w2']}

def reference(x, ctx_1024, L0_xattn_Wq, L0_xattn_Wk, L0_xattn_Wv, L0_xattn_Wo, L0_ffn_gate_w, L0_ffn_w1, L0_ffn_w2):
    import jax
    import jax.numpy as jnp

    def _L0_xattn_ref(query, key, value, Wq, Wk, Wv, Wo):
        import jax, jax.numpy as jnp
        import numpy as np
        import math
        EMBED_DIM = 256
        NUM_HEADS = 16
        HEAD_DIM = EMBED_DIM // NUM_HEADS
        BLOCK = 64
        SPARSITY = 0.05
        BATCH = 2
        SEQ = 512

        def _block_pattern(seq_len, block_size, sparsity_ratio, is_causal):
            nb = seq_len // block_size
            total = nb * nb
            keep = int(total * (1.0 - sparsity_ratio))
            idx = [(i, i) for i in range(nb)]
            band = max(1, int(math.sqrt(keep - nb) / 2))
            for i in range(nb):
                for o in range(1, band + 1):
                    if i + o < nb:
                        idx.append((i, i + o))
                        if not is_causal:
                            idx.append((i + o, i))
                    if not is_causal and i - o >= 0:
                        idx.append((i, i - o))
            for skip in (2, 4, 8, 16):
                if len(idx) >= keep:
                    break
                for i in range(0, nb - skip, skip):
                    if len(idx) < keep:
                        idx.append((i, i + skip))
                        if not is_causal and len(idx) < keep:
                            idx.append((i + skip, i))
            uniq = sorted(set(idx))
            if is_causal:
                uniq = [(r, c) for r, c in uniq if r >= c]
            uniq = uniq[:keep]
            rows = np.array([r for r, c in uniq], dtype=np.int32)
            cols = np.array([c for r, c in uniq], dtype=np.int32)
            return (rows, cols)
        ROWS, COLS = _block_pattern(SEQ, BLOCK, SPARSITY, is_causal=False)
        B, S, E = query.shape
        nb = S // BLOCK
        scale = HEAD_DIM ** (-0.5)

        def proj_blocks(x, W):
            h = (x @ W.T).reshape(B, S, NUM_HEADS, HEAD_DIM).transpose(0, 2, 1, 3)
            return h.reshape(B, NUM_HEADS, nb, BLOCK, HEAD_DIM)
        qb = proj_blocks(query, Wq)
        kb = proj_blocks(key, Wk)
        vb = proj_blocks(value, Wv)
        rows = jnp.asarray(ROWS)
        cols = jnp.asarray(COLS)
        qg = qb[:, :, rows]
        kg = kb[:, :, cols]
        vg = vb[:, :, cols]
        scores = jnp.einsum('bhpqd,bhpkd->bhpqk', qg, kg) * scale
        attn = jax.nn.softmax(scores, axis=-1)
        ob = jnp.einsum('bhpqk,bhpkd->bhpqd', attn, vg)
        acc = jax.ops.segment_sum(ob.transpose(2, 0, 1, 3, 4), rows, num_segments=nb)
        out = acc.transpose(1, 2, 0, 3, 4).reshape(B, NUM_HEADS, S, HEAD_DIM)
        out = out.transpose(0, 2, 1, 3).reshape(B, S, E)
        return out @ Wo.T

    def _L0_ffn_ref(x, gate_w, w1, w2):
        import jax, jax.numpy as jnp
        import numpy as np
        TOP_K = 2
        E = gate_w.shape[-1]
        probs = jax.nn.softmax(x @ gate_w, axis=-1)
        topw, topi = jax.lax.top_k(probs, TOP_K)
        topw = topw / topw.sum(axis=-1, keepdims=True)
        combine = (jax.nn.one_hot(topi, E, dtype=x.dtype) * topw[..., None]).sum(axis=-2)

        def body(acc, params):
            w1_i, w2_i, cw = params
            h = jax.nn.gelu(x @ w1_i, approximate=False)
            return (acc + cw[..., None] * (h @ w2_i), None)
        acc0 = jnp.zeros_like(x)
        out, _ = jax.lax.scan(body, acc0, (w1, w2, jnp.moveaxis(combine, -1, 0)))
        return out
    x = x + _L0_xattn_ref(_layernorm(x, axis=-1), ctx_1024, ctx_1024, L0_xattn_Wq, L0_xattn_Wk, L0_xattn_Wv, L0_xattn_Wo)
    x = x + _L0_ffn_ref(_layernorm(x, axis=-1), L0_ffn_gate_w, L0_ffn_w1, L0_ffn_w2)
    return x

_drawn_inputs = setup_inputs


def setup_inputs(seed=0):
    import zlib

    import numpy as np

    out = dict(_drawn_inputs(seed))
    spreads = {}
    factors = {}
    for name, (base, spread) in spreads.items():
        noise = np.random.default_rng([zlib.crc32(name.encode()), seed]).standard_normal(out[name].shape)
        drawn = base * np.exp(spread * noise) if base else spread * noise
        out[name] = jnp.asarray(drawn.astype(out[name].dtype))
    for name, factor in factors.items():
        out[name] = (out[name] * factor).astype(out[name].dtype)
    return out
```

```python
import math
from contextlib import ExitStack

import concourse.bass as bass
import numpy as np
from concourse import mybir

F32, F16 = mybir.dt.float32, mybir.dt.float16
I32, U32 = mybir.dt.int32, mybir.dt.uint32
ACT, ALU, AX = mybir.ActivationFunctionType, mybir.AluOpType, mybir.AxisListType


def key_block_counts(batch_blocks):
    seq, block = 512, 64
    nb = seq // block
    total = nb * nb
    keep = int(total * (1.0 - 0.05))
    idx = [(i, i) for i in range(nb)]
    band = max(1, int(math.sqrt(keep - nb) / 2))
    for i in range(nb):
        for o in range(1, band + 1):
            if i + o < nb:
                idx += [(i, i + o), (i + o, i)]
            if i - o >= 0:
                idx.append((i, i - o))
    for skip in (2, 4, 8, 16):
        if len(idx) >= keep:
            break
        for i in range(0, nb - skip, skip):
            if len(idx) < keep:
                idx.append((i, i + skip))
                if len(idx) < keep:
                    idx.append((i + skip, i))
    pairs = sorted(set(idx))[:keep]
    counts = np.zeros((batch_blocks, batch_blocks), int)
    for r, c in pairs:
        if r < batch_blocks:
            counts[r, min(c, batch_blocks - 1)] += 1
    return counts


def build(nc, x, ctxt, wq, wk, wv, wo, gate_w, w1, w2, out):
    B, S, E = x.shape
    P = 128
    assert S == P and E == 2 * P
    EC = E // P
    D = 16
    H = E // D
    HH = H // 2
    BLK = 64
    NX = gate_w.shape[1]
    F = w1.shape[2]
    FC = F // P
    T = B * S
    G4 = 4
    NG = B // G4
    SLOTS = 256
    NT = 2 * T // SLOTS + NX - 1
    TCOL = T // P
    LCOL = NX * TCOL
    EPS = 1e-5
    VW = D + 1
    counts = key_block_counts(S // BLK)
    WSZ = NX * EC * F
    P_SHIFT = 12
    assert NT % 3 == 0

    qd = nc.dram_tensor("q_split", (B, 2, E, S), F16).ap()
    kd = nc.dram_tensor("k_split", (B, 2, E, S), F16).ap()
    vd = nc.dram_tensor("v_split", (B, S, 2 * H * VW), F16).ap()
    xs = nc.dram_tensor("x2_split", (T, 2 * E), F16).ap()
    ys = nc.dram_tensor("expert_out", (2 * T, E), F32).ap()

    ctx = ExitStack()
    with ctx:
        def sb(name, shape, dt):
            return ctx.enter_context(nc.sbuf_tensor(name, shape, dt))

        def pb(name):
            return ctx.enter_context(nc.psum_tensor(name, [P, 512], F32))

        WS = sb("expert_weights", [P, 4 * WSZ], F16)
        w1h, w1l, w2h, w2l = (WS[:, i * WSZ:(i + 1) * WSZ] for i in range(4))
        WSF = WS[:, :].bitcast(F32)
        xres = sb("residual", [P, B, E], F32)
        R = sb("phase_region", [P, 8192], F32)
        region_at = [0]

        def carve(n, dt):
            size = n * (4 if dt in (F32, I32, U32) else 2)
            a = region_at[0]
            region_at[0] += size // 4
            assert region_at[0] <= 8192
            v = R[:, a:region_at[0]]
            return v if dt == F32 else v.bitcast(dt)

        aux = sb("beside_region", [P, 3072], F32)
        aux_at = [0]

        def beside(n, dt):
            size = n * (4 if dt in (F32, I32, U32) else 2)
            a = aux_at[0]
            aux_at[0] += size // 4
            assert aux_at[0] <= 3072
            v = aux[:, a:aux_at[0]]
            return v if dt == F32 else v.bitcast(dt)

        identf = sb("identf", [P, P], F32)
        identh = sb("identh", [P, P], F16)
        absmax = sb("absmax", [P, 8], F32)
        gmax = sb("gmax", [P, 8], F32)
        pw = sb("pow2", [P, 8], F32)
        sc = sb("to_fp16_scale", [P, 8], F32)
        CTX, WQ, WK, WV, WO, WG, W1, W2 = 4, 0, 1, 2, 3, 5, 6, 7
        s_attn = sb("s_attn", [P, 1], F32)
        s_res = sb("s_res", [P, 1], F32)
        s_gate = sb("s_gate", [P, 1], F32)
        s_pre = sb("s_pre", [P, 1], F32)
        s_hid = sb("s_hid", [P, 1], F32)
        s_out = sb("s_out", [P, 1], F32)
        eps1 = sb("eps1", [P, 1], F32)
        pbias = sb("pbias", [P, 1], F32)
        zero1 = sb("zero1", [P, 1], F32)
        wcoef = sb("wcoef", [P, 2], F32)
        WT = sb("attn_weights", [P, 2, 4, EC, E], F16)
        gT = sb("gate_weights", [P, 2, EC, NX], F16)
        st = sb("bn_st", [P, 2, G4, 6], F32)
        mv = sb("bn_mv", [P, 2, G4, 2], F32)
        sd = sb("std", [P, 2, G4], F32)
        rstd = sb("rstd", [P, 2, G4], F32)
        MX = sb("top_logit", [P, B, 2], F32)
        IX = sb("top_expert", [P, B, 2], F32)
        wt_region = WT[:].rearrange("p s w c n -> p (s w c n)").bitcast(I32)
        listT = wt_region[:, 0:2 * (LCOL + 2)].rearrange("p (n a) -> p n a", a=2)
        iota_i = wt_region[:, 2 * (LCOL + 2):2 * (LCOL + 2) + LCOL]
        gi = wt_region[:, 1024:1024 + 3 * 2 * SLOTS // P].rearrange("p (u n) -> p u n", u=3)
        tmap = sb("tile_map", [1, 2, NT + 1], I32)
        coef = sb("combine_coef", [P, B, 2], F32)
        psb = [pb(f"bank{i}") for i in range(8)]

        passed_dve = ctx.enter_context(nc.semaphore("passed_dve"))
        passed_pool = ctx.enter_context(nc.semaphore("passed_pool"))
        phases = iter("ABCDEFGHIJ")

        def sems(*names):
            tag = next(phases)
            return [ctx.enter_context(nc.semaphore(f"{tag}_{n}")) for n in names]

        def pow2_scales(dve, lo, hi, chain, done):
            n = [0]

            def link(ins):
                n[0] += 1
                ins.then_inc(chain, 1)
                dve.wait_ge(chain, n[0])

            link(nc.vector.tensor_scalar(pw[:, lo:hi], gmax[:, lo:hi], 2.0 ** -30, 2.0 ** 30, ALU.max, ALU.min))
            link(nc.vector.tensor_scalar(pw[:, lo:hi].bitcast(I32), pw[:, lo:hi].bitcast(I32),
                                         0x7F800000, None, ALU.bitwise_and))
            link(nc.vector.tensor_scalar(sc[:, lo:hi].bitcast(I32), pw[:, lo:hi].bitcast(I32),
                                         -1.0, float((254 + 14) << 23), ALU.mult, ALU.add))
            return link

        region_at[0] = 0
        wst = carve(4 * EC * E, F32).rearrange("p (w c n) -> p w c n", w=4, c=EC)
        gst = carve(EC * NX, F32).rearrange("p (c n) -> p c n", c=EC)
        ctx_all = WSF[:, 0:B * E].rearrange("p (b e) -> p b e", b=B)
        (weights_in, gate_in, ctx_in, x_in, absmax_done, gmax_done, chain, scales_done, ident_set, ident_done,
         weights_T, weights_hi, weights_split, consts_done, gate_hi) = sems(
            "weights_in", "gate_in", "ctx_in", "x_in", "absmax_done", "gmax_done", "chain", "scales_done",
            "ident_set", "ident_done", "weights_T", "weights_hi", "weights_split", "consts_done", "gate_hi")
        with nc.Block() as block:
            @block.sync
            def _(sp):
                for n, w in enumerate((wq, wk, wv, wo)):
                    sp.dma_start(wst[:, n], w.rearrange("(c p) n -> p c n", p=P)).then_inc(weights_in, 16)
                sp.dma_start(gst, gate_w.rearrange("(c p) n -> p c n", p=P)).then_inc(gate_in, 16)
                for q in range(4):
                    b0, b1 = q * B // 4, (q + 1) * B // 4
                    sp.dma_start(ctx_all[:, b0:b1], ctxt[b0:b1].rearrange("b s e -> s b e")).then_inc(ctx_in, 16)
                for q in range(4):
                    b0, b1 = q * B // 4, (q + 1) * B // 4
                    sp.dma_start(xres[:, b0:b1], x[b0:b1].rearrange("b s e -> s b e")).then_inc(x_in, 16)
                sp.wait_ge(x_in, 64)

            @block.gpsimd
            def _(pool):
                nc.gpsimd.memset(zero1[:, :], 0.0).then_inc(consts_done, 1)
                for m in (identf, identh):
                    nc.gpsimd.memset(m[:, :], 0.0).then_inc(ident_set, 1)
                pool.wait_ge(ident_set, 2)
                for m in (identf, identh):
                    nc.gpsimd.affine_select(out=m[:, :], in_=m[:, :], compare_op=ALU.not_equal, fill=1.0, base=0,
                                            pattern=[[-1, P]], channel_multiplier=1).then_inc(ident_done, 1)
                nc.gpsimd.memset(eps1[:, :], EPS * 2.0 ** -22).then_inc(consts_done, 1)
                nc.gpsimd.memset(pbias[:, :], P_SHIFT * math.log(2.0)).then_inc(consts_done, 1)
                pool.wait_ge(consts_done, 3 + counts.size)
                pool.wait_ge(absmax_done, 3)
                nc.gpsimd.partition_all_reduce(gmax[:, 0:6], absmax[:, 0:6], P, bass.bass_isa.ReduceOp.max)\
                    .then_inc(gmax_done, 1)

            @block.vector
            def _(dve):
                for r in range(S // BLK):
                    for c in range(S // BLK):
                        nc.vector.memset(wcoef[r * BLK:(r + 1) * BLK, c:c + 1], float(counts[r, c]) / 8.0)\
                            .then_inc(consts_done, 1)
                dve.wait_ge(weights_in, 64)
                nc.vector.tensor_reduce(absmax[:, 0:4], wst.rearrange("p w c n -> p w (c n)"), AX.X, ALU.max,
                                        apply_absolute_value=True).then_inc(absmax_done, 1)
                dve.wait_ge(gate_in, 16)
                nc.vector.tensor_reduce(absmax[:, WG:WG + 1], gst, AX.XY, ALU.max,
                                        apply_absolute_value=True).then_inc(absmax_done, 1)
                dve.wait_ge(ctx_in, 64)
                nc.vector.tensor_reduce(absmax[:, CTX:CTX + 1], ctx_all, AX.XY, ALU.max,
                                        apply_absolute_value=True).then_inc(absmax_done, 1)
                dve.wait_ge(gmax_done, 1)
                link = pow2_scales(dve, 0, 6, chain, None)
                nc.vector.tensor_tensor(s_gate[:, :], pw[:, WV:WV + 1], pw[:, WO:WO + 1], ALU.mult)
                link(nc.vector.tensor_tensor(s_attn[:, :], pw[:, WQ:WQ + 1], pw[:, WK:WK + 1], ALU.mult))
                nc.vector.tensor_scalar(s_res[:, :], s_gate[:, :], pw[:, CTX:CTX + 1], 2.0 ** -16, ALU.mult, ALU.mult)
                link(nc.vector.tensor_scalar(s_attn[:, :], s_attn[:, :], pw[:, CTX:CTX + 1],
                                             2.0 ** -7 * D ** -0.5, ALU.mult, ALU.mult))
                nc.vector.tensor_scalar(s_gate[:, :], pw[:, WG:WG + 1], 2.0 ** -25, None, ALU.mult)\
                    .then_inc(scales_done, 1)
                nc.vector.tensor_scalar(gT[:, 0], gst, sc[:, WG:WG + 1], None, ALU.mult).then_inc(gate_hi, 1)
                dve.wait_ge(gate_hi, 1)
                nc.vector.scalar_tensor_tensor(gT[:, 1], gst, sc[:, WG:WG + 1], gT[:, 0], ALU.mult, ALU.subtract)\
                    .then_inc(weights_split, 1)
                for n in range(4):
                    dve.wait_ge(weights_hi, n + 1)
                    nc.vector.scalar_tensor_tensor(
                        WT[:, 1, n].rearrange("p c n -> p (c n)"), psb[n][:, :], sc[:, n:n + 1],
                        WT[:, 0, n].rearrange("p c n -> p (c n)"), ALU.mult, ALU.subtract).then_inc(weights_split, 1)
                dve.wait_ge(weights_split, 5)

            @block.tensor
            def _(pe):
                pe.wait_ge(ident_done, 2)
                pe.wait_ge(weights_in, 64)
                for n in range(4):
                    for oc in range(EC):
                        for ic in range(EC):
                            last = nc.tensor.transpose(psb[n][:, ic * E + oc * P:ic * E + (oc + 1) * P],
                                                       wst[:, n, oc, ic * P:(ic + 1) * P], identf[:, :])
                    last.then_inc(weights_T, 1)

            @block.scalar
            def _(act):
                act.wait_ge(scales_done, 1)
                for n in range(4):
                    act.wait_ge(weights_T, n + 1)
                    nc.scalar.activation(WT[:, 0, n].rearrange("p c n -> p (c n)"), psb[n][:, :], ACT.Copy,
                                         scale=sc[:, n:n + 1]).then_inc(weights_hi, 1)

        region_at[0] = 0
        cst = [carve(G4 * E, F32).rearrange("p (b e) -> p b e", b=G4) for _ in range(2)]
        xh = carve(G4 * E, F32).rearrange("p (b e) -> p b e", b=G4)
        inT = carve(2 * 2 * EC * 512, F16).rearrange("p (w s c n) -> p w s c n", w=2, s=2, c=EC)
        qk = carve(2 * 2 * EC * 512, F16).rearrange("p (w s c n) -> p w s c n", w=2, s=2, c=EC)
        vS = beside(G4 * 2 * H * VW, F16).rearrange("p (b s h v) -> p b s h v", b=G4, s=2, h=H)
        (ctx_ld0, ctx_ld1, mv_done, sd_done, rstd_done, xh_done, x_T, c_T, x_hi, x_split, c_hi, c_split,
         q_mm, k_mm, v_mm, q_hi, k_hi, v_hi, q_split, k_split, v_split, stored, ones_set, bn_done) = sems(
            "ctx_ld0", "ctx_ld1", "mv_done", "sd_done", "rstd_done", "xh_done", "x_T", "c_T", "x_hi", "x_split",
            "c_hi", "c_split", "q_mm", "k_mm", "v_mm", "q_hi", "k_hi", "v_hi", "q_split", "k_split", "v_split",
            "stored", "ones_set", "bn_done")
        ctx_ld = [ctx_ld0, ctx_ld1]
        NSTORE = 9

        def groups(eng, body):
            for j in range(2):
                body(j, 0, j, True)
            with eng.Fori(1, NG // 2) as i:
                for j in range(2):
                    body(i * 2 + j, i, j, False)

        with nc.Block() as block:
            @block.sync
            def _(sp):
                def load(g, j):
                    sp.dma_start(cst[j], ctxt[bass.ds(g * G4, G4)].rearrange("b s e -> s b e")).then_inc(ctx_ld[j], 16)

                def store(g):
                    for w, (dst, ready) in enumerate(((qd, q_split), (kd, k_split))):
                        sp.wait_ge(ready, g + 1)
                        for s in range(2):
                            for c in range(EC):
                                sp.dma_start(dst[bass.ds(g * G4, G4), s, c * P:(c + 1) * P].rearrange("b p n -> p b n"),
                                             qk[:, w, s, c].rearrange("p (b n) -> p b n", b=G4)).then_inc(stored, 16)
                    sp.wait_ge(v_split, g + 1)
                    sp.dma_start(vd[bass.ds(g * G4, G4)].rearrange("b p n -> p b n"),
                                 vS.rearrange("p b s h v -> p b (s h v)")).then_inc(stored, 16)

                def body(g, i, j, first):
                    if not (first and j == 0):
                        store(g - 1)
                        sp.wait_ge(c_T, g - 1) if not first else None
                    load(g, j)

                groups(sp, body)
                store(NG - 1)
                sp.wait_ge(stored, 16 * NSTORE * NG)

            @block.vector
            def _(dve):
                nc.vector.memset(vS[:, :, 0, :, D:VW], 1.0)
                nc.vector.memset(vS[:, :, 1, :, D:VW], 0.0).then_inc(ones_set, 1)

                def body(g, i, j, first):
                    gfirst = first and j == 0
                    for b in range(G4):
                        xb = xres[:, g * G4 + b, :] if first else xres[:, bass.ds(g * G4 + b, 1), :].rearrange("p a e -> p (a e)")
                        last = nc.vector.bn_stats(st[:, j, b, :], xb)
                    last.then_inc(bn_done, 1)
                    dve.wait_ge(bn_done, g + 1)
                    dve.sem_inc(passed_dve, 1)
                    for b in range(G4):
                        last = nc.vector.bn_aggr(mv[:, j, b, :], st[:, j, b, :])
                    last.then_inc(mv_done, 1)
                    dve.wait_ge(sd_done, g + 1)
                    nc.vector.reciprocal(rstd[:, j, :], sd[:, j, :]).then_inc(rstd_done, 1)
                    dve.wait_ge(rstd_done, g + 1)
                    if not gfirst:
                        dve.wait_ge(x_T, g)
                    for b in range(G4):
                        xb = xres[:, g * G4 + b, :] if first else xres[:, bass.ds(g * G4 + b, 1), :].rearrange("p a e -> p (a e)")
                        last = nc.vector.tensor_scalar(xh[:, b, :], xb, mv[:, j, b, 0:1], rstd[:, j, b:b + 1],
                                                       ALU.subtract, ALU.mult)
                    last.then_inc(xh_done, 1)
                    dve.wait_ge(x_hi, g + 1)
                    for c in range(EC):
                        last = nc.vector.tensor_tensor(inT[:, 0, 1, c], psb[c][:, :], inT[:, 0, 0, c], ALU.subtract)
                    last.then_inc(x_split, 1)
                    dve.wait_ge(c_hi, g + 1)
                    for c in range(EC):
                        last = nc.vector.scalar_tensor_tensor(inT[:, 1, 1, c], psb[2 + c][:, :], sc[:, CTX:CTX + 1],
                                                              inT[:, 1, 0, c], ALU.mult, ALU.subtract)
                    last.then_inc(c_split, 1)
                    for w, (hi, split, k) in enumerate(((q_hi, q_split, 2.0 ** -21), (k_hi, k_split, 2.0 ** -25))):
                        dve.wait_ge(hi, g + 1)
                        for c in range(EC):
                            last = nc.vector.scalar_tensor_tensor(qk[:, w, 1, c], psb[4 + 2 * w + c][:, :], k,
                                                                  qk[:, w, 0, c], ALU.mult, ALU.subtract)
                        last.then_inc(split, 1)
                    dve.wait_ge(v_hi, g + 1)
                    for b in range(G4):
                        last = nc.vector.scalar_tensor_tensor(
                            vS[:, b, 1, :, 0:D],
                            psb[b // 2][:, (b % 2) * E:(b % 2 + 1) * E].rearrange("p (h d) -> p h d", h=H),
                            2.0 ** -23, vS[:, b, 0, :, 0:D], ALU.mult, ALU.subtract)
                    last.then_inc(v_split, 1)

                groups(dve, body)

            @block.scalar
            def _(act):
                def body(g, i, j, first):
                    gfirst = first and j == 0
                    act.wait_ge(mv_done, g + 1)
                    nc.scalar.activation(sd[:, j, :], mv[:, j, :, 1], ACT.Sqrt, bias=eps1[:, :], scale=2.0 ** -22)\
                        .then_inc(sd_done, 1)
                    act.wait_ge(x_T, g + 1)
                    if not gfirst:
                        act.wait_ge(q_mm, g)
                    for c in range(EC):
                        last = nc.scalar.activation(inT[:, 0, 0, c], psb[c][:, :], ACT.Copy)
                    last.then_inc(x_hi, 1)
                    act.wait_ge(c_T, g + 1)
                    if not gfirst:
                        act.wait_ge(v_mm, g)
                    for c in range(EC):
                        last = nc.scalar.activation(inT[:, 1, 0, c], psb[2 + c][:, :], ACT.Copy, scale=sc[:, CTX:CTX + 1])
                    last.then_inc(c_hi, 1)
                    for w, (mm, hi, k) in enumerate(((q_mm, q_hi, 2.0 ** -21), (k_mm, k_hi, 2.0 ** -25))):
                        act.wait_ge(mm, g + 1)
                        if w == 0 and not gfirst:
                            act.wait_ge(stored, g * (16 * NSTORE))
                        for c in range(EC):
                            last = nc.scalar.activation(qk[:, w, 0, c], psb[4 + 2 * w + c][:, :], ACT.Copy, scale=k)
                        last.then_inc(hi, 1)
                    act.wait_ge(v_mm, g + 1)
                    act.wait_ge(ones_set, 1)
                    for b in range(G4):
                        last = nc.scalar.activation(
                            vS[:, b, 0, :, 0:D],
                            psb[b // 2][:, (b % 2) * E:(b % 2 + 1) * E].rearrange("p (h d) -> p h d", h=H),
                            ACT.Copy, scale=2.0 ** -23)
                    last.then_inc(v_hi, 1)

                groups(act, body)

            @block.tensor
            def _(pe):
                def project(bank0, w, src):
                    for m in range(EC):
                        terms = [(a, b, c) for a, b in ((0, 0), (0, 1), (1, 0)) for c in range(EC)]
                        for n, (a, b, c) in enumerate(terms):
                            last = nc.tensor.matmul(psb[bank0 + m][:, :], WT[:, a, w, c, m * P:(m + 1) * P],
                                                    inT[:, src, b, c], start=(n == 0), stop=(n == len(terms) - 1))
                    return last

                def body(g, i, j, first):
                    gfirst = first and j == 0
                    pe.wait_ge(ctx_ld[j], (i + 1) * 16)
                    if not gfirst:
                        pe.wait_ge(c_split, g)
                    for c in range(EC):
                        for b in range(G4):
                            last = nc.tensor.transpose(psb[2 + c][:, b * P:(b + 1) * P],
                                                       cst[j][:, b, c * P:(c + 1) * P], identf[:, :])
                    last.then_inc(c_T, 1)
                    pe.wait_ge(xh_done, g + 1)
                    if not gfirst:
                        pe.wait_ge(v_split, g)
                    for c in range(EC):
                        for b in range(G4):
                            last = nc.tensor.transpose(psb[c][:, b * P:(b + 1) * P],
                                                       xh[:, b, c * P:(c + 1) * P], identf[:, :])
                    last.then_inc(x_T, 1)
                    pe.wait_ge(x_split, g + 1)
                    if not gfirst:
                        pe.wait_ge(q_split, g)
                    project(4, 0, 0).then_inc(q_mm, 1)
                    pe.wait_ge(c_split, g + 1)
                    if not gfirst:
                        pe.wait_ge(k_split, g)
                    project(6, 1, 1).then_inc(k_mm, 1)
                    for b in range(G4):
                        terms = [(a, s, c) for a, s in ((0, 0), (0, 1), (1, 0)) for c in range(EC)]
                        for n, (a, s, c) in enumerate(terms):
                            last = nc.tensor.matmul(psb[b // 2][:, (b % 2) * E:(b % 2 + 1) * E],
                                                    inT[:, 1, s, c, b * P:(b + 1) * P], WT[:, a, WV, c, :],
                                                    start=(n == 0), stop=(n == len(terms) - 1))
                    last.then_inc(v_mm, 1)

                groups(pe, body)

        region_at[0] = 0
        CH = 2048
        wstage = [carve(CH, F32) for _ in range(4)]
        NCH = WSZ // CH
        (w_all, w_absmax, w_gmax, w_scales, wchain, w_ld0, w_ld1, w_ld2, w_ld3, w_hi, w_split) = sems(
            "w_all", "w_absmax", "w_gmax", "w_scales", "wchain", "w_ld0", "w_ld1", "w_ld2", "w_ld3", "w_hi", "w_split")
        w_ld = [w_ld0, w_ld1, w_ld2, w_ld3]
        w_dram = [w1.rearrange("e (c p) n -> e p c n", p=P), w2.rearrange("e (c p) n -> e p c n", p=P)]
        w_rows = [EC, FC]

        with nc.Block() as block:
            @block.sync
            def _(sp):
                for m in range(2):
                    for e in range(NX):
                        sp.dma_start(WSF[:, (m * NX + e) * CH:(m * NX + e + 1) * CH]
                                     .rearrange("p (c n) -> p c n", c=w_rows[m]), w_dram[m][e]).then_inc(w_all, 16)
                for n in range(2 * NX):
                    if n >= 4:
                        sp.wait_ge(w_split, n - 3)
                    sp.dma_start(wstage[n % 4].rearrange("p (c n) -> p c n", c=w_rows[n // NX]),
                                 w_dram[n // NX][n % NX]).then_inc(w_ld[n % 4], 16)

            @block.vector
            def _(dve):
                dve.wait_ge(w_all, 16 * 2 * NX)
                for m in range(2):
                    nc.vector.tensor_reduce(absmax[:, W1 + m:W1 + m + 1], WSF[:, m * WSZ:(m + 1) * WSZ], AX.X, ALU.max,
                                            apply_absolute_value=True).then_inc(w_absmax, 1)
                dve.wait_ge(w_gmax, 1)
                link = pow2_scales(dve, W1, W2 + 1, wchain, None)
                nc.vector.tensor_scalar(s_pre[:, :], pw[:, W1:W1 + 1], 2.0 ** -25, None, ALU.mult)
                nc.vector.tensor_scalar(s_hid[:, :], sc[:, W1:W1 + 1], 2.0 ** -8, None, ALU.mult)
                link(nc.vector.tensor_tensor(s_out[:, :], pw[:, W1:W1 + 1], pw[:, W2:W2 + 1], ALU.mult))
                nc.vector.tensor_scalar(s_out[:, :], s_out[:, :], 2.0 ** -20, None, ALU.mult).then_inc(w_scales, 1)
                for n in range(2 * NX):
                    m, e = n // NX, n % NX
                    dve.wait_ge(w_hi, n + 1)
                    hi, lo = (w1h, w1l) if m == 0 else (w2h, w2l)
                    nc.vector.scalar_tensor_tensor(lo[:, e * CH:(e + 1) * CH], wstage[n % 4], sc[:, W1 + m:W1 + m + 1],
                                                   hi[:, e * CH:(e + 1) * CH], ALU.mult, ALU.subtract)\
                        .then_inc(w_split, 1)
                dve.wait_ge(w_split, 2 * NX)

            @block.gpsimd
            def _(pool):
                pool.wait_ge(w_absmax, 2)
                nc.gpsimd.partition_all_reduce(gmax[:, W1:W2 + 1], absmax[:, W1:W2 + 1], P, bass.bass_isa.ReduceOp.max)\
                    .then_inc(w_gmax, 1)

            @block.scalar
            def _(act):
                act.wait_ge(w_scales, 1)
                for n in range(2 * NX):
                    m, e = n // NX, n % NX
                    act.wait_ge(w_ld[n % 4], 16 * (n // 4 + 1))
                    hi = w1h if m == 0 else w2h
                    nc.scalar.activation(hi[:, e * CH:(e + 1) * CH], wstage[n % 4], ACT.Copy,
                                         scale=sc[:, W1 + m:W1 + m + 1]).then_inc(w_hi, 1)

        region_at[0] = 0
        UW = HH * P
        Kst = [carve(H * P, F16).rearrange("p (h n) -> p h n", h=H) for _ in range(2)]
        Qst = [carve(H * P, F16).rearrange("p (h n) -> p h n", h=H) for _ in range(2)]
        prob = [carve(UW, F32) for _ in range(2)]
        ph = carve(2 * 2 * UW, F16).rearrange("p (u s n) -> p u s n", u=2, s=2)
        aux_at[0] = 0
        VA = [beside(2 * 2 * H * VW, F16).rearrange("p (s k n) -> p s k n", s=2, k=2) for _ in range(2)]
        sel = beside(HH * P, F16).rearrange("p (h n) -> p h n", h=HH)
        mxu = beside(2 * 2 * HH, F32).rearrange("p (u n) -> p u n", u=2)
        negm = beside(2 * 4 * HH, F16).rearrange("p (u n) -> p u n", u=2)
        mT = beside(2 * P, F16).rearrange("p (u n) -> p u n", u=2)
        rec = beside(2 * 2 * HH, F32).rearrange("p (u n) -> p u n", u=2)
        ob = beside(E, F32)
        oT = beside(2 * EC * P, F16).rearrange("p (s c n) -> p s c n", s=2, c=EC)
        otmp = beside(2 * HH * D, F32)
        S0, ST0, PO, OT, MI = 0, 2, 4, 6, 7
        (ld0, ld1, zeroed, sel_set, sel_done, scores, max_done, negm_done, m_T, m_copied, scoresT, exp_done, p_hi,
         p_split, pv_done, normed, o_T, o_hi, o_split, o_proj, x1_done, dchain) = sems(
            "ld0", "ld1", "zeroed", "sel_set", "sel_done", "scores", "max_done", "negm_done", "m_T", "m_copied",
            "scoresT", "exp_done", "p_hi", "p_split", "pv_done", "normed", "o_T", "o_hi", "o_split", "o_proj",
            "x1_done", "dchain")
        ld = [ld0, ld1]
        NLD = 10
        MSC = 2.0 ** 15

        def batches(eng, body):
            for j in range(2):
                body(j, 0, j, True)
            with eng.Fori(1, B // 2) as i:
                for j in range(2):
                    body(i * 2 + j, i, j, False)

        with nc.Block() as block:
            @block.sync
            def _(sp):
                sp.wait_ge(zeroed, 6)

                def body(b, i, j, first):
                    if not first:
                        sp.wait_ge(pv_done, (b - 1) * 2)
                    q = qd[bass.ds(b, 1)].rearrange("a s (h d) n -> (a s) d h n", d=D)
                    k = kd[bass.ds(b, 1)].rearrange("a s (h d) n -> (a s) d h n", d=D)
                    for row, (sq, sk) in enumerate(((0, 0), (0, 1), (1, 0))):
                        sp.dma_start(Qst[j][row * D:(row + 1) * D], q[sq]).then_inc(ld[j], 16)
                        sp.dma_start(Kst[j][row * D:(row + 1) * D], k[sk]).then_inc(ld[j], 16)
                    for s in range(2):
                        for kb in range(2):
                            sp.dma_start(VA[j][kb * BLK:(kb + 1) * BLK, s, kb],
                                         vd[bass.ds(b, 1), kb * BLK:(kb + 1) * BLK, s * H * VW:(s + 1) * H * VW]
                                         .rearrange("a p n -> (a p) n")).then_inc(ld[j], 16)

                batches(sp, body)

            @block.gpsimd
            def _(pool):
                for j in range(2):
                    nc.gpsimd.memset(Kst[j], 0.0).then_inc(zeroed, 1)
                    nc.gpsimd.memset(Qst[j], 0.0).then_inc(zeroed, 1)
                    nc.gpsimd.memset(VA[j], 0.0).then_inc(zeroed, 1)
                nc.gpsimd.memset(mT, 0.0).then_inc(sel_set, 1)
                nc.gpsimd.memset(sel, 0.0).then_inc(sel_set, 1)
                pool.wait_ge(sel_set, 2)
                for s in range(2):
                    for kb in range(2):
                        v = sel[:, :, kb * BLK:(kb + 1) * BLK]
                        nc.gpsimd.affine_select(out=v, in_=v, compare_op=ALU.not_equal, fill=MSC,
                                                base=-(s * 2 * HH + kb), pattern=[[-2, HH], [0, BLK]],
                                                channel_multiplier=1).then_inc(sel_set, 1)
                        pool.wait_ge(sel_set, 3 + s * 2 + kb)
                nc.gpsimd.memset(negm, 0.0).then_inc(sel_done, 1)

                def body(b, i, j, first):
                    for h in range(2):
                        u = b * 2 + h
                        pool.wait_ge(p_hi, u + 1)
                        nc.gpsimd.tensor_tensor(ph[:, h, 1], prob[h], ph[:, h, 0], ALU.subtract).then_inc(p_split, 1)

                batches(pool, body)

            @block.vector
            def _(dve):
                def norm(u, h, first_ever):
                    dve.wait_ge(pv_done, u + 1)
                    po = psb[PO + h][:, 0:HH * 2 * VW].rearrange("p (h k v) -> p h k v", h=HH, k=2)
                    r = rec[:, h, :].rearrange("p (h k) -> p h k", k=2)
                    t = otmp.rearrange("p (h k d) -> p h k d", h=HH, k=2)
                    o = ob[:, h * HH * D:(h + 1) * HH * D].rearrange("p (h d) -> p h d", d=D)
                    nc.vector.reciprocal(r, po[:, :, :, D]).then_inc(dchain, 1)
                    dve.wait_ge(dchain, u * 3 + 1)
                    nc.vector.tensor_tensor(r, r, wcoef[:, :].unsqueeze(1).broadcast_to([P, HH, 2]), ALU.mult)\
                        .then_inc(dchain, 1)
                    dve.wait_ge(dchain, u * 3 + 2)
                    nc.vector.tensor_tensor(t, po[:, :, :, 0:D], r.unsqueeze(3).broadcast_to([P, HH, 2, D]), ALU.mult)\
                        .then_inc(dchain, 1)
                    dve.wait_ge(dchain, u * 3 + 3)
                    nc.vector.tensor_tensor(o, t[:, :, 0, :], t[:, :, 1, :], ALU.add).then_inc(normed, 1)

                def o_lo(b):
                    dve.wait_ge(o_hi, b + 1)
                    nc.vector.tensor_tensor(oT[:, 1].rearrange("p c n -> p (c n)"), psb[OT][:, 0:E],
                                            oT[:, 0].rearrange("p c n -> p (c n)"), ALU.subtract).then_inc(o_split, 1)

                def residual(b, static):
                    dve.wait_ge(o_proj, b + 1)
                    xb = xres[:, b, :] if static else xres[:, bass.ds(b, 1), :].rearrange("p a e -> p (a e)")
                    nc.vector.scalar_tensor_tensor(xb, psb[MI][:, 0:E], s_res[:, :], xb, ALU.mult, ALU.add)\
                        .then_inc(x1_done, 1)

                def body(b, i, j, first):
                    for h in range(2):
                        u = b * 2 + h
                        ufirst = first and j == 0 and h == 0
                        dve.wait_ge(scores, u + 1)
                        for n in range(2):
                            last = nc.vector.tensor_reduce(
                                mxu[:, h, n * HH:(n + 1) * HH],
                                psb[S0 + n][:, :].rearrange("p (g k) -> p g k", k=BLK), AX.X, ALU.max)
                        last.then_inc(max_done, 1)
                        dve.wait_ge(max_done, u + 1)
                        if not (first and j == 0):
                            dve.wait_ge(m_T, u - 1)
                        nc.vector.tensor_scalar(negm[:, h, 0:2 * HH], mxu[:, h, :], -1.0 / MSC, None, ALU.mult)\
                            .then_inc(negm_done, 1)
                        dve.wait_ge(negm_done, u * 2 + 1)
                        nc.vector.scalar_tensor_tensor(negm[:, h, 2 * HH:4 * HH], mxu[:, h, :], -1.0 / MSC,
                                                       negm[:, h, 0:2 * HH], ALU.mult, ALU.subtract)\
                            .then_inc(negm_done, 1)
                        if not ufirst:
                            if h == 1 or first:
                                norm(u - 1, 1 - h, False)
                            else:
                                norm(u - 1, 1, False)
                        if not (first and j == 0):
                            if h == 0:
                                o_lo(b - 1)
                            else:
                                residual(b - 1, first)

                dve.wait_ge(sel_done, 1)
                batches(dve, body)
                norm(2 * B - 1, 1, False)
                o_lo(B - 1)
                residual(B - 1, True)

            @block.scalar
            def _(act):
                act.wait_ge(sel_done, 1)

                def o_high(b):
                    act.wait_ge(o_T, b + 1)
                    nc.scalar.activation(oT[:, 0].rearrange("p c n -> p (c n)"), psb[OT][:, 0:E], ACT.Copy)\
                        .then_inc(o_hi, 1)

                def body(b, i, j, first):
                    for h in range(2):
                        u = b * 2 + h
                        bfirst = first and j == 0
                        act.wait_ge(m_T, u + 1)
                        if not bfirst:
                            act.wait_ge(scoresT, u - 1)
                        nc.scalar.activation(mT[0:4 * HH, h, :], psb[MI][0:4 * HH, 256:256 + P // 2].bitcast(F16), ACT.Copy)\
                            .then_inc(m_copied, 1)
                        act.wait_ge(scoresT, u + 1)
                        if not bfirst:
                            act.wait_ge(p_split, u - 1)
                        for n in range(2):
                            last = nc.scalar.activation(prob[h][:, n * 512:(n + 1) * 512], psb[ST0 + n][:, :], ACT.Exp,
                                                        bias=pbias[:, :], scale=s_attn[:, :])
                        last.then_inc(exp_done, 1)
                        act.wait_ge(exp_done, u + 1)
                        if not bfirst:
                            act.wait_ge(pv_done, u - 1)
                        nc.scalar.activation(ph[:, h, 0], prob[h], ACT.Copy).then_inc(p_hi, 1)
                        if h == 0 and not bfirst:
                            o_high(b - 1)

                batches(act, body)
                o_high(B - 1)

            @block.tensor
            def _(pe):
                pe.wait_ge(sel_done, 1)

                def pv(u, h, jv, ready):
                    pe.wait_ge(p_split, ready)
                    for hd in range(HH):
                        head = h * HH + hd
                        for n, (a, s) in enumerate(((0, 0), (1, 0), (0, 1))):
                            last = nc.tensor.matmul(psb[PO + h][:, hd * 2 * VW:(hd + 1) * 2 * VW],
                                                    ph[:, h, a, hd * P:(hd + 1) * P],
                                                    VA[jv][:, s, :, head * VW:(head + 1) * VW],
                                                    start=(n == 0), stop=(n == 2))
                    last.then_inc(pv_done, 1)

                def o_transpose(b):
                    pe.wait_ge(normed, b * 2 + 2)
                    for c in range(EC):
                        last = nc.tensor.transpose(psb[OT][:, c * P:(c + 1) * P], ob[:, c * P:(c + 1) * P], identf[:, :])
                    last.then_inc(o_T, 1)

                def o_project(b):
                    pe.wait_ge(o_split, b + 1)
                    terms = [(a, s, c) for a, s in ((0, 0), (0, 1), (1, 0)) for c in range(EC)]
                    for n, (a, s, c) in enumerate(terms):
                        last = nc.tensor.matmul(psb[MI][:, 0:E], oT[:, s, c], WT[:, a, WO, c, :],
                                                start=(n == 0), stop=(n == len(terms) - 1))
                    last.then_inc(o_proj, 1)

                def body(b, i, j, first):
                    for h in range(2):
                        u = b * 2 + h
                        bfirst = first and j == 0
                        ufirst = bfirst and h == 0
                        if h == 0:
                            pe.wait_ge(ld[j], (i + 1) * (16 * NLD))
                        for hd in range(HH):
                            head = h * HH + hd
                            if hd == 0 and not ufirst:
                                pe.wait_ge(max_done, u)
                            last = nc.tensor.matmul(psb[S0 + hd // 4][:, (hd % 4) * P:(hd % 4 + 1) * P],
                                                    Qst[j][:, head, :], Kst[j][:, head, :], start=True, stop=True)
                        last.then_inc(scores, 1)
                        if not ufirst:
                            if not bfirst:
                                pe.wait_ge(normed, u - 2)
                            pv(u - 1, 1 - h, j if h == 1 else 1 - j, u)
                        pe.wait_ge(negm_done, u * 2 + 2)
                        if not ufirst:
                            pe.wait_ge(m_copied, u)
                        nc.tensor.transpose(psb[MI][0:4 * HH, 256:256 + P // 2].bitcast(F16), negm[:, h, :], identh[:, :])\
                            .then_inc(m_T, 1)
                        pe.wait_ge(m_copied, u + 1)
                        if not ufirst:
                            pe.wait_ge(exp_done, u)
                        for hd in range(HH):
                            head = h * HH + hd
                            o = psb[ST0 + hd // 4][:, (hd % 4) * P:(hd % 4 + 1) * P]
                            nc.tensor.matmul(o, Kst[j][:, head, :], Qst[j][:, head, :], start=True, stop=False)
                            last = nc.tensor.matmul(o, sel[:, hd, :], mT[:, h, :], start=False, stop=True)
                        last.then_inc(scoresT, 1)
                        if not bfirst:
                            if h == 0:
                                o_transpose(b - 1)
                            else:
                                if not (first and j == 1):
                                    pe.wait_ge(x1_done, b - 1)
                                o_project(b - 1)

                batches(pe, body)
                pe.wait_ge(normed, 2 * B - 2)
                pv(2 * B - 1, 1, 1, 2 * B)
                o_transpose(B - 1)
                pe.wait_ge(x1_done, B - 1)
                o_project(B - 1)

        region_at[0] = 0
        xn = carve(G4 * E, F32).rearrange("p (b e) -> p b e", b=G4)
        xrow = [carve(G4 * 2 * E, F16).rearrange("p (b s e) -> p b s e", b=G4, s=2) for _ in range(2)]
        xT2 = carve(G4 * 2 * E, F16).rearrange("p (b s c n) -> p b s c n", b=G4, s=2, c=EC)
        lg = carve(2 * G4 * NX, F32).rearrange("p (j b n) -> p j b n", j=2, b=G4)
        mx8 = carve(2 * G4 * 8, F32).rearrange("p (j b n) -> p j b n", j=2, b=G4)
        ix8 = carve(2 * G4 * 8, U32).rearrange("p (j b n) -> p j b n", j=2, b=G4)
        (bn2, mv2, sd2, rstd2, xn_done, xr_hi, xr_split, xr_T, xr_cp, lg_mm, lg_cp, mx_done, ix_done, top_done,
         st0, st1) = sems("bn2", "mv2", "sd2", "rstd2", "xn_done", "xr_hi", "xr_split", "xr_T", "xr_cp", "lg_mm",
                          "lg_cp", "mx_done", "ix_done", "top_done", "st0", "st1")
        st_ = [st0, st1]
        with nc.Block() as block:
            @block.vector
            def _(dve):
                def body(g, i, j, first):
                    gfirst = first and j == 0

                    def row(b):
                        return xres[:, g * G4 + b, :] if first else \
                            xres[:, bass.ds(g * G4 + b, 1), :].rearrange("p a e -> p (a e)")
                    for b in range(G4):
                        last = nc.vector.bn_stats(st[:, j, b, :], row(b))
                    last.then_inc(bn2, 1)
                    dve.wait_ge(bn2, g + 1)
                    dve.sem_inc(passed_dve, 1)
                    for b in range(G4):
                        last = nc.vector.bn_aggr(mv[:, j, b, :], st[:, j, b, :])
                    last.then_inc(mv2, 1)
                    dve.wait_ge(sd2, g + 1)
                    nc.vector.reciprocal(rstd[:, j, :], sd[:, j, :]).then_inc(rstd2, 1)
                    dve.wait_ge(rstd2, g + 1)
                    for b in range(G4):
                        last = nc.vector.tensor_scalar(xn[:, b, :], row(b), mv[:, j, b, 0:1], rstd[:, j, b:b + 1],
                                                       ALU.subtract, ALU.mult)
                    last.then_inc(xn_done, 1)
                    dve.wait_ge(xr_hi, g + 1)
                    nc.vector.tensor_tensor(xrow[j][:, :, 1, :], xn, xrow[j][:, :, 0, :], ALU.subtract)\
                        .then_inc(xr_split, 1)
                    dve.wait_ge(lg_mm, g + 1)
                    nc.vector.tensor_copy(lg[:, j].rearrange("p b n -> p (b n)"), psb[4][:, 0:G4 * NX]).then_inc(lg_cp, 1)
                    dve.wait_ge(lg_cp, g + 1)
                    dve.sem_inc(passed_dve, 1)
                    for b in range(G4):
                        last = nc.vector.max(mx8[:, j, b, :], lg[:, j, b, :])
                    last.then_inc(mx_done, 1)
                    dve.wait_ge(mx_done, g + 1)
                    dve.sem_inc(passed_dve, 1)
                    for b in range(G4):
                        last = nc.vector.max_index(ix8[:, j, b, :], mx8[:, j, b, :], lg[:, j, b, :])
                    last.then_inc(ix_done, 1)
                    dve.wait_ge(ix_done, g + 1)
                    dve.sem_inc(passed_dve, 1)
                    nc.vector.tensor_copy(MX[:, bass.ds(g * G4, G4), :], mx8[:, j, :, 0:2])
                    nc.vector.tensor_copy(IX[:, bass.ds(g * G4, G4), :], ix8[:, j, :, 0:2]).then_inc(top_done, 1)

                groups(dve, body)

            @block.scalar
            def _(act):
                def body(g, i, j, first):
                    act.wait_ge(mv2, g + 1)
                    nc.scalar.activation(sd[:, j, :], mv[:, j, :, 1], ACT.Sqrt, bias=eps1[:, :], scale=2.0 ** -22)\
                        .then_inc(sd2, 1)
                    act.wait_ge(xn_done, g + 1)
                    if not first:
                        act.wait_ge(st_[j], i * 16)
                        act.wait_ge(xr_T, g - 1)
                    nc.scalar.activation(xrow[j][:, :, 0, :], xn, ACT.Copy).then_inc(xr_hi, 1)
                    act.wait_ge(xr_T, g + 1)
                    if not (first and j == 0):
                        act.wait_ge(lg_mm, g)
                    for n in range(2):
                        last = nc.scalar.activation(xT2[:, 2 * n:2 * n + 2].rearrange("p b s c n -> p (b s c n)"),
                                                    psb[n][:, :].bitcast(F16), ACT.Copy)
                    last.then_inc(xr_cp, 1)

                groups(act, body)

            @block.tensor
            def _(pe):
                def body(g, i, j, first):
                    gfirst = first and j == 0
                    pe.wait_ge(xr_split, g + 1)
                    if not gfirst:
                        pe.wait_ge(xr_cp, g)
                    for b in range(G4):
                        bank = psb[b // 2][:, :].bitcast(F16).rearrange("p (b s c n) -> p b s c n", b=2, s=2, c=EC)
                        for s in range(2):
                            for c in range(EC):
                                last = nc.tensor.transpose(bank[:, b % 2, s, c, :], xrow[j][:, b, s, c * P:(c + 1) * P],
                                                           identh[:, :])
                    last.then_inc(xr_T, 1)
                    pe.wait_ge(xr_cp, g + 1)
                    if not gfirst:
                        pe.wait_ge(lg_cp, g)
                    for b in range(G4):
                        terms = [(a, s, c) for a, s in ((0, 0), (0, 1), (1, 0)) for c in range(EC)]
                        for n, (a, s, c) in enumerate(terms):
                            last = nc.tensor.matmul(psb[4][:, b * NX:(b + 1) * NX], xT2[:, b, s, c, :], gT[:, a, c, :],
                                                    start=(n == 0), stop=(n == len(terms) - 1))
                    last.then_inc(lg_mm, 1)

                groups(pe, body)

            @block.sync
            def _(sp):
                def body(g, i, j, first):
                    sp.wait_ge(xr_split, g + 1)
                    sp.dma_start(xs[bass.ds(g * (G4 * S), G4 * S), :].rearrange("(b p) n -> p b n", p=P),
                                 xrow[j].rearrange("p b s e -> p b (s e)")).then_inc(st_[j], 16)

                groups(sp, body)
                for j in range(2):
                    sp.wait_ge(st_[j], 16 * NG // 2)

        region_at[0] = 0
        upper = carve(P, F16)
        ones = carve(P, F16)
        zeros = carve(P, F16)
        iot = carve(LCOL, F16)
        iob = carve(B, F32)
        pval = carve(2, F32)
        lsT = carve(4 * LCOL, F16).rearrange("p (s n) -> p s n", s=4)
        lsR = carve(4 * 2 * P, F16).rearrange("p (s a n) -> p s a n", s=4, a=2)
        oh = carve(2 * B * NX, F32).rearrange("p (k b n) -> p k b n", k=2, b=B)
        Mh = carve(B * NX, F16)
        cum = carve(B * NX, F32)
        cex = carve(B * NX, F16)
        rsel = carve(2 * B * NX, F32).rearrange("p (k b n) -> p k b n", k=2, b=B)
        rk = carve(2 * B, F32)
        rki = carve(2 * 2 * B, I32).rearrange("p (a n) -> p a n", a=2)
        rr = carve(2 * B, F32).rearrange("p (k b) -> p k b", k=2)
        cc = carve(2 * B, F32).rearrange("p (k b) -> p k b", k=2)
        ew = carve(2 * B, F32).rearrange("p (k b) -> p k b", k=2)
        val = carve(LCOL, F32)
        isneg = carve(LCOL, F32)
        vali = carve(LCOL, I32)
        nti = carve(NX, I32)
        ntf = carve(NX, F32)
        ncum = carve(NX, F32)
        iotile = carve(NT, F32)
        cmp_ = carve(NT * NX, F32).rearrange("p (t n) -> p t n", n=NX)
        cmp2 = carve(NT * NX, F32).rearrange("p (t n) -> p t n", n=NX)
        et = carve(NT, F32)
        jt = carve(NT, F32)
        iota8 = iot[:, 0:NX]
        (io_set, io_done, tri_set, tri_done, rchain, c_mm, rank_mm, list_set, list_mm, exped, pchain, zd) = sems(
            "io_set", "io_done", "tri_set", "tri_done", "rchain", "c_mm", "rank_mm", "list_set", "list_mm",
            "exped", "pchain", "zd")
        with nc.Block() as block:
            @block.gpsimd
            def _(pool):
                nc.gpsimd.iota(iota_i[:, :], [[1, LCOL]], base=0, channel_multiplier=0).then_inc(io_set, 1)
                pool.wait_ge(io_set, 1)
                nc.gpsimd.tensor_copy(iot, iota_i[:, :]).then_inc(io_set, 1)
                nc.gpsimd.tensor_copy(iotile, iota_i[:, 0:NT]).then_inc(io_set, 1)
                pool.wait_ge(io_set, 3)
                nc.gpsimd.iota(iota_i[:, 0:B], [[256, B]], base=0, channel_multiplier=0).then_inc(io_set, 1)
                nc.gpsimd.iota(iota_i[:, B:B + 2], [[1, 2]], base=1, channel_multiplier=2).then_inc(io_set, 1)
                pool.wait_ge(io_set, 5)
                nc.gpsimd.tensor_copy(iob, iota_i[:, 0:B]).then_inc(io_set, 1)
                nc.gpsimd.tensor_copy(pval, iota_i[:, B:B + 2]).then_inc(io_set, 1)
                nc.gpsimd.memset(ones, 1.0).then_inc(io_set, 1)
                nc.gpsimd.memset(zeros, 0.0).then_inc(io_set, 1)
                nc.gpsimd.memset(upper, 1.0).then_inc(io_set, 1)
                pool.wait_ge(io_set, 10)
                nc.gpsimd.affine_select(out=upper, in_=upper, compare_op=ALU.is_ge, fill=0.0, base=-1,
                                        pattern=[[1, P]], channel_multiplier=-1).then_inc(io_done, 1)

            @block.vector
            def _(dve):
                n = [0]

                def link(ins):
                    n[0] += 1
                    ins.then_inc(rchain, 1)
                    dve.wait_ge(rchain, n[0])

                link(nc.vector.tensor_tensor(ew[:, 0, :], MX[:, :, 1], MX[:, :, 0], ALU.subtract))
                dve.wait_ge(io_done, 1)
                for k in range(2):
                    link(nc.vector.tensor_tensor(oh[:, k], iota8.unsqueeze(1).broadcast_to([P, B, NX]),
                                                 IX[:, :, k].unsqueeze(2).broadcast_to([P, B, NX]), ALU.is_equal))
                ohf = [oh[:, k].rearrange("p b n -> p (b n)") for k in range(2)]
                link(nc.vector.tensor_tensor(Mh, ohf[0], ohf[1], ALU.add))
                cumv = cum.rearrange("p (b n) -> p b n", n=NX)
                mv_ = Mh.rearrange("p (b n) -> p b n", n=NX)
                for e in range(NX):
                    last = nc.vector.tensor_tensor_scan(cumv[:, :, e], mv_[:, :, e], mv_[:, :, e], 0.0, ALU.add, ALU.bypass)
                link(last)
                nc.vector.tensor_tensor(cex, cum, Mh, ALU.subtract).then_inc(c_mm, 1)
                dve.wait_ge(exped, 1)
                link(nc.vector.tensor_scalar(ew[:, 0, :], ew[:, 1, :], 1.0, None, ALU.add))
                link(nc.vector.reciprocal(ew[:, 0, :], ew[:, 0, :]))
                link(nc.vector.tensor_scalar(coef[:, :, 0], ew[:, 0, :], s_out[:, :], None, ALU.mult))
                link(nc.vector.tensor_tensor(coef[:, :, 1], coef[:, :, 0], ew[:, 1, :], ALU.mult))
                dve.wait_ge(rank_mm, 1)
                for k in range(2):
                    link(nc.vector.tensor_tensor(rsel[:, k].rearrange("p b n -> p (b n)"), psb[0][:, 0:B * NX], ohf[k], ALU.mult))
                    link(nc.vector.tensor_reduce(rk[:, k * B:(k + 1) * B], rsel[:, k], AX.X, ALU.add))
                link(nc.vector.tensor_copy(rki[:, 0], rk))
                link(nc.vector.tensor_scalar(rki[:, 1], rki[:, 0], 7, None, ALU.logical_shift_right))
                link(nc.vector.tensor_scalar(rki[:, 0], rki[:, 0], P - 1, None, ALU.bitwise_and))
                link(nc.vector.tensor_copy(rr.rearrange("p k b -> p (k b)"), rki[:, 0]))
                link(nc.vector.tensor_copy(cc.rearrange("p k b -> p (k b)"), rki[:, 1]))
                for k in range(2):
                    link(nc.vector.scalar_tensor_tensor(cc[:, k], IX[:, :, k], float(TCOL), cc[:, k], ALU.mult, ALU.add))

                def body(b, i, j, first):
                    if not first:
                        dve.wait_ge(list_mm, b - 1)
                    for k in range(2):
                        s = 2 * j + k
                        r = rr[:, k, bass.ds(b, 1)]
                        c = cc[:, k, bass.ds(b, 1)]
                        nc.vector.tensor_scalar(lsR[:, s, 0], iot[:, 0:P], r, pval[:, k:k + 1], ALU.is_equal, ALU.mult)
                        nc.vector.tensor_scalar(lsR[:, s, 1], iot[:, 0:P], r, iob[:, bass.ds(b, 1)], ALU.is_equal, ALU.mult)
                        last = nc.vector.tensor_scalar(lsT[:, s], iot, c, None, ALU.is_equal)
                    last.then_inc(list_set, 1)

                batches(dve, body)

                link(nc.vector.tensor_scalar(ntf, psb[1][:, 0:NX], float(SLOTS - 1), None, ALU.add))
                link(nc.vector.tensor_copy(nti, ntf))
                link(nc.vector.tensor_scalar(nti, nti, int(math.log2(SLOTS)), None, ALU.logical_shift_right))
                link(nc.vector.tensor_copy(ntf, nti))
                link(nc.vector.tensor_tensor_scan(ncum, ntf, ntf, 0.0, ALU.add, ALU.bypass))
                link(nc.vector.tensor_tensor(cmp_, ncum.unsqueeze(1).broadcast_to([P, NT, NX]),
                                             iotile.unsqueeze(2).broadcast_to([P, NT, NX]), ALU.is_le))
                link(nc.vector.tensor_tensor(cmp2, cmp_, ntf.unsqueeze(1).broadcast_to([P, NT, NX]), ALU.mult))
                link(nc.vector.tensor_reduce(et, cmp_, AX.X, ALU.add))
                link(nc.vector.tensor_reduce(jt, cmp2, AX.X, ALU.add))
                link(nc.vector.tensor_tensor(jt, iotile, jt, ALU.subtract))
                link(nc.vector.tensor_scalar(jt, jt, float(SLOTS // P), None, ALU.mult))
                link(nc.vector.scalar_tensor_tensor(jt, et, float(TCOL), jt, ALU.mult, ALU.add))
                link(nc.vector.tensor_scalar(jt, jt, float(LCOL), None, ALU.min))
                link(nc.vector.tensor_scalar(et, et, float(NX - 1), None, ALU.min))
                nc.vector.tensor_copy(tmap[0:1, 0, 0:NT], et[0:1, :])
                link(nc.vector.tensor_copy(tmap[0:1, 1, 0:NT], jt[0:1, :]))

                dve.wait_ge(list_mm, B + 1)
                link(nc.vector.tensor_scalar(val, psb[2][:, 0:LCOL], -1.0, None, ALU.add))
                link(nc.vector.tensor_scalar(isneg, val, 0.0, float(4 * T), ALU.is_lt, ALU.mult))
                link(nc.vector.tensor_tensor(listT[:, 0:LCOL, 1], val, isneg, ALU.add))
                link(nc.vector.tensor_scalar(vali, val, 0.0, None, ALU.max))
                link(nc.vector.tensor_scalar(listT[:, 0:LCOL, 0], vali, 1, None, ALU.logical_shift_right))
                nc.vector.memset(listT[:, LCOL:LCOL + 2, 0], 0)
                link(nc.vector.memset(listT[:, LCOL:LCOL + 2, 1], 4 * T))

            @block.scalar
            def _(act):
                act.wait_ge(rchain, 1)
                nc.scalar.activation(ew[:, 1, :], ew[:, 0, :], ACT.Exp, bias=zero1[:, :], scale=s_gate[:, :]).then_inc(exped, 1)

            @block.tensor
            def _(pe):
                pe.wait_ge(c_mm, 1)
                nc.tensor.matmul(psb[0][:, 0:B * NX], upper, Mh, start=True, stop=False)
                nc.tensor.matmul(psb[0][:, 0:B * NX], ones, cex, start=False, stop=True)
                nc.tensor.matmul(psb[1][:, 0:NX], ones, cex[:, (B - 1) * NX:B * NX], start=True, stop=False)
                nc.tensor.matmul(psb[1][:, 0:NX], ones, Mh[:, (B - 1) * NX:B * NX], start=False, stop=True)\
                    .then_inc(rank_mm, 1)

                def body(b, i, j, first):
                    pe.wait_ge(list_set, b + 1)
                    for k in range(2):
                        for a in range(2):
                            last = nc.tensor.matmul(psb[2][:, 0:LCOL], lsR[:, 2 * j + k, a], lsT[:, 2 * j + k],
                                                    start=(first and j == 0 and k == 0 and a == 0), stop=False)
                    last.then_inc(list_mm, 1)

                batches(pe, body)
                nc.tensor.matmul(psb[2][:, 0:LCOL], zeros, lsT[:, 0], start=False, stop=True).then_inc(list_mm, 1)

        region_at[0] = 0
        hid = carve(2 * 2 * FC * SLOTS, F16).rearrange("p (u s f n) -> p u s f n", u=2, s=2, f=FC)
        gel = carve(2 * 512, F32).rearrange("p (u n) -> p u n", u=2)
        xT = carve(2 * 4 * SLOTS, F16).rearrange("p (u a n) -> p u a n", u=2, a=4)
        SH = SLOTS // P
        aux_at[0] = 0
        xg = [beside(SH * 2 * E, F16).rearrange("p (h n) -> p h n", h=SH) for _ in range(3)]
        ysb = [beside(SH * E, F32).rearrange("p (h n) -> p h n", h=SH) for _ in range(3)]
        (g_idx, g0, g1, g2, t_T, t_cp, h_mm, gel_done, h_hi, h_split, y_mm, y_cp, sc0, sc1, sc2) = sems(
            "g_idx", "g0", "g1", "g2", "t_T", "t_cp", "h_mm", "gel_done", "h_hi", "h_split", "y_mm", "y_cp",
            "sc0", "sc1", "sc2")
        gsem, ssem = [g0, g1, g2], [sc0, sc1, sc2]
        NQ = FC // 2

        TP = 6
        PEEL = 3
        assert (NT - PEEL) % TP == 0

        class Tile:
            def __init__(self, i, o):
                self.i, self.o = i, o
                self.t = i * TP + o
                self.par, self.buf = o % 2, o % 3
                self.uses = i * (TP // 3) + o // 3

            def next(self, d):
                return Tile(self.i, self.o + d)

        def tiles(eng, body):
            for o in range(PEEL):
                body(Tile(0, o))
            with eng.Fori(0, (NT - PEEL) // TP) as i:
                for o in range(PEEL, PEEL + TP):
                    body(Tile(i, o))

        def at_least(tile, n):
            return tile.o >= n

        with nc.Block() as block:
            @block.gpsimd
            def _(pool):
                def fetch(tile):
                    r = tile.buf
                    col = pool.value_load(tmap[0:1, 1, bass.ds(tile.t, 1)], min_val=0, max_val=LCOL)
                    if at_least(tile, 3):
                        pool.wait_ge(ssem[r], tile.uses * (16 * SH))
                        pool.wait_ge(t_T, tile.t - 2)
                    nc.gpsimd.tensor_copy(gi[:, r, :].rearrange("p (h a) -> p h a", a=2), listT[:, bass.ds(col, SH), :])\
                        .then_inc(g_idx, 1)
                    pool.wait_ge(g_idx, tile.t + 1)
                    pool.sem_inc(passed_pool, 1)
                    for h in range(SH):
                        nc.gpsimd.indirect_dma_start(
                            out=xg[r][:, h, :], out_offset=None, in_=xs[:, :],
                            in_offset=bass.IndirectOffsetOnAxis(ap=gi[:, r, 2 * h:2 * h + 1].bitcast(U32), axis=0))\
                            .then_inc(gsem[r], 16)

                def scatter(tile):
                    r = tile.buf
                    pool.wait_ge(y_cp, tile.t + 1)
                    pool.sem_inc(passed_pool, 1)
                    for h in range(SH):
                        nc.gpsimd.indirect_dma_start(
                            out=ys[:, :],
                            out_offset=bass.IndirectOffsetOnAxis(ap=gi[:, r, 2 * h + 1:2 * h + 2].bitcast(U32), axis=0),
                            in_=ysb[r][:, h, :], in_offset=None, bounds_check=2 * T - 1, oob_is_err=False)\
                            .then_inc(ssem[r], 16)

                def body(tile):
                    fetch(tile)
                    if at_least(tile, 2):
                        scatter(tile.next(-2))

                tiles(pool, body)
                scatter(Tile(0, NT - 2))
                scatter(Tile(0, NT - 1))
                for r in range(3):
                    pool.wait_ge(ssem[r], 16 * SH * (NT // 3))

            @block.tensor
            def _(pe):
                def rows_T(tile):
                    pe.wait_ge(gsem[tile.buf], tile.uses * (16 * SH) + 16 * SH)
                    if at_least(tile, 1):
                        pe.wait_ge(t_cp, tile.t)
                    bank = psb[6][:, :].bitcast(F16).rearrange("p (a n) -> p a n", a=4)
                    for h in range(SH):
                        for a in range(4):
                            last = nc.tensor.transpose(bank[:, a, h * P:(h + 1) * P],
                                                       xg[tile.buf][:, h, a * P:(a + 1) * P], identh[:, :])
                    last.then_inc(t_T, 1)

                def expert(tile):
                    return pe.value_load(tmap[0:1, 0, bass.ds(tile.t, 1)], min_val=0, max_val=NX - 1)

                def hidden(tile, e):
                    pe.wait_ge(t_cp, tile.t + 1)
                    for q in range(NQ):
                        if at_least(tile, 1):
                            pe.wait_ge(gel_done, tile.t * NQ + (q + 1 - NQ))
                        for f in (2 * q, 2 * q + 1):
                            terms = [(w, s, c) for w, s in ((w1h, 0), (w1h, 1), (w1l, 0)) for c in range(EC)]
                            for n, (w, s, c) in enumerate(terms):
                                last = nc.tensor.matmul(psb[q][:, (f % 2) * SLOTS:(f % 2 + 1) * SLOTS],
                                                        w[:, bass.ds(e * (EC * F) + (c * F + f * P), P)],
                                                        xT[:, tile.par, 2 * s + c, :],
                                                        start=(n == 0), stop=(n == len(terms) - 1))
                        last.then_inc(h_mm, 1)

                def output(tile, e):
                    if at_least(tile, 2):
                        pe.wait_ge(y_cp, tile.t - 1)
                    for h in range(SH):
                        terms = [(s, w, f) for f in range(FC) for s, w in ((0, w2h), (0, w2l), (1, w2h))]
                        for n, (s, w, f) in enumerate(terms):
                            if h == 0 and n % (3 * FC // NQ) == 0:
                                pe.wait_ge(h_split, tile.t * NQ + (f // 2 + 1))
                            last = nc.tensor.matmul(psb[4 + tile.par][:, h * E:(h + 1) * E],
                                                    hid[:, tile.par, s, f, h * P:(h + 1) * P],
                                                    w[:, bass.ds(e * (FC * E) + f * E, E)],
                                                    start=(n == 0), stop=(n == len(terms) - 1))
                    last.then_inc(y_mm, 1)

                def body(tile):
                    rows_T(tile)
                    if at_least(tile, 1):
                        before = tile.next(-1)
                        output(before, expert(before))
                    hidden(tile, expert(tile))

                tiles(pe, body)
                output(Tile(0, NT - 1), expert(Tile(0, NT - 1)))

            @block.scalar
            def _(act):
                def body(tile):
                    act.wait_ge(t_T, tile.t + 1)
                    if at_least(tile, 2):
                        act.wait_ge(h_mm, tile.t * NQ - NQ)
                    nc.scalar.activation(xT[:, tile.par].rearrange("p a n -> p (a n)"), psb[6][:, :].bitcast(F16), ACT.Copy)\
                        .then_inc(t_cp, 1)
                    for q in range(NQ):
                        act.wait_ge(h_mm, tile.t * NQ + (q + 1))
                        if at_least(tile, 1) or q >= 2:
                            act.wait_ge(h_split, tile.t * NQ + (q - 1))
                        nc.scalar.activation(gel[:, q % 2], psb[q][:, :], ACT.Gelu, bias=zero1[:, :], scale=s_pre[:, :])\
                            .then_inc(gel_done, 1)

                tiles(act, body)

            @block.vector
            def _(dve):
                def y_copy(tile):
                    dve.wait_ge(y_mm, tile.t + 1)
                    if at_least(tile, 3):
                        dve.wait_ge(ssem[tile.buf], tile.uses * (16 * SH))
                    nc.vector.tensor_copy(ysb[tile.buf].rearrange("p h n -> p (h n)"), psb[4 + tile.par][:, :])\
                        .then_inc(y_cp, 1)

                def body(tile):
                    if at_least(tile, 1):
                        y_copy(tile.next(-1))
                    for q in range(NQ):
                        dve.wait_ge(gel_done, tile.t * NQ + (q + 1))
                        hi = hid[:, tile.par, 0, 2 * q:2 * q + 2, :].rearrange("p f n -> p (f n)")
                        lo = hid[:, tile.par, 1, 2 * q:2 * q + 2, :].rearrange("p f n -> p (f n)")
                        nc.vector.tensor_scalar(hi, gel[:, q % 2], s_hid[:, :], None, ALU.mult).then_inc(h_hi, 1)
                        dve.wait_ge(h_hi, tile.t * NQ + (q + 1))
                        nc.vector.scalar_tensor_tensor(lo, gel[:, q % 2], s_hid[:, :], hi, ALU.mult, ALU.subtract)\
                            .then_inc(h_split, 1)

                tiles(dve, body)
                y_copy(Tile(0, NT - 1))

        ybuf = WSF[:, 0:B * 2 * E].rearrange("p (b k e) -> p b k e", b=B, k=2)
        obuf = WSF[:, B * 2 * E:B * 3 * E].rearrange("p (b e) -> p b e", b=B)
        NC8 = 8
        BB = B // NC8
        ysems = sems(*[f"y_ld{n}" for n in range(NC8)])
        c_one, c_done, out_st = sems("c_one", "c_done", "out_st")
        with nc.Block() as block:
            @block.sync
            def _(sp):
                for n in range(NC8):
                    sp.dma_start(ybuf[:, n * BB:(n + 1) * BB].rearrange("p b k e -> p b (k e)"),
                                 ys.rearrange("(b p k) e -> b p (k e)", p=P, k=2)[n * BB:(n + 1) * BB].rearrange("b p n -> p b n"))\
                        .then_inc(ysems[n], 16)
                for n in range(NC8):
                    sp.wait_ge(c_done, BB * (n + 1))
                    sp.dma_start(out[n * BB:(n + 1) * BB].rearrange("b s e -> s b e"), obuf[:, n * BB:(n + 1) * BB])\
                        .then_inc(out_st, 16)
                sp.wait_ge(out_st, 16 * NC8)

            @block.vector
            def _(dve):
                for n in range(NC8):
                    dve.wait_ge(ysems[n], 16)
                    for b in range(n * BB, (n + 1) * BB):
                        nc.vector.scalar_tensor_tensor(obuf[:, b], ybuf[:, b, 0], coef[:, b, 0:1], xres[:, b], ALU.mult, ALU.add)\
                            .then_inc(c_one, 1)
                    for b in range(n * BB, (n + 1) * BB):
                        dve.wait_ge(c_one, b + 1)
                        nc.vector.scalar_tensor_tensor(obuf[:, b], ybuf[:, b, 1], coef[:, b, 1:2], obuf[:, b], ALU.mult, ALU.add)\
                            .then_inc(c_done, 1)


_INS = ["x", "ctx_1024", "L0_xattn_Wq", "L0_xattn_Wk", "L0_xattn_Wv", "L0_xattn_Wo", "L0_ffn_gate_w", "L0_ffn_w1",
        "L0_ffn_w2"]


def kernel(**inputs):
    import numpy as _np
    import concourse.bacc as _bacc
    from concourse import mybir as _mybir
    from concourse.bass_utils import run_bass_kernel_spmd as _run

    nc = _bacc.Bacc("TRN2", target_bir_lowering=False, num_devices=1, dynamic_dma_scratch_size=8192)
    arrays, args = {}, []
    for name in _INS:
        a = _np.ascontiguousarray(inputs[name])
        arrays[f"in_{name}_dram"] = a
        args.append(nc.dram_tensor(f"in_{name}_dram", a.shape, _mybir.dt.from_np(a.dtype), kind="ExternalInput").ap())
    shape = arrays["in_x_dram"].shape
    out = nc.dram_tensor("out_0_dram", shape, _mybir.dt.from_np(_np.dtype("float32")), kind="ExternalOutput").ap()
    build(nc, *args, out)
    r = _run(nc, [arrays], core_ids=[0])
    return r.results[0]["out_0_dram"]
```

```python
import math
from contextlib import ExitStack

import concourse.bass as bass
import numpy as np
from concourse import mybir

F32, F16 = mybir.dt.float32, mybir.dt.float16
I32, U32 = mybir.dt.int32, mybir.dt.uint32
ACT, ALU, AX = mybir.ActivationFunctionType, mybir.AluOpType, mybir.AxisListType


def key_block_counts(batch_blocks):
    seq, block = 512, 64
    nb = seq // block
    total = nb * nb
    keep = int(total * (1.0 - 0.05))
    idx = [(i, i) for i in range(nb)]
    band = max(1, int(math.sqrt(keep - nb) / 2))
    for i in range(nb):
        for o in range(1, band + 1):
            if i + o < nb:
                idx += [(i, i + o), (i + o, i)]
            if i - o >= 0:
                idx.append((i, i - o))
    for skip in (2, 4, 8, 16):
        if len(idx) >= keep:
            break
        for i in range(0, nb - skip, skip):
            if len(idx) < keep:
                idx.append((i, i + skip))
                if len(idx) < keep:
                    idx.append((i + skip, i))
    pairs = sorted(set(idx))[:keep]
    counts = np.zeros((batch_blocks, batch_blocks), int)
    for r, c in pairs:
        if r < batch_blocks:
            counts[r, min(c, batch_blocks - 1)] += 1
    return counts


def build(nc, x, ctxt, wq, wk, wv, wo, gate_w, w1, w2, out):
    B, S, E = x.shape
    P = 128
    assert S == P and E == 2 * P
    EC = E // P
    D = 16
    H = E // D
    HH = H // 2
    BLK = 64
    NX = gate_w.shape[1]
    F = w1.shape[2]
    FC = F // P
    T = B * S
    G4 = 4
    NG = B // G4
    SLOTS = 256
    NT = 2 * T // SLOTS + NX - 1
    TCOL = T // P
    LCOL = NX * TCOL
    EPS = 1e-5
    VW = D + 1
    counts = key_block_counts(S // BLK)
    PIECE = F
    NPIECE = 2 * NX * EC
    P_SHIFT = 12
    assert NT % 3 == 0

    qkd = nc.dram_tensor("qk_split", (NG, 2, D, 2, 2, HH, G4 * S), F16).ap()
    vd = nc.dram_tensor("v_split", (B, S, 2 * H * VW), F16).ap()
    xs = nc.dram_tensor("x2_split", (T, 2 * E), F16).ap()
    ys = nc.dram_tensor("expert_out", (2 * T, E), F32).ap()

    ctx = ExitStack()
    with ctx:
        def sb(name, shape, dt):
            return ctx.enter_context(nc.sbuf_tensor(name, shape, dt))

        def pb(name):
            return ctx.enter_context(nc.psum_tensor(name, [P, 512], F32))

        WS = sb("expert_weights", [P, (NPIECE + 1) * 2 * PIECE], F16)
        WSF = WS[:, :].bitcast(F32)
        xres = sb("residual", [P, B, E], F32)
        wsc = sb("weight_scales", [P, NPIECE], F32)
        R = sb("phase_region", [P, 8192], F32)
        region_at = [0]

        def carve(n, dt):
            size = n * (4 if dt in (F32, I32, U32) else 2)
            a = region_at[0]
            region_at[0] += size // 4
            assert region_at[0] <= 8192
            v = R[:, a:region_at[0]]
            return v if dt == F32 else v.bitcast(dt)

        aux = sb("beside_region", [P, 3136], F32)
        aux_at = [0]

        def beside(n, dt):
            size = n * (4 if dt in (F32, I32, U32) else 2)
            a = aux_at[0]
            aux_at[0] += size // 4
            assert aux_at[0] <= 3136
            v = aux[:, a:aux_at[0]]
            return v if dt == F32 else v.bitcast(dt)

        identf = sb("identf", [P, P], F32)
        identh = sb("identh", [P, P], F16)
        absmax = sb("absmax", [P, 8], F32)
        gmax = sb("gmax", [P, 8], F32)
        pw = sb("pow2", [P, 8], F32)
        sc = sb("to_fp16_scale", [P, 8], F32)
        CTX, WQ, WK, WV, WO, WG, W1, W2 = 4, 0, 1, 2, 3, 5, 6, 7
        s_attn = sb("s_attn", [P, 1], F32)
        s_res = sb("s_res", [P, 1], F32)
        s_gate = sb("s_gate", [P, 1], F32)
        s_pre = sb("s_pre", [P, 1], F32)
        s_hid = sb("s_hid", [P, 1], F32)
        s_out = sb("s_out", [P, 1], F32)
        eps1 = sb("eps1", [P, 1], F32)
        pbias = sb("pbias", [P, 1], F32)
        zero1 = sb("zero1", [P, 1], F32)
        wcoef = sb("wcoef", [P, 2], F32)
        WT = sb("attn_weights", [P, 2, 4, EC, E], F16)
        gT = sb("gate_weights", [P, 2, EC, NX], F16)
        st = sb("bn_st", [P, 2, G4, 6], F32)
        mv = sb("bn_mv", [P, 2, G4, 2], F32)
        sd = sb("std", [P, 2, G4], F32)
        rstd = sb("rstd", [P, 2, G4], F32)
        MX = sb("top_logit", [P, B, 2], F32)
        IX = sb("top_expert", [P, B, 2], F32)
        wt_region = WT[:].rearrange("p s w c n -> p (s w c n)").bitcast(I32)
        listT = wt_region[:, 0:2 * (LCOL + 2)].rearrange("p (n a) -> p n a", a=2)
        iota_i = wt_region[:, 2 * (LCOL + 2):2 * (LCOL + 2) + LCOL]
        gi = wt_region[:, 1024:1024 + 3 * 2 * SLOTS // P].rearrange("p (u n) -> p u n", u=3)
        tmap = sb("tile_map", [1, 2, NT + 1], I32)
        coef = sb("combine_coef", [P, B, 2], F32)
        psb = [pb(f"bank{i}") for i in range(8)]

        passed_dve = ctx.enter_context(nc.semaphore("passed_dve"))
        passed_pool = ctx.enter_context(nc.semaphore("passed_pool"))
        phases = iter("ABCDEFGHIJ")

        def sems(*names):
            tag = next(phases)
            return [ctx.enter_context(nc.semaphore(f"{tag}_{n}")) for n in names]

        def pow2_scales(dve, lo, hi, chain, done):
            n = [0]

            def link(ins):
                n[0] += 1
                ins.then_inc(chain, 1)
                dve.wait_ge(chain, n[0])

            link(nc.vector.tensor_scalar(pw[:, lo:hi], gmax[:, lo:hi], 2.0 ** -30, 2.0 ** 30, ALU.max, ALU.min))
            link(nc.vector.tensor_scalar(pw[:, lo:hi].bitcast(I32), pw[:, lo:hi].bitcast(I32),
                                         0x7F800000, None, ALU.bitwise_and))
            link(nc.vector.tensor_scalar(sc[:, lo:hi].bitcast(I32), pw[:, lo:hi].bitcast(I32),
                                         -1.0, float((254 + 14) << 23), ALU.mult, ALU.add))
            return link

        region_at[0] = 0
        wst = carve(4 * EC * E, F32).rearrange("p (w c n) -> p w c n", w=4, c=EC)
        gst = carve(EC * NX, F32).rearrange("p (c n) -> p c n", c=EC)
        ctx_all = WSF[:, (NPIECE + 1) * PIECE - B * E:(NPIECE + 1) * PIECE]
        (weights_in, gate_in, ctx_in, x_in, absmax_done, gmax_done, chain, scales_done, ident_set, ident_done,
         weights_T, weights_hi, weights_split, consts_done, gate_hi) = sems(
            "weights_in", "gate_in", "ctx_in", "x_in", "absmax_done", "gmax_done", "chain", "scales_done",
            "ident_set", "ident_done", "weights_T", "weights_hi", "weights_split", "consts_done", "gate_hi")
        with nc.Block() as block:
            @block.sync
            def _(sp):
                for n, w in enumerate((wq, wk, wv, wo)):
                    sp.dma_start(wst[:, n], w.rearrange("(c p) n -> p c n", p=P)).then_inc(weights_in, 16)
                sp.dma_start(gst, gate_w.rearrange("(c p) n -> p c n", p=P)).then_inc(gate_in, 16)
                for q in range(4):
                    b0, b1 = q * B // 4, (q + 1) * B // 4
                    sp.dma_start(ctx_all[:, b0 * E:b1 * E].rearrange("p (b e) -> p b e", e=E), ctxt[b0:b1].rearrange("b s e -> s b e")).then_inc(ctx_in, 16)
                for q in range(4):
                    b0, b1 = q * B // 4, (q + 1) * B // 4
                    sp.dma_start(xres[:, b0:b1], x[b0:b1].rearrange("b s e -> s b e")).then_inc(x_in, 16)
                sp.wait_ge(x_in, 64)

            @block.gpsimd
            def _(pool):
                nc.gpsimd.memset(zero1[:, :], 0.0).then_inc(consts_done, 1)
                for m in (identf, identh):
                    nc.gpsimd.memset(m[:, :], 0.0).then_inc(ident_set, 1)
                pool.wait_ge(ident_set, 2)
                for m in (identf, identh):
                    nc.gpsimd.affine_select(out=m[:, :], in_=m[:, :], compare_op=ALU.not_equal, fill=1.0, base=0,
                                            pattern=[[-1, P]], channel_multiplier=1).then_inc(ident_done, 1)
                nc.gpsimd.memset(eps1[:, :], EPS * 2.0 ** -22).then_inc(consts_done, 1)
                nc.gpsimd.memset(pbias[:, :], P_SHIFT * math.log(2.0)).then_inc(consts_done, 1)
                pool.wait_ge(consts_done, 3 + counts.size)
                pool.wait_ge(absmax_done, 3)
                nc.gpsimd.partition_all_reduce(gmax[:, 0:6], absmax[:, 0:6], P, bass.bass_isa.ReduceOp.max)\
                    .then_inc(gmax_done, 1)

            @block.vector
            def _(dve):
                for r in range(S // BLK):
                    for c in range(S // BLK):
                        nc.vector.memset(wcoef[r * BLK:(r + 1) * BLK, c:c + 1], float(counts[r, c]) / 8.0)\
                            .then_inc(consts_done, 1)
                dve.wait_ge(weights_in, 64)
                nc.vector.tensor_reduce(absmax[:, 0:4], wst.rearrange("p w c n -> p w (c n)"), AX.X, ALU.max,
                                        apply_absolute_value=True).then_inc(absmax_done, 1)
                dve.wait_ge(gate_in, 16)
                nc.vector.tensor_reduce(absmax[:, WG:WG + 1], gst, AX.XY, ALU.max,
                                        apply_absolute_value=True).then_inc(absmax_done, 1)
                dve.wait_ge(ctx_in, 64)
                nc.vector.tensor_reduce(absmax[:, CTX:CTX + 1], ctx_all, AX.X, ALU.max,
                                        apply_absolute_value=True).then_inc(absmax_done, 1)
                dve.wait_ge(gmax_done, 1)
                link = pow2_scales(dve, 0, 6, chain, None)
                nc.vector.tensor_tensor(s_gate[:, :], pw[:, WV:WV + 1], pw[:, WO:WO + 1], ALU.mult)
                link(nc.vector.tensor_tensor(s_attn[:, :], pw[:, WQ:WQ + 1], pw[:, WK:WK + 1], ALU.mult))
                nc.vector.tensor_scalar(s_res[:, :], s_gate[:, :], pw[:, CTX:CTX + 1], 2.0 ** -16, ALU.mult, ALU.mult)
                link(nc.vector.tensor_scalar(s_attn[:, :], s_attn[:, :], pw[:, CTX:CTX + 1],
                                             2.0 ** -7 * D ** -0.5, ALU.mult, ALU.mult))
                nc.vector.tensor_scalar(s_gate[:, :], pw[:, WG:WG + 1], 2.0 ** -25, None, ALU.mult)\
                    .then_inc(scales_done, 1)
                nc.vector.tensor_scalar(gT[:, 0], gst, sc[:, WG:WG + 1], None, ALU.mult).then_inc(gate_hi, 1)
                dve.wait_ge(gate_hi, 1)
                nc.vector.scalar_tensor_tensor(gT[:, 1], gst, sc[:, WG:WG + 1], gT[:, 0], ALU.mult, ALU.subtract)\
                    .then_inc(weights_split, 1)
                for n in range(4):
                    dve.wait_ge(weights_hi, n + 1)
                    nc.vector.scalar_tensor_tensor(
                        WT[:, 1, n].rearrange("p c n -> p (c n)"), psb[n][:, :], sc[:, n:n + 1],
                        WT[:, 0, n].rearrange("p c n -> p (c n)"), ALU.mult, ALU.subtract).then_inc(weights_split, 1)
                dve.wait_ge(weights_split, 5)

            @block.tensor
            def _(pe):
                pe.wait_ge(ident_done, 2)
                pe.wait_ge(weights_in, 64)
                for n in range(4):
                    for oc in range(EC):
                        for ic in range(EC):
                            last = nc.tensor.transpose(psb[n][:, ic * E + oc * P:ic * E + (oc + 1) * P],
                                                       wst[:, n, oc, ic * P:(ic + 1) * P], identf[:, :])
                    last.then_inc(weights_T, 1)

            @block.scalar
            def _(act):
                act.wait_ge(scales_done, 1)
                for n in range(4):
                    act.wait_ge(weights_T, n + 1)
                    nc.scalar.activation(WT[:, 0, n].rearrange("p c n -> p (c n)"), psb[n][:, :], ACT.Copy,
                                         scale=sc[:, n:n + 1]).then_inc(weights_hi, 1)

        region_at[0] = aux_at[0] = 0
        xh = [carve(G4 * E, F32).rearrange("p (b e) -> p b e", b=G4) for _ in range(2)]
        cst = carve(G4 * E, F32).rearrange("p (b e) -> p b e", b=G4)
        inT = carve(2 * 2 * 2 * EC * 512, F16).rearrange("p (u w s c n) -> p u w s c n", u=2, w=2, s=2, c=EC)
        qk = beside(2 * 2 * EC * 512, F16).rearrange("p (w s c n) -> p w s c n", w=2, s=2, c=EC)
        vS = beside(G4 * 2 * H * VW, F16).rearrange("p (b s h v) -> p b s h v", b=G4, s=2, h=H)
        amx = carve(2 * NX, F32)
        CH = 2 * PIECE
        assert 2 * NX == 2 * NG and G4 * E == PIECE
        (mv_done, sd_done, rstd_done, xh_done, x_T, c_T, x_hi, x_split, c_hi, c_split,
         q_mm, k_mm, v_mm, q_hi, k_hi, v_hi, q_split, k_split, v_split, st_q, st_k, st_v, ones_set, bn_done,
         c_copied, w_ld0, w_ld1, amx_done, w_absmax, w_gmax, wchain) = sems(
            "mv_done", "sd_done", "rstd_done", "xh_done", "x_T", "c_T", "x_hi", "x_split",
            "c_hi", "c_split", "q_mm", "k_mm", "v_mm", "q_hi", "k_hi", "v_hi", "q_split", "k_split", "v_split",
            "st_q", "st_k", "st_v", "ones_set", "bn_done", "c_copied", "w_ld0", "w_ld1", "amx_done",
            "w_absmax", "w_gmax", "wchain")
        w_ld = [w_ld0, w_ld1]

        class Group:
            def __init__(self, i, o):
                self.i, self.o = i, o
                self.g = i * 2 + o
                self.par = o % 2
                self.turn = i + o // 2

            def next(self, d):
                return Group(self.i, self.o + d)

            def exists(self):
                return not isinstance(self.g, int) or 0 <= self.g < NG

            def row(self, b):
                if isinstance(self.g, int):
                    return xres[:, self.g * G4 + b, :]
                return xres[:, bass.ds(self.g * G4 + b, 1), :].rearrange("p a e -> p (a e)")

        def groups(eng, body, drain=0):
            for o in range(-1, 2):
                body(Group(0, o))
            with eng.Fori(0, NG // 2 - 2) as i:
                for o in (2, 3):
                    body(Group(i, o))
            for o in range(NG - 2, NG + drain):
                body(Group(0, o))

        with nc.Block() as block:
            @block.sync
            def _(sp):
                def weight(w, m, gr):
                    sp.dma_start(
                        WSF[:, bass.ds((m * NX + gr.g) * CH + PIECE, CH)].rearrange("p (c n) -> p c n", n=w.shape[2]),
                        w[bass.ds(gr.g, 1)].rearrange("a (c p) n -> p (a c) n", p=P)).then_inc(w_ld[gr.par], 16)

                def body(gr):
                    nx, g = gr.next(1), gr.g
                    if nx.exists():
                        weight(w1, 0, nx)
                    if gr.exists():
                        for w, ready, st_sem in ((0, q_split, st_q), (1, k_split, st_k)):
                            sp.wait_ge(ready, g + 1)
                            for s in range(2):
                                for c in range(EC):
                                    sp.dma_start(qkd[bass.ds(g, 1), s ^ w, :, c, w]
                                                 .rearrange("a d h m -> (a h) d m"), qk[:, w, s, c]).then_inc(st_sem, 16)
                    if nx.exists():
                        sp.wait_ge(c_T, nx.g + 1)
                        weight(w2, 1, nx)
                    if gr.exists():
                        sp.wait_ge(v_split, g + 1)
                        sp.dma_start(vd[bass.ds(g * G4, G4)].rearrange("b p n -> p b n"),
                                     vS.rearrange("p b s h v -> p b (s h v)")).then_inc(st_v, 16)

                groups(sp, body)
                sp.wait_ge(st_q, 16 * 4 * NG)
                sp.wait_ge(st_k, 16 * 4 * NG)
                sp.wait_ge(st_v, 16 * NG)

            @block.vector
            def _(dve):
                nc.vector.memset(vS[:, :, 0, :, D:VW], 1.0)
                nc.vector.memset(vS[:, :, 1, :, D:VW], 0.0).then_inc(ones_set, 1)

                def body(gr):
                    nx, g = gr.next(1), gr.g
                    if nx.exists():
                        for b in range(G4):
                            last = nc.vector.bn_stats(st[:, nx.par, b, :], nx.row(b))
                        last.then_inc(bn_done, 1)
                        dve.wait_ge(bn_done, nx.g + 1)
                        dve.sem_inc(passed_dve, 1)
                        for b in range(G4):
                            last = nc.vector.bn_aggr(mv[:, nx.par, b, :], st[:, nx.par, b, :])
                        last.then_inc(mv_done, 1)
                        dve.wait_ge(sd_done, nx.g + 1)
                        nc.vector.reciprocal(rstd[:, nx.par, :], sd[:, nx.par, :]).then_inc(rstd_done, 1)
                        dve.wait_ge(rstd_done, nx.g + 1)
                        if nx.o >= 2:
                            dve.wait_ge(x_T, nx.g - 1)
                        for b in range(G4):
                            last = nc.vector.tensor_scalar(xh[nx.par][:, b, :], nx.row(b), mv[:, nx.par, b, 0:1],
                                                           rstd[:, nx.par, b:b + 1], ALU.subtract, ALU.mult)
                        last.then_inc(xh_done, 1)
                    if gr.exists():
                        for w, (hi, split, k) in enumerate(((q_hi, q_split, 2.0 ** -21), (k_hi, k_split, 2.0 ** -25))):
                            dve.wait_ge(hi, g + 1)
                            for c in range(EC):
                                last = nc.vector.scalar_tensor_tensor(qk[:, w, 1, c], psb[4 + 2 * w + c][:, :], k,
                                                                      qk[:, w, 0, c], ALU.mult, ALU.subtract)
                            last.then_inc(split, 1)
                    if nx.exists():
                        dve.wait_ge(x_hi, nx.g + 1)
                        for c in range(EC):
                            last = nc.vector.tensor_tensor(inT[:, nx.par, 0, 1, c], psb[c][:, :],
                                                           inT[:, nx.par, 0, 0, c], ALU.subtract)
                        last.then_inc(x_split, 1)
                        dve.wait_ge(c_hi, nx.g + 1)
                        for c in range(EC):
                            last = nc.vector.scalar_tensor_tensor(inT[:, nx.par, 1, 1, c], psb[2 + c][:, :],
                                                                  sc[:, CTX:CTX + 1], inT[:, nx.par, 1, 0, c],
                                                                  ALU.mult, ALU.subtract)
                        last.then_inc(c_split, 1)
                    if gr.exists():
                        dve.wait_ge(w_ld[gr.par], gr.turn * 32 + 32)
                        nc.vector.tensor_reduce(
                            amx.rearrange("p (m n) -> p m n", m=2)[:, :, bass.ds(g, 1)],
                            WSF[:, PIECE:].rearrange("p (m c) -> p m c", m=2)[:, :, bass.ds(g * CH, CH)],
                            AX.X, ALU.max, apply_absolute_value=True).then_inc(amx_done, 1)
                        dve.wait_ge(v_hi, g + 1)
                        for b in range(G4):
                            last = nc.vector.scalar_tensor_tensor(
                                vS[:, b, 1, :, 0:D],
                                psb[4 + b // 2][:, (b % 2) * E:(b % 2 + 1) * E].rearrange("p (h d) -> p h d", h=H),
                                2.0 ** -23, vS[:, b, 0, :, 0:D], ALU.mult, ALU.subtract)
                        last.then_inc(v_split, 1)

                groups(dve, body)
                dve.wait_ge(amx_done, NG)
                nc.vector.tensor_reduce(absmax[:, W1:W2 + 1], amx.rearrange("p (m n) -> p m n", m=2), AX.X, ALU.max)\
                    .then_inc(w_absmax, 1)
                dve.wait_ge(w_gmax, 1)
                link = pow2_scales(dve, W1, W2 + 1, wchain, None)
                link(nc.vector.tensor_scalar(s_pre[:, :], pw[:, W1:W1 + 1], 2.0 ** -25, None, ALU.mult))
                link(nc.vector.tensor_scalar(s_hid[:, :], sc[:, W1:W1 + 1], 2.0 ** -8, None, ALU.mult))
                link(nc.vector.tensor_tensor(s_out[:, :], pw[:, W1:W1 + 1], pw[:, W2:W2 + 1], ALU.mult))
                link(nc.vector.tensor_scalar(s_out[:, :], s_out[:, :], 2.0 ** -20, None, ALU.mult))
                for m in range(2):
                    link(nc.vector.tensor_copy(wsc[:, m * NX * EC:(m + 1) * NX * EC],
                                               sc[:, W1 + m:W1 + m + 1].broadcast_to([P, NX * EC])))

            @block.gpsimd
            def _(pool):
                def body(gr):
                    nx = gr.next(1)
                    if nx.exists():
                        if nx.o >= 1:
                            pool.wait_ge(c_T, nx.g)
                        nc.gpsimd.tensor_copy(cst.rearrange("p b e -> p (b e)"),
                                              ctx_all[:, bass.ds(nx.g * (G4 * E), G4 * E)]).then_inc(c_copied, 1)

                groups(pool, body)
                pool.wait_ge(w_absmax, 1)
                nc.gpsimd.partition_all_reduce(gmax[:, W1:W2 + 1], absmax[:, W1:W2 + 1], P, bass.bass_isa.ReduceOp.max)\
                    .then_inc(w_gmax, 1)

            @block.scalar
            def _(act):
                def body(gr):
                    nx, g = gr.next(1), gr.g
                    if nx.exists():
                        act.wait_ge(mv_done, nx.g + 1)
                        nc.scalar.activation(sd[:, nx.par, :], mv[:, nx.par, :, 1], ACT.Sqrt, bias=eps1[:, :],
                                             scale=2.0 ** -22).then_inc(sd_done, 1)
                    if gr.exists():
                        for w, (mm, hi, k, st_sem) in enumerate(((q_mm, q_hi, 2.0 ** -21, st_q),
                                                                 (k_mm, k_hi, 2.0 ** -25, st_k))):
                            act.wait_ge(mm, g + 1)
                            if gr.o >= 1:
                                act.wait_ge(st_sem, g * 64)
                            for c in range(EC):
                                last = nc.scalar.activation(qk[:, w, 0, c], psb[4 + 2 * w + c][:, :], ACT.Copy, scale=k)
                            last.then_inc(hi, 1)
                    if nx.exists():
                        act.wait_ge(x_T, nx.g + 1)
                        if gr.o >= 1:
                            act.wait_ge(q_mm, g)
                        for c in range(EC):
                            last = nc.scalar.activation(inT[:, nx.par, 0, 0, c], psb[c][:, :], ACT.Copy)
                        last.then_inc(x_hi, 1)
                        act.wait_ge(c_T, nx.g + 1)
                        if gr.o >= 1:
                            act.wait_ge(v_mm, g)
                        for c in range(EC):
                            last = nc.scalar.activation(inT[:, nx.par, 1, 0, c], psb[2 + c][:, :], ACT.Copy,
                                                        scale=sc[:, CTX:CTX + 1])
                        last.then_inc(c_hi, 1)
                    if gr.exists():
                        act.wait_ge(v_mm, g + 1)
                        if gr.o >= 1:
                            act.wait_ge(st_v, g * 16)
                        else:
                            act.wait_ge(ones_set, 1)
                        for b in range(G4):
                            last = nc.scalar.activation(
                                vS[:, b, 0, :, 0:D],
                                psb[4 + b // 2][:, (b % 2) * E:(b % 2 + 1) * E].rearrange("p (h d) -> p h d", h=H),
                                ACT.Copy, scale=2.0 ** -23)
                        last.then_inc(v_hi, 1)

                groups(act, body)

            @block.tensor
            def _(pe):
                def project(bank0, w, src):
                    for m in range(EC):
                        terms = [(a, b, c) for a, b in ((0, 0), (0, 1), (1, 0)) for c in range(EC)]
                        for n, (a, b, c) in enumerate(terms):
                            last = nc.tensor.matmul(psb[bank0 + m][:, :], WT[:, a, w, c, m * P:(m + 1) * P],
                                                    src[:, b, c], start=(n == 0), stop=(n == len(terms) - 1))
                    return last

                def body(gr):
                    nx, g = gr.next(1), gr.g
                    if gr.exists():
                        pe.wait_ge(x_split, g + 1)
                        if gr.o >= 1:
                            pe.wait_ge(v_split, g)
                        project(4, WQ, inT[:, gr.par, 0]).then_inc(q_mm, 1)
                        pe.wait_ge(c_split, g + 1)
                        if gr.o >= 1:
                            pe.wait_ge(k_split, g)
                        project(6, WK, inT[:, gr.par, 1]).then_inc(k_mm, 1)
                    if nx.exists():
                        pe.wait_ge(xh_done, nx.g + 1)
                        for c in range(EC):
                            for b in range(G4):
                                last = nc.tensor.transpose(psb[c][:, b * P:(b + 1) * P],
                                                           xh[nx.par][:, b, c * P:(c + 1) * P], identf[:, :])
                        last.then_inc(x_T, 1)
                        pe.wait_ge(c_copied, nx.g + 1)
                        for c in range(EC):
                            for b in range(G4):
                                last = nc.tensor.transpose(psb[2 + c][:, b * P:(b + 1) * P],
                                                           cst[:, b, c * P:(c + 1) * P], identf[:, :])
                        last.then_inc(c_T, 1)
                    if gr.exists():
                        pe.wait_ge(q_split, g + 1)
                        for b in range(G4):
                            terms = [(a, s, c) for a, s in ((0, 0), (0, 1), (1, 0)) for c in range(EC)]
                            for n, (a, s, c) in enumerate(terms):
                                last = nc.tensor.matmul(psb[4 + b // 2][:, (b % 2) * E:(b % 2 + 1) * E],
                                                        inT[:, gr.par, 1, s, c, b * P:(b + 1) * P], WT[:, a, WV, c, :],
                                                        start=(n == 0), stop=(n == len(terms) - 1))
                        last.then_inc(v_mm, 1)

                groups(pe, body)

        region_at[0] = aux_at[0] = 0
        NU = 2 * B
        UW = HH * P
        QK = [carve(2 * HH * P, F16).rearrange("p (w h n) -> p w h n", w=2, h=HH) for _ in range(4)]
        prob = [carve(UW, F32) for _ in range(2)]
        ph = carve(2 * 2 * UW, F16).rearrange("p (u s n) -> p u s n", u=2, s=2)
        VA = [beside(2 * 2 * H * VW, F16).rearrange("p (s k n) -> p s k n", s=2, k=2) for _ in range(2)]
        sel = beside(HH * P, F16).rearrange("p (h n) -> p h n", h=HH)
        mxu = beside(2 * 2 * HH, F32).rearrange("p (u n) -> p u n", u=2)
        negm = beside(2 * 4 * HH, F16).rearrange("p (u n) -> p u n", u=2)
        mT = beside(2 * P, F16).rearrange("p (u n) -> p u n", u=2)
        rec = beside(2 * 2 * HH, F32).rearrange("p (u n) -> p u n", u=2)
        ob = beside(2 * E, F32).rearrange("p (j n) -> p j n", j=2)
        oT = beside(2 * EC * P, F16).rearrange("p (s c n) -> p s c n", s=2, c=EC)
        otmp = beside(2 * HH * D, F32)
        S0, ST0, PO, OT, MI = 0, 2, 4, 6, 7
        (ld_s0, ld_s1, ld_s2, ld_s3, ld_v0, ld_v1, zeroed, sel_set, sel_done, scores, max_done, negm_done, m_T, m_copied, scoresT,
         exp_done, p_hi, p_split, pv_done, normed, o_T, o_hi, o_split, o_proj, x1_done, dchain,
         wp_hi, wp_split) = sems(
            "ld_s0", "ld_s1", "ld_s2", "ld_s3", "ld_v0", "ld_v1", "zeroed", "sel_set", "sel_done", "scores", "max_done", "negm_done",
            "m_T", "m_copied", "scoresT", "exp_done", "p_hi", "p_split", "pv_done", "normed", "o_T", "o_hi",
            "o_split", "o_proj", "x1_done", "dchain", "wp_hi", "wp_split")
        ld_s, ld_v = [ld_s0, ld_s1, ld_s2, ld_s3], [ld_v0, ld_v1]
        MSC = 2.0 ** 15
        TU = 8
        HEAD, TAIL, LAG = 8, 8, 5

        class Unit:
            def __init__(self, i, o):
                self.i, self.o = i, o
                self.u = i * TU + o
                self.h = o % 2
                self.b = i * (TU // 2) + o // 2
                self.j = (o // 2) % 2
                self.r = o % 4
                self.turn = i * (TU // 4) + o // 4

            def next(self, d):
                return Unit(self.i, self.o + d)

            def exists(self):
                return not isinstance(self.u, int) or 0 <= self.u < NU

        def units(eng, body):
            for o in range(-1, HEAD):
                body(Unit(0, o))
            with eng.Fori(0, (NU - HEAD - TAIL) // TU) as i:
                for o in range(HEAD, HEAD + TU):
                    body(Unit(i, o))
            for o in range(NU - TAIL, NU + LAG):
                body(Unit(0, o))

        def batches(eng, body):
            for j in range(2):
                body(j, 0, j, True)
            with eng.Fori(1, B // 2) as i:
                for j in range(2):
                    body(i * 2 + j, i, j, False)

        with nc.Block() as block:
            @block.sync
            def _(sp):
                sp.wait_ge(zeroed, 6)

                def stacks(un):
                    g, t = un.i + un.o // TU, (un.o // 2 % G4) * S
                    src = qkd[bass.ds(g, 1), :, :, un.h, :, :, t:t + S]
                    for w in range(2):
                        sp.dma_start(QK[un.r][0:D, w], src[:, w, :, w].rearrange("a d h n -> (a d) h n"))\
                            .then_inc(ld_s[un.r], 16)
                    sp.dma_start(QK[un.r][D:3 * D].rearrange("p w h n -> p (w h) n"),
                                 src.rearrange("a s d w h n -> (a s d) (w h) n")).then_inc(ld_s[un.r], 16)

                def values(un):
                    for kb in range(2):
                        sp.dma_start(VA[un.j][kb * BLK:(kb + 1) * BLK, :, kb],
                                     vd[bass.ds(un.b, 1), kb * BLK:(kb + 1) * BLK, :]
                                     .rearrange("a p (s n) -> (a p) s n", s=2)).then_inc(ld_v[un.j], 16)

                def body(un):
                    nxt = un.next(3)
                    if nxt.exists():
                        if un.o >= 1:
                            sp.wait_ge(scoresT, un.u * 2)
                        stacks(nxt)
                    if un.h == 0 and un.exists():
                        if un.o >= 4:
                            sp.wait_ge(pv_done, un.b * 2 - 2)
                        values(un)

                for o in range(2):
                    stacks(Unit(0, o))
                units(sp, body)

            @block.gpsimd
            def _(pool):
                for m in QK + VA:
                    nc.gpsimd.memset(m, 0.0).then_inc(zeroed, 1)
                nc.gpsimd.memset(mT, 0.0).then_inc(sel_set, 1)
                nc.gpsimd.memset(sel, 0.0).then_inc(sel_set, 1)
                pool.wait_ge(sel_set, 2)
                for s in range(2):
                    for kb in range(2):
                        v = sel[:, :, kb * BLK:(kb + 1) * BLK]
                        last = nc.gpsimd.affine_select(out=v, in_=v, compare_op=ALU.not_equal, fill=MSC,
                                                       base=-(s * 2 * HH + kb), pattern=[[-2, HH], [0, BLK]],
                                                       channel_multiplier=1)
                        last.then_inc(sel_set, 1)
                        pool.wait_ge(sel_set, 3 + s * 2 + kb)
                pool.sem_inc(sel_done, 1)

                def body(un):
                    done = un.next(-1)
                    if done.exists():
                        pool.wait_ge(p_hi, done.u + 1)
                        nc.gpsimd.tensor_tensor(ph[:, done.h, 1], prob[done.h], ph[:, done.h, 0], ALU.subtract)\
                            .then_inc(p_split, 1)

                units(pool, body)

            @block.vector
            def _(dve):
                def norm(un):
                    u, h = un.u, un.h
                    dve.wait_ge(pv_done, u + 1)
                    po = psb[PO + h][:, 0:HH * 2 * VW].rearrange("p (h k v) -> p h k v", h=HH, k=2)
                    r = rec[:, h, :].rearrange("p (h k) -> p h k", k=2)
                    t = otmp.rearrange("p (h k d) -> p h k d", h=HH, k=2)
                    o = ob[:, un.j, h * HH * D:(h + 1) * HH * D].rearrange("p (h d) -> p h d", d=D)
                    nc.vector.reciprocal(r, po[:, :, :, D]).then_inc(dchain, 1)
                    dve.wait_ge(dchain, u * 3 + 1)
                    nc.vector.tensor_tensor(r, r, wcoef[:, :].unsqueeze(1).broadcast_to([P, HH, 2]), ALU.mult)\
                        .then_inc(dchain, 1)
                    dve.wait_ge(dchain, u * 3 + 2)
                    nc.vector.tensor_tensor(t, po[:, :, :, 0:D], r.unsqueeze(3).broadcast_to([P, HH, 2, D]), ALU.mult)\
                        .then_inc(dchain, 1)
                    dve.wait_ge(dchain, u * 3 + 3)
                    if un.o >= 4:
                        dve.wait_ge(o_T, un.b - 1)
                    nc.vector.tensor_tensor(o, t[:, :, 0, :], t[:, :, 1, :], ALU.add).then_inc(normed, 1)

                def weights_lo(un, half):
                    N = PIECE // 2
                    if half == 0:
                        dve.wait_ge(wp_hi, un.b + 1)
                    nc.vector.scalar_tensor_tensor(
                        WS[:, bass.ds(un.b * (2 * PIECE) + (PIECE + half * N), N)],
                        WSF[:, bass.ds(un.b * PIECE + (PIECE + half * N), N)], wsc[:, bass.ds(un.b, 1)],
                        WS[:, bass.ds(un.b * (2 * PIECE) + half * N, N)], ALU.mult, ALU.subtract).then_inc(wp_split, 1)

                def body(un):
                    nx, done = un.next(1), un.next(-3)
                    if nx.exists():
                        u, h = nx.u, nx.h
                        for n in range(2):
                            dve.wait_ge(scores, u * 2 + (n + 1))
                            nc.vector.tensor_reduce(
                                mxu[:, h, n * HH:(n + 1) * HH],
                                psb[S0 + n][:, :].rearrange("p (g k) -> p g k", k=BLK), AX.X, ALU.max)\
                                .then_inc(max_done, 1)
                        dve.wait_ge(max_done, u * 2 + 2)
                        if nx.o >= 2:
                            dve.wait_ge(m_T, u - 1)
                        nc.vector.tensor_scalar(negm[:, h, 0:2 * HH], mxu[:, h, :], -1.0 / MSC, None, ALU.mult)\
                            .then_inc(negm_done, 1)
                        dve.wait_ge(negm_done, u * 2 + 1)
                        nc.vector.scalar_tensor_tensor(negm[:, h, 2 * HH:4 * HH], mxu[:, h, :], -1.0 / MSC,
                                                       negm[:, h, 0:2 * HH], ALU.mult, ALU.subtract)\
                            .then_inc(negm_done, 1)
                    if un.h == 1 and un.exists():
                        weights_lo(un, 0)
                    if un.h == 0 and un.next(-2).exists():
                        weights_lo(un.next(-2), 1)
                    if done.exists():
                        norm(done)
                    if un.h == 1:
                        ob_of = un.next(-5)
                        if ob_of.exists():
                            dve.wait_ge(o_hi, ob_of.b + 1)
                            nc.vector.tensor_tensor(oT[:, 1].rearrange("p c n -> p (c n)"), psb[OT][:, 0:E],
                                                    oT[:, 0].rearrange("p c n -> p (c n)"), ALU.subtract)\
                                .then_inc(o_split, 1)
                    else:
                        x_of = un.next(-6)
                        if x_of.exists():
                            dve.wait_ge(o_proj, x_of.b + 1)
                            xb = xres[:, x_of.b, :] if isinstance(x_of.b, int) else \
                                xres[:, bass.ds(x_of.b, 1), :].rearrange("p a e -> p (a e)")
                            nc.vector.scalar_tensor_tensor(xb, psb[OT][:, E:2 * E], s_res[:, :], xb, ALU.mult, ALU.add)\
                                .then_inc(x1_done, 1)

                units(dve, body)

            @block.scalar
            def _(act):
                act.wait_ge(sel_done, 1)

                def exps(un, n):
                    u, h = un.u, un.h
                    act.wait_ge(scoresT, u * 2 + (n + 1))
                    if n == 0 and un.o >= 2:
                        act.wait_ge(p_split, u - 1)
                    nc.scalar.activation(prob[h][:, n * 512:(n + 1) * 512], psb[ST0 + n][:, :], ACT.Exp,
                                         bias=pbias[:, :], scale=s_attn[:, :]).then_inc(exp_done, 1)

                def body(un):
                    pr = un.next(-1)
                    if pr.exists():
                        exps(pr, 0)
                    if un.exists():
                        u, h = un.u, un.h
                        act.wait_ge(m_T, u + 1)
                        if un.o >= 2:
                            act.wait_ge(scoresT, u * 2 - 2)
                        nc.scalar.activation(mT[0:4 * HH, h, :], psb[MI][0:4 * HH, 0:P // 2].bitcast(F16),
                                             ACT.Copy).then_inc(m_copied, 1)
                    if pr.exists():
                        exps(pr, 1)
                        act.wait_ge(exp_done, pr.u * 2 + 2)
                        if pr.o >= 2:
                            act.wait_ge(pv_done, pr.u - 1)
                        nc.scalar.activation(ph[:, pr.h, 0], prob[pr.h], ACT.Copy).then_inc(p_hi, 1)
                    if un.h == 1:
                        ob_of = un.next(-5)
                        if ob_of.exists():
                            act.wait_ge(o_T, ob_of.b + 1)
                            if ob_of.o >= 2:
                                act.wait_ge(o_proj, ob_of.b)
                            nc.scalar.activation(oT[:, 0].rearrange("p c n -> p (c n)"), psb[OT][:, 0:E], ACT.Copy)\
                                .then_inc(o_hi, 1)
                    if un.h == 0 and un.exists():
                        if un.o >= 2:
                            act.wait_ge(wp_split, un.b * 2)
                        nc.scalar.activation(WS[:, bass.ds(un.b * (2 * PIECE), PIECE)],
                                             WSF[:, bass.ds(un.b * PIECE + PIECE, PIECE)], ACT.Copy,
                                             scale=wsc[:, bass.ds(un.b, 1)]).then_inc(wp_hi, 1)

                units(act, body)

            @block.tensor
            def _(pe):
                pe.wait_ge(sel_done, 1)

                def body(un):
                    nx, done = un.next(1), un.next(-2)
                    if nx.exists():
                        pe.wait_ge(ld_s[nx.r], nx.turn * 48 + 48)
                        for hd in range(HH):
                            head = nx.h * HH + hd
                            n = hd // 4
                            if hd % 4 == 0 and nx.o >= 1:
                                pe.wait_ge(max_done, nx.u * 2 + (n - 1))
                            last = nc.tensor.matmul(psb[S0 + n][:, (hd % 4) * P:(hd % 4 + 1) * P],
                                                    QK[nx.r][:, 0, hd, :], QK[nx.r][:, 1, hd, :], start=True, stop=True)
                            if hd % 4 == 3:
                                last.then_inc(scores, 1)
                    if un.exists():
                        u, h = un.u, un.h
                        pe.wait_ge(negm_done, u * 2 + 2)
                        if un.o >= 1:
                            pe.wait_ge(m_copied, u)
                        nc.tensor.transpose(psb[MI][0:4 * HH, 0:P // 2].bitcast(F16), negm[:, h, :], identh[:, :])\
                            .then_inc(m_T, 1)
                    if un.h == 0:
                        p_of = un.next(-6)
                        if p_of.exists():
                            pe.wait_ge(o_split, p_of.b + 1)
                            terms = [(a, s, c) for a, s in ((0, 0), (0, 1), (1, 0)) for c in range(EC)]
                            for n, (a, s, c) in enumerate(terms):
                                last = nc.tensor.matmul(psb[OT][:, E:2 * E], oT[:, s, c], WT[:, a, WO, c, :],
                                                        start=(n == 0), stop=(n == len(terms) - 1))
                            last.then_inc(o_proj, 1)
                    if un.exists():
                        pe.wait_ge(m_copied, u + 1)
                        for hd in range(HH):
                            head = h * HH + hd
                            n = hd // 4
                            if hd % 4 == 0 and un.o >= 1:
                                pe.wait_ge(exp_done, u * 2 + (n - 1))
                            o = psb[ST0 + n][:, (hd % 4) * P:(hd % 4 + 1) * P]
                            nc.tensor.matmul(o, QK[un.r][:, 1, hd, :], QK[un.r][:, 0, hd, :], start=True, stop=False)
                            last = nc.tensor.matmul(o, sel[:, hd, :], mT[:, h, :], start=False, stop=True)
                            if hd % 4 == 3:
                                last.then_inc(scoresT, 1)
                    if done.exists():
                        if done.h == 0:
                            pe.wait_ge(ld_v[done.j], done.turn * 32 + 32)
                        if done.o >= 2:
                            pe.wait_ge(normed, done.u - 1)
                        pe.wait_ge(p_split, done.u + 1)
                        for hd in range(HH):
                            head = done.h * HH + hd
                            for n, (a, s) in enumerate(((0, 0), (1, 0), (0, 1))):
                                last = nc.tensor.matmul(psb[PO + done.h][:, hd * 2 * VW:(hd + 1) * 2 * VW],
                                                        ph[:, done.h, a, hd * P:(hd + 1) * P],
                                                        VA[done.j][:, s, :, head * VW:(head + 1) * VW],
                                                        start=(n == 0), stop=(n == 2))
                        last.then_inc(pv_done, 1)
                    if un.h == 1:
                        t_of = un.next(-5)
                        if t_of.exists():
                            pe.wait_ge(normed, t_of.b * 2 + 2)
                            if t_of.o >= 2:
                                pe.wait_ge(x1_done, t_of.b)
                            for c in range(EC):
                                last = nc.tensor.transpose(psb[OT][:, c * P:(c + 1) * P],
                                                           ob[:, t_of.j, c * P:(c + 1) * P], identf[:, :])
                            last.then_inc(o_T, 1)

                units(pe, body)

        region_at[0] = 0
        xn = [carve(G4 * E, F32).rearrange("p (b e) -> p b e", b=G4) for _ in range(2)]
        xrow = [carve(G4 * 2 * E, F16).rearrange("p (b s e) -> p b s e", b=G4, s=2) for _ in range(2)]
        xT2 = carve(G4 * 2 * E, F16).rearrange("p (b s c n) -> p b s c n", b=G4, s=2, c=EC)
        lg = carve(2 * G4 * NX, F32).rearrange("p (j b n) -> p j b n", j=2, b=G4)
        mx8 = carve(2 * G4 * 8, F32).rearrange("p (j b n) -> p j b n", j=2, b=G4)
        ix8 = carve(2 * G4 * 8, U32).rearrange("p (j b n) -> p j b n", j=2, b=G4)
        (bn2, mv2, sd2, rstd2, xn_done, xr_hi, xr_split, xr_T, xr_cp, lg_mm, lg_cp, mx_done, ix_done, top_done,
         st0, st1) = sems("bn2", "mv2", "sd2", "rstd2", "xn_done", "xr_hi", "xr_split", "xr_T", "xr_cp", "lg_mm",
                          "lg_cp", "mx_done", "ix_done", "top_done", "st0", "st1")
        st_ = [st0, st1]
        with nc.Block() as block:
            @block.vector
            def _(dve):
                def body(gr):
                    nx, done = gr.next(1), gr.next(-1)
                    if nx.exists():
                        for b in range(G4):
                            last = nc.vector.bn_stats(st[:, nx.par, b, :], nx.row(b))
                        last.then_inc(bn2, 1)
                        dve.wait_ge(bn2, nx.g + 1)
                        dve.sem_inc(passed_dve, 1)
                        for b in range(G4):
                            last = nc.vector.bn_aggr(mv[:, nx.par, b, :], st[:, nx.par, b, :])
                        last.then_inc(mv2, 1)
                    if done.exists():
                        j, g = done.par, done.g
                        dve.wait_ge(lg_mm, g + 1)
                        nc.vector.tensor_copy(lg[:, j].rearrange("p b n -> p (b n)"), psb[4][:, 0:G4 * NX])\
                            .then_inc(lg_cp, 1)
                        dve.wait_ge(lg_cp, g + 1)
                        dve.sem_inc(passed_dve, 1)
                        for b in range(G4):
                            last = nc.vector.max(mx8[:, j, b, :], lg[:, j, b, :])
                        last.then_inc(mx_done, 1)
                        dve.wait_ge(mx_done, g + 1)
                        dve.sem_inc(passed_dve, 1)
                        for b in range(G4):
                            last = nc.vector.max_index(ix8[:, j, b, :], mx8[:, j, b, :], lg[:, j, b, :])
                        last.then_inc(ix_done, 1)
                    if nx.exists():
                        dve.wait_ge(sd2, nx.g + 1)
                        nc.vector.reciprocal(rstd[:, nx.par, :], sd[:, nx.par, :]).then_inc(rstd2, 1)
                        dve.wait_ge(rstd2, nx.g + 1)
                        if nx.o >= 2:
                            dve.wait_ge(xr_split, nx.g - 1)
                        for b in range(G4):
                            last = nc.vector.tensor_scalar(xn[nx.par][:, b, :], nx.row(b), mv[:, nx.par, b, 0:1],
                                                           rstd[:, nx.par, b:b + 1], ALU.subtract, ALU.mult)
                        last.then_inc(xn_done, 1)
                    if done.exists():
                        dve.wait_ge(ix_done, g + 1)
                        dve.sem_inc(passed_dve, 1)
                        nc.vector.tensor_copy(MX[:, bass.ds(g * G4, G4), :], mx8[:, j, :, 0:2])
                        nc.vector.tensor_copy(IX[:, bass.ds(g * G4, G4), :], ix8[:, j, :, 0:2]).then_inc(top_done, 1)

                groups(dve, body, drain=1)

            @block.gpsimd
            def _(pool):
                def body(gr):
                    nx = gr.next(1)
                    if nx.exists():
                        pool.wait_ge(xr_hi, nx.g + 1)
                        nc.gpsimd.tensor_tensor(xrow[nx.par][:, :, 1, :], xn[nx.par], xrow[nx.par][:, :, 0, :],
                                                ALU.subtract).then_inc(xr_split, 1)

                groups(pool, body)

            @block.scalar
            def _(act):
                def body(gr):
                    nx, g = gr.next(1), gr.g
                    if nx.exists():
                        act.wait_ge(mv2, nx.g + 1)
                        nc.scalar.activation(sd[:, nx.par, :], mv[:, nx.par, :, 1], ACT.Sqrt, bias=eps1[:, :],
                                             scale=2.0 ** -22).then_inc(sd2, 1)
                        act.wait_ge(xn_done, nx.g + 1)
                        if nx.o >= 2:
                            act.wait_ge(lg_mm, nx.g - 1)
                            act.wait_ge(st_[nx.par], nx.turn * 16)
                        nc.scalar.activation(xrow[nx.par][:, :, 0, :], xn[nx.par], ACT.Copy).then_inc(xr_hi, 1)
                    if gr.exists():
                        act.wait_ge(xr_T, g + 1)
                        if gr.o >= 1:
                            act.wait_ge(lg_mm, g)
                        for n in range(2):
                            last = nc.scalar.activation(xT2[:, 2 * n:2 * n + 2].rearrange("p b s c n -> p (b s c n)"),
                                                        psb[n][:, :].bitcast(F16), ACT.Copy)
                        last.then_inc(xr_cp, 1)

                groups(act, body)

            @block.tensor
            def _(pe):
                def body(gr):
                    if not gr.exists():
                        return
                    g, j = gr.g, gr.par
                    pe.wait_ge(xr_split, g + 1)
                    if gr.o >= 1:
                        pe.wait_ge(xr_cp, g)
                    for b in range(G4):
                        bank = psb[b // 2][:, :].bitcast(F16).rearrange("p (b s c n) -> p b s c n", b=2, s=2, c=EC)
                        for s in range(2):
                            for c in range(EC):
                                last = nc.tensor.transpose(bank[:, b % 2, s, c, :], xrow[j][:, b, s, c * P:(c + 1) * P],
                                                           identh[:, :])
                    last.then_inc(xr_T, 1)
                    pe.wait_ge(xr_cp, g + 1)
                    if gr.o >= 1:
                        pe.wait_ge(lg_cp, g)
                    for b in range(G4):
                        terms = [(a, s, c) for a, s in ((0, 0), (0, 1), (1, 0)) for c in range(EC)]
                        for n, (a, s, c) in enumerate(terms):
                            last = nc.tensor.matmul(psb[4][:, b * NX:(b + 1) * NX], xT2[:, b, s, c, :], gT[:, a, c, :],
                                                    start=(n == 0), stop=(n == len(terms) - 1))
                    last.then_inc(lg_mm, 1)

                groups(pe, body)

            @block.sync
            def _(sp):
                def body(gr):
                    if gr.exists():
                        sp.wait_ge(xr_split, gr.g + 1)
                        sp.dma_start(xs[bass.ds(gr.g * (G4 * S), G4 * S), :].rearrange("(b p) n -> p b n", p=P),
                                     xrow[gr.par].rearrange("p b s e -> p b (s e)")).then_inc(st_[gr.par], 16)

                groups(sp, body)
                for j in range(2):
                    sp.wait_ge(st_[j], 16 * NG // 2)

        region_at[0] = 0
        upper = carve(P, F16)
        ones = carve(P, F16)
        zeros = carve(P, F16)
        iot = carve(LCOL, F16)
        iob = carve(B, F32)
        pval = carve(2, F32)
        lsT = carve(4 * LCOL, F16).rearrange("p (s n) -> p s n", s=4)
        lsR = carve(4 * 2 * P, F16).rearrange("p (s a n) -> p s a n", s=4, a=2)
        oh = carve(2 * B * NX, F32).rearrange("p (k b n) -> p k b n", k=2, b=B)
        Mh = carve(B * NX, F16)
        cum = carve(B * NX, F32)
        cex = carve(B * NX, F16)
        rsel = carve(2 * B * NX, F32).rearrange("p (k b n) -> p k b n", k=2, b=B)
        rk = carve(2 * B, F32)
        rki = carve(2 * 2 * B, I32).rearrange("p (a n) -> p a n", a=2)
        rr = carve(2 * B, F32).rearrange("p (k b) -> p k b", k=2)
        cc = carve(2 * B, F32).rearrange("p (k b) -> p k b", k=2)
        ew = carve(2 * B, F32).rearrange("p (k b) -> p k b", k=2)
        val = carve(LCOL, F32)
        isneg = carve(LCOL, F32)
        vali = carve(LCOL, I32)
        nti = carve(NX, I32)
        ntf = carve(NX, F32)
        ncum = carve(NX, F32)
        iotile = carve(NT, F32)
        cmp_ = carve(NT * NX, F32).rearrange("p (t n) -> p t n", n=NX)
        cmp2 = carve(NT * NX, F32).rearrange("p (t n) -> p t n", n=NX)
        et = carve(NT, F32)
        jt = carve(NT, F32)
        iota8 = iot[:, 0:NX]
        (io_set, io_done, tri_set, tri_done, rchain, c_mm, rank_mm, list_set, list_mm, exped, pchain, zd) = sems(
            "io_set", "io_done", "tri_set", "tri_done", "rchain", "c_mm", "rank_mm", "list_set", "list_mm",
            "exped", "pchain", "zd")
        with nc.Block() as block:
            @block.gpsimd
            def _(pool):
                nc.gpsimd.iota(iota_i[:, :], [[1, LCOL]], base=0, channel_multiplier=0).then_inc(io_set, 1)
                pool.wait_ge(io_set, 1)
                nc.gpsimd.tensor_copy(iot, iota_i[:, :]).then_inc(io_set, 1)
                nc.gpsimd.tensor_copy(iotile, iota_i[:, 0:NT]).then_inc(io_set, 1)
                pool.wait_ge(io_set, 3)
                nc.gpsimd.iota(iota_i[:, 0:B], [[256, B]], base=0, channel_multiplier=0).then_inc(io_set, 1)
                nc.gpsimd.iota(iota_i[:, B:B + 2], [[1, 2]], base=1, channel_multiplier=2).then_inc(io_set, 1)
                pool.wait_ge(io_set, 5)
                nc.gpsimd.tensor_copy(iob, iota_i[:, 0:B]).then_inc(io_set, 1)
                nc.gpsimd.tensor_copy(pval, iota_i[:, B:B + 2]).then_inc(io_set, 1)
                nc.gpsimd.memset(ones, 1.0).then_inc(io_set, 1)
                nc.gpsimd.memset(zeros, 0.0).then_inc(io_set, 1)
                nc.gpsimd.memset(upper, 1.0).then_inc(io_set, 1)
                pool.wait_ge(io_set, 10)
                nc.gpsimd.affine_select(out=upper, in_=upper, compare_op=ALU.is_ge, fill=0.0, base=-1,
                                        pattern=[[1, P]], channel_multiplier=-1).then_inc(io_done, 1)

            @block.vector
            def _(dve):
                n = [0]

                def link(ins):
                    n[0] += 1
                    ins.then_inc(rchain, 1)
                    dve.wait_ge(rchain, n[0])

                link(nc.vector.tensor_tensor(ew[:, 0, :], MX[:, :, 1], MX[:, :, 0], ALU.subtract))
                dve.wait_ge(io_done, 1)
                for k in range(2):
                    link(nc.vector.tensor_tensor(oh[:, k], iota8.unsqueeze(1).broadcast_to([P, B, NX]),
                                                 IX[:, :, k].unsqueeze(2).broadcast_to([P, B, NX]), ALU.is_equal))
                ohf = [oh[:, k].rearrange("p b n -> p (b n)") for k in range(2)]
                link(nc.vector.tensor_tensor(Mh, ohf[0], ohf[1], ALU.add))
                cumv = cum.rearrange("p (b n) -> p b n", n=NX)
                mv_ = Mh.rearrange("p (b n) -> p b n", n=NX)
                for e in range(NX):
                    last = nc.vector.tensor_tensor_scan(cumv[:, :, e], mv_[:, :, e], mv_[:, :, e], 0.0, ALU.add, ALU.bypass)
                link(last)
                nc.vector.tensor_tensor(cex, cum, Mh, ALU.subtract).then_inc(c_mm, 1)
                dve.wait_ge(exped, 1)
                link(nc.vector.tensor_scalar(ew[:, 0, :], ew[:, 1, :], 1.0, None, ALU.add))
                link(nc.vector.reciprocal(ew[:, 0, :], ew[:, 0, :]))
                link(nc.vector.tensor_scalar(coef[:, :, 0], ew[:, 0, :], s_out[:, :], None, ALU.mult))
                link(nc.vector.tensor_tensor(coef[:, :, 1], coef[:, :, 0], ew[:, 1, :], ALU.mult))
                dve.wait_ge(rank_mm, 1)
                for k in range(2):
                    link(nc.vector.tensor_tensor(rsel[:, k].rearrange("p b n -> p (b n)"), psb[0][:, 0:B * NX], ohf[k], ALU.mult))
                    link(nc.vector.tensor_reduce(rk[:, k * B:(k + 1) * B], rsel[:, k], AX.X, ALU.add))
                link(nc.vector.tensor_copy(rki[:, 0], rk))
                link(nc.vector.tensor_scalar(rki[:, 1], rki[:, 0], 7, None, ALU.logical_shift_right))
                link(nc.vector.tensor_scalar(rki[:, 0], rki[:, 0], P - 1, None, ALU.bitwise_and))
                link(nc.vector.tensor_copy(rr.rearrange("p k b -> p (k b)"), rki[:, 0]))
                link(nc.vector.tensor_copy(cc.rearrange("p k b -> p (k b)"), rki[:, 1]))
                for k in range(2):
                    link(nc.vector.scalar_tensor_tensor(cc[:, k], IX[:, :, k], float(TCOL), cc[:, k], ALU.mult, ALU.add))

                def body(b, i, j, first):
                    if not first:
                        dve.wait_ge(list_mm, b - 1)
                    for k in range(2):
                        s = 2 * j + k
                        r = rr[:, k, bass.ds(b, 1)]
                        c = cc[:, k, bass.ds(b, 1)]
                        nc.vector.tensor_scalar(lsR[:, s, 0], iot[:, 0:P], r, pval[:, k:k + 1], ALU.is_equal, ALU.mult)
                        nc.vector.tensor_scalar(lsR[:, s, 1], iot[:, 0:P], r, iob[:, bass.ds(b, 1)], ALU.is_equal, ALU.mult)
                        last = nc.vector.tensor_scalar(lsT[:, s], iot, c, None, ALU.is_equal)
                    last.then_inc(list_set, 1)

                batches(dve, body)

                link(nc.vector.tensor_scalar(ntf, psb[1][:, 0:NX], float(SLOTS - 1), None, ALU.add))
                link(nc.vector.tensor_copy(nti, ntf))
                link(nc.vector.tensor_scalar(nti, nti, int(math.log2(SLOTS)), None, ALU.logical_shift_right))
                link(nc.vector.tensor_copy(ntf, nti))
                link(nc.vector.tensor_tensor_scan(ncum, ntf, ntf, 0.0, ALU.add, ALU.bypass))
                link(nc.vector.tensor_tensor(cmp_, ncum.unsqueeze(1).broadcast_to([P, NT, NX]),
                                             iotile.unsqueeze(2).broadcast_to([P, NT, NX]), ALU.is_le))
                link(nc.vector.tensor_tensor(cmp2, cmp_, ntf.unsqueeze(1).broadcast_to([P, NT, NX]), ALU.mult))
                link(nc.vector.tensor_reduce(et, cmp_, AX.X, ALU.add))
                link(nc.vector.tensor_reduce(jt, cmp2, AX.X, ALU.add))
                link(nc.vector.tensor_tensor(jt, iotile, jt, ALU.subtract))
                link(nc.vector.tensor_scalar(jt, jt, float(SLOTS // P), None, ALU.mult))
                link(nc.vector.scalar_tensor_tensor(jt, et, float(TCOL), jt, ALU.mult, ALU.add))
                link(nc.vector.tensor_scalar(jt, jt, float(LCOL), None, ALU.min))
                link(nc.vector.tensor_scalar(et, et, float(NX - 1), None, ALU.min))
                nc.vector.tensor_copy(tmap[0:1, 0, 0:NT], et[0:1, :])
                link(nc.vector.tensor_copy(tmap[0:1, 1, 0:NT], jt[0:1, :]))

                dve.wait_ge(list_mm, B + 1)
                link(nc.vector.tensor_scalar(val, psb[2][:, 0:LCOL], -1.0, None, ALU.add))
                link(nc.vector.tensor_scalar(isneg, val, 0.0, float(4 * T), ALU.is_lt, ALU.mult))
                link(nc.vector.tensor_tensor(listT[:, 0:LCOL, 1], val, isneg, ALU.add))
                link(nc.vector.tensor_scalar(vali, val, 0.0, None, ALU.max))
                link(nc.vector.tensor_scalar(listT[:, 0:LCOL, 0], vali, 1, None, ALU.logical_shift_right))
                nc.vector.memset(listT[:, LCOL:LCOL + 2, 0], 0)
                link(nc.vector.memset(listT[:, LCOL:LCOL + 2, 1], 4 * T))

            @block.scalar
            def _(act):
                act.wait_ge(rchain, 1)
                nc.scalar.activation(ew[:, 1, :], ew[:, 0, :], ACT.Exp, bias=zero1[:, :], scale=s_gate[:, :]).then_inc(exped, 1)

            @block.tensor
            def _(pe):
                pe.wait_ge(c_mm, 1)
                nc.tensor.matmul(psb[0][:, 0:B * NX], upper, Mh, start=True, stop=False)
                nc.tensor.matmul(psb[0][:, 0:B * NX], ones, cex, start=False, stop=True)
                nc.tensor.matmul(psb[1][:, 0:NX], ones, cex[:, (B - 1) * NX:B * NX], start=True, stop=False)
                nc.tensor.matmul(psb[1][:, 0:NX], ones, Mh[:, (B - 1) * NX:B * NX], start=False, stop=True)\
                    .then_inc(rank_mm, 1)

                def body(b, i, j, first):
                    pe.wait_ge(list_set, b + 1)
                    for k in range(2):
                        for a in range(2):
                            last = nc.tensor.matmul(psb[2][:, 0:LCOL], lsR[:, 2 * j + k, a], lsT[:, 2 * j + k],
                                                    start=(first and j == 0 and k == 0 and a == 0), stop=False)
                    last.then_inc(list_mm, 1)

                batches(pe, body)
                nc.tensor.matmul(psb[2][:, 0:LCOL], zeros, lsT[:, 0], start=False, stop=True).then_inc(list_mm, 1)

        region_at[0] = 0
        hid = carve(2 * 2 * FC * SLOTS, F16).rearrange("p (u s f n) -> p u s f n", u=2, s=2, f=FC)
        gel = carve(2 * 512, F32).rearrange("p (u n) -> p u n", u=2)
        xT = carve(2 * 4 * SLOTS, F16).rearrange("p (u a n) -> p u a n", u=2, a=4)
        SH = SLOTS // P
        aux_at[0] = 0
        xg = [beside(SH * 2 * E, F16).rearrange("p (h n) -> p h n", h=SH) for _ in range(3)]
        ysb = [beside(SH * E, F32).rearrange("p (h n) -> p h n", h=SH) for _ in range(3)]
        (g_idx, g0, g1, g2, t_T, t_cp, h_mm, gel_done, h_hi, h_split, y_mm, y_cp, sc0, sc1, sc2) = sems(
            "g_idx", "g0", "g1", "g2", "t_T", "t_cp", "h_mm", "gel_done", "h_hi", "h_split", "y_mm", "y_cp",
            "sc0", "sc1", "sc2")
        gsem, ssem = [g0, g1, g2], [sc0, sc1, sc2]
        W2_AT = NX * EC * 2 * PIECE
        FH = PIECE // E
        NQ = FC // 2

        TP = 6
        PEEL = 3
        assert (NT - PEEL) % TP == 0

        class Tile:
            def __init__(self, i, o):
                self.i, self.o = i, o
                self.t = i * TP + o
                self.par, self.buf = o % 2, o % 3
                self.uses = i * (TP // 3) + o // 3

            def next(self, d):
                return Tile(self.i, self.o + d)

        def tiles(eng, body):
            for o in range(PEEL):
                body(Tile(0, o))
            with eng.Fori(0, (NT - PEEL) // TP) as i:
                for o in range(PEEL, PEEL + TP):
                    body(Tile(i, o))

        def at_least(tile, n):
            return tile.o >= n

        with nc.Block() as block:
            @block.gpsimd
            def _(pool):
                def fetch(tile):
                    r = tile.buf
                    col = pool.value_load(tmap[0:1, 1, bass.ds(tile.t, 1)], min_val=0, max_val=LCOL)
                    if at_least(tile, 3):
                        pool.wait_ge(ssem[r], tile.uses * (16 * SH))
                        pool.wait_ge(t_T, tile.t - 2)
                    nc.gpsimd.tensor_copy(gi[:, r, :].rearrange("p (h a) -> p h a", a=2), listT[:, bass.ds(col, SH), :])\
                        .then_inc(g_idx, 1)
                    pool.wait_ge(g_idx, tile.t + 1)
                    pool.sem_inc(passed_pool, 1)
                    for h in range(SH):
                        nc.gpsimd.indirect_dma_start(
                            out=xg[r][:, h, :], out_offset=None, in_=xs[:, :],
                            in_offset=bass.IndirectOffsetOnAxis(ap=gi[:, r, 2 * h:2 * h + 1].bitcast(U32), axis=0))\
                            .then_inc(gsem[r], 16)

                def scatter(tile):
                    r = tile.buf
                    pool.wait_ge(y_cp, tile.t + 1)
                    pool.sem_inc(passed_pool, 1)
                    for h in range(SH):
                        nc.gpsimd.indirect_dma_start(
                            out=ys[:, :],
                            out_offset=bass.IndirectOffsetOnAxis(ap=gi[:, r, 2 * h + 1:2 * h + 2].bitcast(U32), axis=0),
                            in_=ysb[r][:, h, :], in_offset=None, bounds_check=2 * T - 1, oob_is_err=False)\
                            .then_inc(ssem[r], 16)

                def body(tile):
                    fetch(tile)
                    if at_least(tile, 2):
                        scatter(tile.next(-2))

                tiles(pool, body)
                scatter(Tile(0, NT - 2))
                scatter(Tile(0, NT - 1))
                for r in range(3):
                    pool.wait_ge(ssem[r], 16 * SH * (NT // 3))

            @block.tensor
            def _(pe):
                def rows_T(tile):
                    pe.wait_ge(gsem[tile.buf], tile.uses * (16 * SH) + 16 * SH)
                    if at_least(tile, 1):
                        pe.wait_ge(t_cp, tile.t)
                    bank = psb[6][:, :].bitcast(F16).rearrange("p (a n) -> p a n", a=4)
                    for h in range(SH):
                        for a in range(4):
                            last = nc.tensor.transpose(bank[:, a, h * P:(h + 1) * P],
                                                       xg[tile.buf][:, h, a * P:(a + 1) * P], identh[:, :])
                    last.then_inc(t_T, 1)

                def expert(tile):
                    return pe.value_load(tmap[0:1, 0, bass.ds(tile.t, 1)], min_val=0, max_val=NX - 1)

                def hidden(tile, e):
                    pe.wait_ge(t_cp, tile.t + 1)
                    for q in range(NQ):
                        if at_least(tile, 1):
                            pe.wait_ge(gel_done, tile.t * NQ + (q + 1 - NQ))
                        for f in (2 * q, 2 * q + 1):
                            terms = [(a, s, c) for a, s in ((0, 0), (0, 1), (1, 0)) for c in range(EC)]
                            for n, (a, s, c) in enumerate(terms):
                                last = nc.tensor.matmul(psb[q][:, (f % 2) * SLOTS:(f % 2 + 1) * SLOTS],
                                                        WS[:, bass.ds(e * (2 * EC * PIECE) + ((2 * c + a) * PIECE + f * P), P)],
                                                        xT[:, tile.par, 2 * s + c, :],
                                                        start=(n == 0), stop=(n == len(terms) - 1))
                        last.then_inc(h_mm, 1)

                def output(tile, e):
                    if at_least(tile, 2):
                        pe.wait_ge(y_cp, tile.t - 1)
                    for h in range(SH):
                        terms = [(s, a, f) for f in range(FC) for s, a in ((0, 0), (0, 1), (1, 0))]
                        for n, (s, a, f) in enumerate(terms):
                            if h == 0 and n % (3 * FC // NQ) == 0:
                                pe.wait_ge(h_split, tile.t * NQ + (f // 2 + 1))
                            last = nc.tensor.matmul(psb[4 + tile.par][:, h * E:(h + 1) * E],
                                                    hid[:, tile.par, s, f, h * P:(h + 1) * P],
                                                    WS[:, bass.ds(e * (2 * EC * PIECE) + W2_AT + a * PIECE
                                                                  + f // FH * 2 * PIECE + f % FH * E, E)],
                                                    start=(n == 0), stop=(n == len(terms) - 1))
                    last.then_inc(y_mm, 1)

                def body(tile):
                    rows_T(tile)
                    if at_least(tile, 1):
                        before = tile.next(-1)
                        output(before, expert(before))
                    hidden(tile, expert(tile))

                tiles(pe, body)
                output(Tile(0, NT - 1), expert(Tile(0, NT - 1)))

            @block.scalar
            def _(act):
                def body(tile):
                    act.wait_ge(t_T, tile.t + 1)
                    if at_least(tile, 2):
                        act.wait_ge(h_mm, tile.t * NQ - NQ)
                    nc.scalar.activation(xT[:, tile.par].rearrange("p a n -> p (a n)"), psb[6][:, :].bitcast(F16), ACT.Copy)\
                        .then_inc(t_cp, 1)
                    for q in range(NQ):
                        act.wait_ge(h_mm, tile.t * NQ + (q + 1))
                        if at_least(tile, 1) or q >= 2:
                            act.wait_ge(h_split, tile.t * NQ + (q - 1))
                        nc.scalar.activation(gel[:, q % 2], psb[q][:, :], ACT.Gelu, bias=zero1[:, :], scale=s_pre[:, :])\
                            .then_inc(gel_done, 1)

                tiles(act, body)

            @block.vector
            def _(dve):
                def y_copy(tile):
                    dve.wait_ge(y_mm, tile.t + 1)
                    if at_least(tile, 3):
                        dve.wait_ge(ssem[tile.buf], tile.uses * (16 * SH))
                    nc.vector.tensor_copy(ysb[tile.buf].rearrange("p h n -> p (h n)"), psb[4 + tile.par][:, :])\
                        .then_inc(y_cp, 1)

                def body(tile):
                    if at_least(tile, 1):
                        y_copy(tile.next(-1))
                    for q in range(NQ):
                        dve.wait_ge(gel_done, tile.t * NQ + (q + 1))
                        hi = hid[:, tile.par, 0, 2 * q:2 * q + 2, :].rearrange("p f n -> p (f n)")
                        lo = hid[:, tile.par, 1, 2 * q:2 * q + 2, :].rearrange("p f n -> p (f n)")
                        nc.vector.tensor_scalar(hi, gel[:, q % 2], s_hid[:, :], None, ALU.mult).then_inc(h_hi, 1)
                        dve.wait_ge(h_hi, tile.t * NQ + (q + 1))
                        nc.vector.scalar_tensor_tensor(lo, gel[:, q % 2], s_hid[:, :], hi, ALU.mult, ALU.subtract)\
                            .then_inc(h_split, 1)

                tiles(dve, body)
                y_copy(Tile(0, NT - 1))

        ybuf = WSF[:, 0:B * 2 * E].rearrange("p (b k e) -> p b k e", b=B, k=2)
        obuf = WSF[:, B * 2 * E:B * 3 * E].rearrange("p (b e) -> p b e", b=B)
        NC8 = 8
        BB = B // NC8
        ysems = sems(*[f"y_ld{n}" for n in range(NC8)])
        c_one, c_done, out_st = sems("c_one", "c_done", "out_st")
        with nc.Block() as block:
            @block.sync
            def _(sp):
                for n in range(NC8):
                    sp.dma_start(ybuf[:, n * BB:(n + 1) * BB].rearrange("p b k e -> p b (k e)"),
                                 ys.rearrange("(b p k) e -> b p (k e)", p=P, k=2)[n * BB:(n + 1) * BB].rearrange("b p n -> p b n"))\
                        .then_inc(ysems[n], 16)
                for n in range(NC8):
                    sp.wait_ge(c_done, BB * (n + 1))
                    sp.dma_start(out[n * BB:(n + 1) * BB].rearrange("b s e -> s b e"), obuf[:, n * BB:(n + 1) * BB])\
                        .then_inc(out_st, 16)
                sp.wait_ge(out_st, 16 * NC8)

            @block.vector
            def _(dve):
                for n in range(NC8):
                    dve.wait_ge(ysems[n], 16)
                    for b in range(n * BB, (n + 1) * BB):
                        nc.vector.scalar_tensor_tensor(obuf[:, b], ybuf[:, b, 0], coef[:, b, 0:1], xres[:, b], ALU.mult, ALU.add)\
                            .then_inc(c_one, 1)
                    for b in range(n * BB, (n + 1) * BB):
                        dve.wait_ge(c_one, b + 1)
                        nc.vector.scalar_tensor_tensor(obuf[:, b], ybuf[:, b, 1], coef[:, b, 1:2], obuf[:, b], ALU.mult, ALU.add)\
                            .then_inc(c_done, 1)


_INS = ["x", "ctx_1024", "L0_xattn_Wq", "L0_xattn_Wk", "L0_xattn_Wv", "L0_xattn_Wo", "L0_ffn_gate_w", "L0_ffn_w1",
        "L0_ffn_w2"]


def kernel(**inputs):
    import numpy as _np
    import concourse.bacc as _bacc
    from concourse import mybir as _mybir
    from concourse.bass_utils import run_bass_kernel_spmd as _run

    nc = _bacc.Bacc("TRN2", target_bir_lowering=False, num_devices=1, dynamic_dma_scratch_size=4096)
    arrays, args = {}, []
    for name in _INS:
        a = _np.ascontiguousarray(inputs[name])
        arrays[f"in_{name}_dram"] = a
        args.append(nc.dram_tensor(f"in_{name}_dram", a.shape, _mybir.dt.from_np(a.dtype), kind="ExternalInput").ap())
    shape = arrays["in_x_dram"].shape
    out = nc.dram_tensor("out_0_dram", shape, _mybir.dt.from_np(_np.dtype("float32")), kind="ExternalOutput").ap()
    build(nc, *args, out)
    r = _run(nc, [arrays], core_ids=[0])
    return r.results[0]["out_0_dram"]
```

```python
import math
from contextlib import ExitStack

import concourse.bass as bass
import numpy as np
from concourse import mybir

F32, F16 = mybir.dt.float32, mybir.dt.float16
I32, U32 = mybir.dt.int32, mybir.dt.uint32
ACT, ALU, AX = mybir.ActivationFunctionType, mybir.AluOpType, mybir.AxisListType


def key_block_counts(batch_blocks):
    seq, block = 512, 64
    nb = seq // block
    total = nb * nb
    keep = int(total * (1.0 - 0.05))
    idx = [(i, i) for i in range(nb)]
    band = max(1, int(math.sqrt(keep - nb) / 2))
    for i in range(nb):
        for o in range(1, band + 1):
            if i + o < nb:
                idx += [(i, i + o), (i + o, i)]
            if i - o >= 0:
                idx.append((i, i - o))
    for skip in (2, 4, 8, 16):
        if len(idx) >= keep:
            break
        for i in range(0, nb - skip, skip):
            if len(idx) < keep:
                idx.append((i, i + skip))
                if len(idx) < keep:
                    idx.append((i + skip, i))
    pairs = sorted(set(idx))[:keep]
    counts = np.zeros((batch_blocks, batch_blocks), int)
    for r, c in pairs:
        if r < batch_blocks:
            counts[r, min(c, batch_blocks - 1)] += 1
    return counts


def build(nc, x, ctxt, wq, wk, wv, wo, gate_w, w1, w2, out):
    B, S, E = x.shape
    P = 128
    assert S == P and E == 2 * P
    EC = E // P
    D = 16
    H = E // D
    HH = H // 2
    BLK = 64
    NX = gate_w.shape[1]
    F = w1.shape[2]
    FC = F // P
    T = B * S
    G4 = 4
    NG = B // G4
    SLOTS = 256
    NT = 2 * T // SLOTS + NX - 1
    TCOL = T // P
    LCOL = NX * TCOL
    EPS = 1e-5
    VW = D + 1
    counts = key_block_counts(S // BLK)
    PIECE = F
    NPIECE = 2 * NX * EC
    P_SHIFT = 12
    assert NT % 3 == 0

    qkd = nc.dram_tensor("qk_split", (NG, 2, D, 2, 2, HH, G4 * S), F16).ap()
    vd = nc.dram_tensor("v_split", (B, S, 2 * H * VW), F16).ap()
    xs = nc.dram_tensor("x2_split", (T, 2 * E), F16).ap()
    ys = nc.dram_tensor("expert_out", (2 * T, E), F32).ap()

    ctx = ExitStack()
    with ctx:
        def sb(name, shape, dt):
            return ctx.enter_context(nc.sbuf_tensor(name, shape, dt))

        def pb(name):
            return ctx.enter_context(nc.psum_tensor(name, [P, 512], F32))

        WS = sb("expert_weights", [P, (NPIECE + 1) * 2 * PIECE], F16)
        WSF = WS[:, :].bitcast(F32)
        xres = sb("residual", [P, B, E], F32)
        wsc = sb("weight_scales", [P, NPIECE], F32)
        R = sb("phase_region", [P, 8192], F32)
        region_at = [0]

        def carve(n, dt):
            size = n * (4 if dt in (F32, I32, U32) else 2)
            a = region_at[0]
            region_at[0] += size // 4
            assert region_at[0] <= 8192
            v = R[:, a:region_at[0]]
            return v if dt == F32 else v.bitcast(dt)

        aux = sb("beside_region", [P, 3136], F32)
        aux_at = [0]

        def beside(n, dt):
            size = n * (4 if dt in (F32, I32, U32) else 2)
            a = aux_at[0]
            aux_at[0] += size // 4
            assert aux_at[0] <= 3136
            v = aux[:, a:aux_at[0]]
            return v if dt == F32 else v.bitcast(dt)

        identf = sb("identf", [P, P], F32)
        identh = sb("identh", [P, P], F16)
        absmax = sb("absmax", [P, 8], F32)
        gmax = sb("gmax", [P, 8], F32)
        pw = sb("pow2", [P, 8], F32)
        sc = sb("to_fp16_scale", [P, 8], F32)
        CTX, WQ, WK, WV, WO, WG, W1, W2 = 4, 0, 1, 2, 3, 5, 6, 7
        s_attn = sb("s_attn", [P, 1], F32)
        s_res = sb("s_res", [P, 1], F32)
        s_gate = sb("s_gate", [P, 1], F32)
        s_pre = sb("s_pre", [P, 1], F32)
        s_hid = sb("s_hid", [P, 1], F32)
        s_out = sb("s_out", [P, 1], F32)
        eps1 = sb("eps1", [P, 1], F32)
        pbias = sb("pbias", [P, 1], F32)
        zero1 = sb("zero1", [P, 1], F32)
        wcoef = sb("wcoef", [P, 2], F32)
        WT = sb("attn_weights", [P, 2, 4, EC, E], F16)
        gT = sb("gate_weights", [P, 2, EC, NX], F16)
        st = sb("bn_st", [P, 2, G4, 6], F32)
        mv = sb("bn_mv", [P, 2, G4, 2], F32)
        sd = sb("std", [P, 2, G4], F32)
        rstd = sb("rstd", [P, 2, G4], F32)
        nmr = sb("neg_mean_rstd", [P, 2, G4], F32)
        MX = sb("top_logit", [P, B, 2], F32)
        IX = sb("top_expert", [P, B, 2], F32)
        wt_region = WT[:].rearrange("p s w c n -> p (s w c n)").bitcast(I32)
        listT = wt_region[:, 0:2 * (LCOL + 2)].rearrange("p (n a) -> p n a", a=2)
        iota_i = wt_region[:, 2 * (LCOL + 2):2 * (LCOL + 2) + LCOL]
        gi = wt_region[:, 1024:1024 + 3 * 2 * SLOTS // P].rearrange("p (u n) -> p u n", u=3)
        tmap = sb("tile_map", [1, 2, NT + 1], I32)
        coef = sb("combine_coef", [P, B, 2], F32)
        psb = [pb(f"bank{i}") for i in range(8)]

        passed_dve = ctx.enter_context(nc.semaphore("passed_dve"))
        passed_pool = ctx.enter_context(nc.semaphore("passed_pool"))
        phases = iter("ABCDEFGHIJ")

        def sems(*names):
            tag = next(phases)
            return [ctx.enter_context(nc.semaphore(f"{tag}_{n}")) for n in names]

        def pow2_scales(dve, lo, hi, chain):
            n = [0]

            def link(ins):
                n[0] += 1
                ins.then_inc(chain, 1)
                dve.wait_ge(chain, n[0])

            link(nc.vector.tensor_scalar(pw[:, lo:hi], gmax[:, lo:hi], 2.0 ** -30, 2.0 ** 30, ALU.max, ALU.min))
            link(nc.vector.tensor_scalar(pw[:, lo:hi].bitcast(I32), pw[:, lo:hi].bitcast(I32),
                                         0x7F800000, None, ALU.bitwise_and))
            link(nc.vector.tensor_scalar(sc[:, lo:hi].bitcast(I32), pw[:, lo:hi].bitcast(I32),
                                         -1.0, float((254 + 14) << 23), ALU.mult, ALU.add))
            return link

        region_at[0] = 0
        wst = carve(4 * EC * E, F32).rearrange("p (w c n) -> p w c n", w=4, c=EC)
        gst = carve(EC * NX, F32).rearrange("p (c n) -> p c n", c=EC)
        cmax = carve(4, F32)
        ctx_all = WSF[:, (NPIECE + 1) * PIECE - B * E:(NPIECE + 1) * PIECE]
        (weights_in, gate_in, ctx_in0, ctx_in1, ctx_in2, ctx_in3, x_in0, x_in1, x_in2, x_in3,
         absmax_done, gmax_done, chain, scales_done, ident_set, ident_done, cmax_done,
         weights_T, weights_hi, weights_split, consts_done, gate_hi) = sems(
            "weights_in", "gate_in", "ctx_in0", "ctx_in1", "ctx_in2", "ctx_in3", "x_in0", "x_in1", "x_in2", "x_in3",
            "absmax_done", "gmax_done", "chain", "scales_done",
            "ident_set", "ident_done", "cmax_done", "weights_T", "weights_hi", "weights_split", "consts_done", "gate_hi")
        ctx_in, x_in = [ctx_in0, ctx_in1, ctx_in2, ctx_in3], [x_in0, x_in1, x_in2, x_in3]
        QB = B // 4
        with nc.Block() as block:
            @block.sync
            def _(sp):
                for n, w in enumerate((wq, wk, wv, wo)):
                    sp.dma_start(wst[:, n], w.rearrange("(c p) n -> p c n", p=P)).then_inc(weights_in, 16)
                sp.dma_start(gst, gate_w.rearrange("(c p) n -> p c n", p=P)).then_inc(gate_in, 16)
                for q in range(4):
                    sp.dma_start(ctx_all[:, q * QB * E:(q + 1) * QB * E].rearrange("p (b e) -> p b e", e=E),
                                 ctxt[q * QB:(q + 1) * QB].rearrange("b s e -> s b e")).then_inc(ctx_in[q], 16)
                for q in range(4):
                    sp.dma_start(xres[:, q * QB:(q + 1) * QB],
                                 x[q * QB:(q + 1) * QB].rearrange("b s e -> s b e")).then_inc(x_in[q], 16)

            @block.gpsimd
            def _(pool):
                nc.gpsimd.memset(zero1[:, :], 0.0).then_inc(consts_done, 1)
                for m in (identf, identh):
                    nc.gpsimd.memset(m[:, :], 0.0).then_inc(ident_set, 1)
                pool.wait_ge(ident_set, 2)
                for m in (identf, identh):
                    nc.gpsimd.affine_select(out=m[:, :], in_=m[:, :], compare_op=ALU.not_equal, fill=1.0, base=0,
                                            pattern=[[-1, P]], channel_multiplier=1).then_inc(ident_done, 1)
                nc.gpsimd.memset(eps1[:, :], EPS * 2.0 ** -22).then_inc(consts_done, 1)
                nc.gpsimd.memset(pbias[:, :], P_SHIFT * math.log(2.0)).then_inc(consts_done, 1)
                pool.wait_ge(consts_done, 3 + counts.size)
                pool.wait_ge(absmax_done, 3)
                nc.gpsimd.partition_all_reduce(gmax[:, 0:6], absmax[:, 0:6], P, bass.bass_isa.ReduceOp.max)\
                    .then_inc(gmax_done, 1)

            @block.vector
            def _(dve):
                for r in range(S // BLK):
                    for c in range(S // BLK):
                        nc.vector.memset(wcoef[r * BLK:(r + 1) * BLK, c:c + 1], float(counts[r, c]) / 8.0)\
                            .then_inc(consts_done, 1)
                dve.wait_ge(weights_in, 64)
                nc.vector.tensor_reduce(absmax[:, 0:4], wst.rearrange("p w c n -> p w (c n)"), AX.X, ALU.max,
                                        apply_absolute_value=True).then_inc(absmax_done, 1)
                dve.wait_ge(gate_in, 16)
                nc.vector.tensor_reduce(absmax[:, WG:WG + 1], gst, AX.XY, ALU.max,
                                        apply_absolute_value=True).then_inc(absmax_done, 1)
                for q in range(4):
                    dve.wait_ge(ctx_in[q], 16)
                    nc.vector.tensor_reduce(cmax[:, q:q + 1], ctx_all[:, q * QB * E:(q + 1) * QB * E], AX.X, ALU.max,
                                            apply_absolute_value=True).then_inc(cmax_done, 1)
                dve.wait_ge(cmax_done, 4)
                nc.vector.tensor_reduce(absmax[:, CTX:CTX + 1], cmax, AX.X, ALU.max).then_inc(absmax_done, 1)
                dve.wait_ge(gmax_done, 1)
                link = pow2_scales(dve, 0, 6, chain)
                nc.vector.tensor_tensor(s_gate[:, :], pw[:, WV:WV + 1], pw[:, WO:WO + 1], ALU.mult)
                link(nc.vector.tensor_tensor(s_attn[:, :], pw[:, WQ:WQ + 1], pw[:, WK:WK + 1], ALU.mult))
                nc.vector.tensor_scalar(s_res[:, :], s_gate[:, :], pw[:, CTX:CTX + 1], 2.0 ** -16, ALU.mult, ALU.mult)
                link(nc.vector.tensor_scalar(s_attn[:, :], s_attn[:, :], pw[:, CTX:CTX + 1],
                                             2.0 ** -7 * D ** -0.5, ALU.mult, ALU.mult))
                nc.vector.tensor_scalar(s_gate[:, :], pw[:, WG:WG + 1], 2.0 ** -25, None, ALU.mult)\
                    .then_inc(scales_done, 1)
                nc.vector.tensor_scalar(gT[:, 0], gst, sc[:, WG:WG + 1], None, ALU.mult).then_inc(gate_hi, 1)
                dve.wait_ge(gate_hi, 1)
                nc.vector.scalar_tensor_tensor(gT[:, 1], gst, sc[:, WG:WG + 1], gT[:, 0], ALU.mult, ALU.subtract)\
                    .then_inc(weights_split, 1)
                for n in range(4):
                    dve.wait_ge(weights_hi, n + 1)
                    nc.vector.scalar_tensor_tensor(
                        WT[:, 1, n].rearrange("p c n -> p (c n)"), psb[n][:, :], sc[:, n:n + 1],
                        WT[:, 0, n].rearrange("p c n -> p (c n)"), ALU.mult, ALU.subtract).then_inc(weights_split, 1)
                dve.wait_ge(weights_split, 5)

            @block.tensor
            def _(pe):
                pe.wait_ge(ident_done, 2)
                pe.wait_ge(weights_in, 64)
                for n in range(4):
                    for oc in range(EC):
                        for ic in range(EC):
                            last = nc.tensor.transpose(psb[n][:, ic * E + oc * P:ic * E + (oc + 1) * P],
                                                       wst[:, n, oc, ic * P:(ic + 1) * P], identf[:, :])
                    last.then_inc(weights_T, 1)

            @block.scalar
            def _(act):
                act.wait_ge(scales_done, 1)
                for n in range(4):
                    act.wait_ge(weights_T, n + 1)
                    nc.scalar.activation(WT[:, 0, n].rearrange("p c n -> p (c n)"), psb[n][:, :], ACT.Copy,
                                         scale=sc[:, n:n + 1]).then_inc(weights_hi, 1)

        region_at[0] = aux_at[0] = 0
        xh = carve(G4 * E, F32).rearrange("p (b e) -> p b e", b=G4)
        xhs = carve(2 * G4 * E, F16).rearrange("p (s b e) -> p s b e", s=2, b=G4)
        cst = carve(G4 * E, F32).rearrange("p (b e) -> p b e", b=G4)
        inT = carve(2 * 2 * 2 * EC * 512, F16).rearrange("p (u w s c n) -> p u w s c n", u=2, w=2, s=2, c=EC)
        qk = beside(2 * 2 * EC * 512, F16).rearrange("p (w s c n) -> p w s c n", w=2, s=2, c=EC)
        vS = beside(G4 * 2 * H * VW, F16).rearrange("p (b s h v) -> p b s h v", b=G4, s=2, h=H)
        CH = 2 * PIECE
        amx = carve(2 * NX, F32)
        assert 2 * NX == 2 * NG and G4 * E == PIECE
        (mv_done, sd_done, rstd_done, nmr_done, xh_done, xh_hi, xh_split, x_T, c_T, x_split, c_hi, c_split,
         q_mm, k_mm, v_mm, q_hi, k_hi, v_hi, q_split, k_split, v_split, st_q, st_k, st_v, ones_set, bn_done,
         c_copied, w_ld0, w_ld1, amx_done, w_absmax, w_gmax, wchain) = sems(
            "mv_done", "sd_done", "rstd_done", "nmr_done", "xh_done", "xh_hi", "xh_split", "x_T", "c_T", "x_split",
            "c_hi", "c_split", "q_mm", "k_mm", "v_mm", "q_hi", "k_hi", "v_hi", "q_split", "k_split", "v_split",
            "st_q", "st_k", "st_v", "ones_set", "bn_done", "c_copied", "w_ld0", "w_ld1", "amx_done",
            "w_absmax", "w_gmax", "wchain")
        w_ld = [w_ld0, w_ld1]

        class Group:
            def __init__(self, i, o):
                self.i, self.o = i, o
                self.g = i * 2 + o
                self.par = o % 2
                self.turn = i + o // 2

            def next(self, d):
                return Group(self.i, self.o + d)

            def exists(self):
                return not isinstance(self.g, int) or 0 <= self.g < NG

            def row(self, b):
                if isinstance(self.g, int):
                    return xres[:, self.g * G4 + b, :]
                return xres[:, bass.ds(self.g * G4 + b, 1), :].rearrange("p a e -> p (a e)")

        def groups(eng, body, drain=0):
            for o in range(-1, 2):
                body(Group(0, o))
            with eng.Fori(0, NG // 2 - 2) as i:
                for o in (2, 3):
                    body(Group(i, o))
            for o in range(NG - 2, NG + drain):
                body(Group(0, o))

        with nc.Block() as block:
            @block.sync
            def _(sp):
                def weight(w, m, gr):
                    sp.dma_start(
                        WSF[:, bass.ds((m * NX + gr.g) * CH + PIECE, CH)].rearrange("p (c n) -> p c n", n=w.shape[2]),
                        w[bass.ds(gr.g, 1)].rearrange("a (c p) n -> p (a c) n", p=P)).then_inc(w_ld[gr.par], 16)

                def body(gr):
                    nx, g = gr.next(1), gr.g
                    if nx.exists():
                        if gr.o >= 1:
                            sp.wait_ge(amx_done, g * 2)
                        weight(w1, 0, nx)
                        sp.wait_ge(c_T, nx.g + 1)
                        weight(w2, 1, nx)
                    if gr.exists():
                        for w, ready, st_sem in ((0, q_split, st_q), (1, k_split, st_k)):
                            sp.wait_ge(ready, g + 1)
                            for s in range(2):
                                for c in range(EC):
                                    sp.dma_start(qkd[bass.ds(g, 1), s ^ w, :, c, w]
                                                 .rearrange("a d h m -> (a h) d m"), qk[:, w, s, c]).then_inc(st_sem, 16)
                    if gr.exists():
                        sp.wait_ge(v_split, g + 1)
                        sp.dma_start(vd[bass.ds(g * G4, G4)].rearrange("b p n -> p b n"),
                                     vS.rearrange("p b s h v -> p b (s h v)")).then_inc(st_v, 16)

                groups(sp, body)
                sp.wait_ge(st_q, 16 * 4 * NG)
                sp.wait_ge(st_k, 16 * 4 * NG)
                sp.wait_ge(st_v, 16 * NG)

            @block.vector
            def _(dve):
                nc.vector.memset(vS[:, :, 0, :, D:VW], 1.0)
                nc.vector.memset(vS[:, :, 1, :, D:VW], 0.0).then_inc(ones_set, 1)

                def largest(gr, m):
                    dve.wait_ge(w_ld[gr.par], gr.turn * 32 + 32)
                    nc.vector.tensor_reduce(amx[:, bass.ds(gr.g + m * NX, 1)],
                                            WSF[:, bass.ds((m * NX + gr.g) * CH + PIECE, CH)], AX.X, ALU.max,
                                            apply_absolute_value=True).then_inc(amx_done, 1)

                def statistics(gr):
                    for q in range(4):
                        if not isinstance(gr.g, int) or q == gr.g // 2:
                            dve.wait_ge(x_in[q], 16)
                    for b in range(G4):
                        last = nc.vector.bn_stats(st[:, gr.par, b, :], gr.row(b))
                    last.then_inc(bn_done, 1)
                    dve.wait_ge(bn_done, gr.g + 1)
                    dve.sem_inc(passed_dve, 1)
                    for b in range(G4):
                        last = nc.vector.bn_aggr(mv[:, gr.par, b, :], st[:, gr.par, b, :])
                    last.then_inc(mv_done, 1)

                def factors(gr):
                    dve.wait_ge(sd_done, gr.g + 1)
                    nc.vector.reciprocal(rstd[:, gr.par, :], sd[:, gr.par, :]).then_inc(rstd_done, 1)
                    dve.wait_ge(rstd_done, gr.g + 1)
                    nc.vector.scalar_tensor_tensor(nmr[:, gr.par, :], mv[:, gr.par, :, 0], -1.0, rstd[:, gr.par, :],
                                                   ALU.mult, ALU.mult).then_inc(nmr_done, 1)

                def body(gr):
                    nx, g = gr.next(1), gr.g
                    if gr.exists():
                        largest(gr, 0)
                        for w, (hi, split, k) in enumerate(((q_hi, q_split, 2.0 ** -21), (k_hi, k_split, 2.0 ** -25))):
                            dve.wait_ge(hi, g + 1)
                            for c in range(EC):
                                last = nc.vector.scalar_tensor_tensor(qk[:, w, 1, c], psb[4 + 2 * w + c][:, :], k,
                                                                      qk[:, w, 0, c], ALU.mult, ALU.subtract)
                            last.then_inc(split, 1)
                    if nx.exists():
                        dve.wait_ge(c_hi, nx.g + 1)
                        for c in range(EC):
                            last = nc.vector.scalar_tensor_tensor(inT[:, nx.par, 1, 1, c], psb[2 + c][:, :],
                                                                  sc[:, CTX:CTX + 1], inT[:, nx.par, 1, 0, c],
                                                                  ALU.mult, ALU.subtract)
                        last.then_inc(c_split, 1)
                    if gr.next(2).exists():
                        statistics(gr.next(2))
                    if gr.exists():
                        largest(gr, 1)
                    if gr.next(2).exists():
                        factors(gr.next(2))
                    if gr.exists():
                        dve.wait_ge(v_hi, g + 1)
                        for b in range(G4):
                            last = nc.vector.scalar_tensor_tensor(
                                vS[:, b, 1, :, 0:D],
                                psb[6 + b // 2][:, (b % 2) * E:(b % 2 + 1) * E].rearrange("p (h d) -> p h d", h=H),
                                2.0 ** -23, vS[:, b, 0, :, 0:D], ALU.mult, ALU.subtract)
                        last.then_inc(v_split, 1)

                statistics(Group(0, 0))
                factors(Group(0, 0))
                groups(dve, body)
                dve.wait_ge(amx_done, 2 * NG)
                nc.vector.tensor_reduce(absmax[:, W1:W2 + 1], amx.rearrange("p (m n) -> p m n", m=2), AX.X, ALU.max)\
                    .then_inc(w_absmax, 1)
                dve.wait_ge(w_gmax, 1)
                link = pow2_scales(dve, W1, W2 + 1, wchain)
                link(nc.vector.tensor_scalar(s_pre[:, :], pw[:, W1:W1 + 1], 2.0 ** -25, None, ALU.mult))
                link(nc.vector.tensor_scalar(s_hid[:, :], sc[:, W1:W1 + 1], 2.0 ** -8, None, ALU.mult))
                link(nc.vector.tensor_tensor(s_out[:, :], pw[:, W1:W1 + 1], pw[:, W2:W2 + 1], ALU.mult))
                link(nc.vector.tensor_scalar(s_out[:, :], s_out[:, :], 2.0 ** -20, None, ALU.mult))
                for m in range(2):
                    link(nc.vector.tensor_copy(wsc[:, m * NX * EC:(m + 1) * NX * EC],
                                               sc[:, W1 + m:W1 + m + 1].broadcast_to([P, NX * EC])))

            @block.gpsimd
            def _(pool):
                def body(gr):
                    nx = gr.next(1)
                    if nx.exists():
                        if nx.o >= 1:
                            pool.wait_ge(c_T, nx.g)
                        nc.gpsimd.tensor_copy(cst.rearrange("p b e -> p (b e)"),
                                              ctx_all[:, bass.ds(nx.g * (G4 * E), G4 * E)]).then_inc(c_copied, 1)
                        pool.wait_ge(xh_hi, nx.g + 1)
                        nc.gpsimd.tensor_tensor(xhs[:, 1], xh, xhs[:, 0], ALU.subtract).then_inc(xh_split, 1)

                groups(pool, body)
                pool.wait_ge(w_absmax, 1)
                nc.gpsimd.partition_all_reduce(gmax[:, W1:W2 + 1], absmax[:, W1:W2 + 1], P, bass.bass_isa.ReduceOp.max)\
                    .then_inc(w_gmax, 1)

            @block.scalar
            def _(act):
                def deviation(gr):
                    act.wait_ge(mv_done, gr.g + 1)
                    nc.scalar.activation(sd[:, gr.par, :], mv[:, gr.par, :, 1], ACT.Sqrt, bias=eps1[:, :],
                                         scale=2.0 ** -22).then_inc(sd_done, 1)

                def body(gr):
                    nx, g = gr.next(1), gr.g
                    if nx.exists():
                        act.wait_ge(nmr_done, nx.g + 1)
                        if nx.o >= 1:
                            act.wait_ge(x_T, nx.g)
                        for b in range(G4):
                            last = nc.scalar.activation(xh[:, b, :], nx.row(b), ACT.Identity,
                                                        bias=nmr[:, nx.par, b:b + 1], scale=rstd[:, nx.par, b:b + 1])
                        last.then_inc(xh_done, 1)
                        act.wait_ge(xh_done, nx.g + 1)
                        nc.scalar.activation(xhs[:, 0], xh, ACT.Copy).then_inc(xh_hi, 1)
                    if gr.exists():
                        for w, (mm, hi, k, st_sem) in enumerate(((q_mm, q_hi, 2.0 ** -21, st_q),
                                                                 (k_mm, k_hi, 2.0 ** -25, st_k))):
                            act.wait_ge(mm, g + 1)
                            if gr.o >= 1:
                                act.wait_ge(st_sem, g * 64)
                            for c in range(EC):
                                last = nc.scalar.activation(qk[:, w, 0, c], psb[4 + 2 * w + c][:, :], ACT.Copy, scale=k)
                            last.then_inc(hi, 1)
                    if nx.exists():
                        act.wait_ge(c_T, nx.g + 1)
                        if gr.o >= 1:
                            act.wait_ge(v_mm, g)
                        for c in range(EC):
                            last = nc.scalar.activation(inT[:, nx.par, 1, 0, c], psb[2 + c][:, :], ACT.Copy,
                                                        scale=sc[:, CTX:CTX + 1])
                        last.then_inc(c_hi, 1)
                        act.wait_ge(x_T, nx.g + 1)
                        if gr.o >= 1:
                            act.wait_ge(q_mm, g)
                        for s in range(2):
                            last = nc.scalar.activation(inT[:, nx.par, 0, s].rearrange("p c n -> p (c n)"),
                                                        psb[s][:, :].bitcast(F16), ACT.Copy)
                        last.then_inc(x_split, 1)
                    if gr.next(2).exists():
                        deviation(gr.next(2))
                    if gr.exists():
                        act.wait_ge(v_mm, g + 1)
                        if gr.o >= 1:
                            act.wait_ge(st_v, g * 16)
                        else:
                            act.wait_ge(ones_set, 1)
                        for b in range(G4):
                            last = nc.scalar.activation(
                                vS[:, b, 0, :, 0:D],
                                psb[6 + b // 2][:, (b % 2) * E:(b % 2 + 1) * E].rearrange("p (h d) -> p h d", h=H),
                                ACT.Copy, scale=2.0 ** -23)
                        last.then_inc(v_hi, 1)

                deviation(Group(0, 0))
                groups(act, body)

            @block.tensor
            def _(pe):
                def project(bank0, w, src):
                    for m in range(EC):
                        terms = [(a, b, c) for a, b in ((0, 0), (0, 1), (1, 0)) for c in range(EC)]
                        for n, (a, b, c) in enumerate(terms):
                            last = nc.tensor.matmul(psb[bank0 + m][:, :], WT[:, a, w, c, m * P:(m + 1) * P],
                                                    src[:, b, c], start=(n == 0), stop=(n == len(terms) - 1))
                    return last

                def body(gr):
                    nx, g = gr.next(1), gr.g
                    if gr.exists():
                        pe.wait_ge(x_split, g + 1)
                        if gr.o >= 1:
                            pe.wait_ge(q_split, g)
                        project(4, WQ, inT[:, gr.par, 0]).then_inc(q_mm, 1)
                        pe.wait_ge(c_split, g + 1)
                        if gr.o >= 1:
                            pe.wait_ge(v_split, g)
                        project(6, WK, inT[:, gr.par, 1]).then_inc(k_mm, 1)
                    if nx.exists():
                        pe.wait_ge(c_copied, nx.g + 1)
                        for c in range(EC):
                            for b in range(G4):
                                last = nc.tensor.transpose(psb[2 + c][:, b * P:(b + 1) * P],
                                                           cst[:, b, c * P:(c + 1) * P], identf[:, :])
                        last.then_inc(c_T, 1)
                        pe.wait_ge(xh_split, nx.g + 1)
                        for s in range(2):
                            bank = psb[s][:, :].bitcast(F16).rearrange("p (c n) -> p c n", c=EC)
                            for c in range(EC):
                                for b in range(G4):
                                    last = nc.tensor.transpose(bank[:, c, b * P:(b + 1) * P],
                                                               xhs[:, s, b, c * P:(c + 1) * P], identh[:, :])
                        last.then_inc(x_T, 1)
                    if gr.exists():
                        pe.wait_ge(k_split, g + 1)
                        for b in range(G4):
                            terms = [(a, s, c) for a, s in ((0, 0), (0, 1), (1, 0)) for c in range(EC)]
                            for n, (a, s, c) in enumerate(terms):
                                last = nc.tensor.matmul(psb[6 + b // 2][:, (b % 2) * E:(b % 2 + 1) * E],
                                                        inT[:, gr.par, 1, s, c, b * P:(b + 1) * P], WT[:, a, WV, c, :],
                                                        start=(n == 0), stop=(n == len(terms) - 1))
                        last.then_inc(v_mm, 1)

                groups(pe, body)

        region_at[0] = aux_at[0] = 0
        NU = 2 * B
        UW = HH * P
        QK = [carve(2 * HH * P, F16).rearrange("p (w h n) -> p w h n", w=2, h=HH) for _ in range(4)]
        prob = [carve(UW, F32) for _ in range(2)]
        ph = carve(2 * 2 * UW, F16).rearrange("p (u s n) -> p u s n", u=2, s=2)
        VA = [beside(2 * 2 * H * VW, F16).rearrange("p (s k n) -> p s k n", s=2, k=2) for _ in range(2)]
        sel = beside(HH * P, F16).rearrange("p (h n) -> p h n", h=HH)
        mxu = beside(2 * 2 * HH, F32).rearrange("p (u n) -> p u n", u=2)
        negm = beside(2 * 4 * HH, F16).rearrange("p (u n) -> p u n", u=2)
        mT = beside(2 * P, F16).rearrange("p (u n) -> p u n", u=2)
        rec = beside(2 * 2 * HH, F32).rearrange("p (u n) -> p u n", u=2)
        ob = beside(2 * E, F32).rearrange("p (j n) -> p j n", j=2)
        oT = beside(2 * EC * P, F16).rearrange("p (s c n) -> p s c n", s=2, c=EC)
        otmp = beside(2 * HH * D, F32)
        S0, ST0, PO, OT, MI = 0, 2, 4, 6, 7
        (ld_s0, ld_s1, ld_s2, ld_s3, ld_v0, ld_v1, values_zeroed, qk_zeroed, sel_set, sel_done,
         scores, max_done, negm_done, m_T, m_copied, scoresT,
         exp_done, p_hi, p_split, pv_done, normed, o_T, o_hi, o_split, o_proj, x1_done, dchain, weighed,
         wp_hi, wp_split) = sems(
            "ld_s0", "ld_s1", "ld_s2", "ld_s3", "ld_v0", "ld_v1", "values_zeroed", "qk_zeroed", "sel_set", "sel_done",
            "scores", "max_done", "negm_done",
            "m_T", "m_copied", "scoresT", "exp_done", "p_hi", "p_split", "pv_done", "normed", "o_T", "o_hi",
            "o_split", "o_proj", "x1_done", "dchain", "weighed", "wp_hi", "wp_split")
        ld_s, ld_v = [ld_s0, ld_s1, ld_s2, ld_s3], [ld_v0, ld_v1]
        MSC = 2.0 ** 15
        HPC = PIECE // 2
        TU = 8
        HEAD, TAIL, LAG = 8, 8, 7

        class Unit:
            def __init__(self, i, o):
                self.i, self.o = i, o
                self.u = i * TU + o
                self.h = o % 2
                self.b = i * (TU // 2) + o // 2
                self.j = (o // 2) % 2
                self.r = o % 4
                self.turn = i * (TU // 4) + o // 4

            def next(self, d):
                return Unit(self.i, self.o + d)

            def exists(self):
                return not isinstance(self.u, int) or 0 <= self.u < NU

        def units(eng, body):
            for o in range(-1, HEAD):
                body(Unit(0, o))
            with eng.Fori(0, (NU - HEAD - TAIL) // TU) as i:
                for o in range(HEAD, HEAD + TU):
                    body(Unit(i, o))
            for o in range(NU - TAIL, NU + LAG):
                body(Unit(0, o))

        with nc.Block() as block:
            @block.sync
            def _(sp):
                def stacks(un):
                    if un.o < 4:
                        sp.wait_ge(qk_zeroed, un.o + 1)
                    g, t = un.i + un.o // TU, (un.o // 2 % G4) * S
                    src = qkd[bass.ds(g, 1), :, :, un.h, :, :, t:t + S]
                    for w in range(2):
                        sp.dma_start(QK[un.r][0:D, w], src[:, w, :, w].rearrange("a d h n -> (a d) h n"))\
                            .then_inc(ld_s[un.r], 16)
                    sp.dma_start(QK[un.r][D:3 * D].rearrange("p w h n -> p (w h) n"),
                                 src.rearrange("a s d w h n -> (a s d) (w h) n")).then_inc(ld_s[un.r], 16)

                def values(un):
                    if un.o == 0:
                        sp.wait_ge(values_zeroed, 2)
                    for kb in range(2):
                        sp.dma_start(VA[un.j][kb * BLK:(kb + 1) * BLK, :, kb],
                                     vd[bass.ds(un.b, 1), kb * BLK:(kb + 1) * BLK, :]
                                     .rearrange("a p (s n) -> (a p) s n", s=2)).then_inc(ld_v[un.j], 16)

                def body(un):
                    nxt = un.next(3)
                    if nxt.exists():
                        if un.o >= 1:
                            sp.wait_ge(scoresT, un.u * 2)
                        stacks(nxt)
                    if un.h == 0 and un.exists():
                        if un.o >= 4:
                            sp.wait_ge(pv_done, un.b * 2 - 2)
                        values(un)

                for o in range(2):
                    stacks(Unit(0, o))
                units(sp, body)

            @block.gpsimd
            def _(pool):
                nc.gpsimd.memset(mT, 0.0).then_inc(sel_set, 1)
                nc.gpsimd.memset(sel, 0.0).then_inc(sel_set, 1)
                pool.wait_ge(sel_set, 2)
                for s in range(2):
                    for kb in range(2):
                        v = sel[:, :, kb * BLK:(kb + 1) * BLK]
                        last = nc.gpsimd.affine_select(out=v, in_=v, compare_op=ALU.not_equal, fill=MSC,
                                                       base=-(s * 2 * HH + kb), pattern=[[-2, HH], [0, BLK]],
                                                       channel_multiplier=1)
                        last.then_inc(sel_set, 1)
                        pool.wait_ge(sel_set, 3 + s * 2 + kb)
                pool.sem_inc(sel_done, 1)
                for m in VA:
                    nc.gpsimd.memset(m, 0.0).then_inc(values_zeroed, 1)

                def body(un):
                    pr, done = un.next(-1), un.next(-3)
                    if done.exists():
                        pool.wait_ge(weighed, done.u + 1)
                        if done.o >= 4:
                            pool.wait_ge(o_T, done.b - 1)
                        t = otmp.rearrange("p (h k d) -> p h k d", h=HH, k=2)
                        o = ob[:, done.j, done.h * HH * D:(done.h + 1) * HH * D].rearrange("p (h d) -> p h d", d=D)
                        nc.gpsimd.tensor_tensor(o, t[:, :, 0, :], t[:, :, 1, :], ALU.add).then_inc(normed, 1)
                    if pr.exists():
                        pool.wait_ge(p_hi, pr.u + 1)
                        nc.gpsimd.tensor_tensor(ph[:, pr.h, 1], prob[pr.h], ph[:, pr.h, 0], ALU.subtract)\
                            .then_inc(p_split, 1)

                units(pool, body)

            @block.vector
            def _(dve):
                for m in QK:
                    nc.vector.memset(m, 0.0).then_inc(qk_zeroed, 1)

                def norm(un, step):
                    u, h = un.u, un.h
                    po = psb[PO + h][:, 0:HH * 2 * VW].rearrange("p (h k v) -> p h k v", h=HH, k=2)
                    r = rec[:, h, :].rearrange("p (h k) -> p h k", k=2)
                    t = otmp.rearrange("p (h k d) -> p h k d", h=HH, k=2)
                    if step == 0:
                        dve.wait_ge(pv_done, u + 1)
                        nc.vector.reciprocal(r, po[:, :, :, D]).then_inc(dchain, 1)
                    elif step == 1:
                        dve.wait_ge(dchain, u * 2 + 1)
                        nc.vector.tensor_tensor(r, r, wcoef[:, :].unsqueeze(1).broadcast_to([P, HH, 2]), ALU.mult)\
                            .then_inc(dchain, 1)
                    else:
                        dve.wait_ge(dchain, u * 2 + 2)
                        if un.o >= 1:
                            dve.wait_ge(normed, u)
                        nc.vector.tensor_tensor(t, po[:, :, :, 0:D], r.unsqueeze(3).broadcast_to([P, HH, 2, D]),
                                                ALU.mult).then_inc(weighed, 1)

                def weights_lo(un):
                    dve.wait_ge(wp_hi, un.u + 1)
                    nc.vector.scalar_tensor_tensor(
                        WS[:, bass.ds(un.b * (2 * PIECE) + (PIECE + un.h * HPC), HPC)],
                        WSF[:, bass.ds(un.b * PIECE + (PIECE + un.h * HPC), HPC)], wsc[:, bass.ds(un.b, 1)],
                        WS[:, bass.ds(un.b * (2 * PIECE) + un.h * HPC, HPC)], ALU.mult, ALU.subtract)\
                        .then_inc(wp_split, 1)

                def maximum(un, n):
                    dve.wait_ge(scores, un.u * 2 + (n + 1))
                    nc.vector.tensor_reduce(mxu[:, un.h, n * HH:(n + 1) * HH],
                                            psb[S0 + n][:, :].rearrange("p (g k) -> p g k", k=BLK), AX.X, ALU.max)\
                        .then_inc(max_done, 1)

                def body(un):
                    nx, done = un.next(1), un.next(-3)
                    if nx.exists():
                        maximum(nx, 0)
                    if done.exists():
                        norm(done, 0)
                    if nx.exists():
                        maximum(nx, 1)
                    if done.exists():
                        norm(done, 1)
                    if nx.exists():
                        u, h = nx.u, nx.h
                        dve.wait_ge(max_done, u * 2 + 2)
                        if nx.o >= 2:
                            dve.wait_ge(m_T, u - 1)
                        nc.vector.tensor_scalar(negm[:, h, 0:2 * HH], mxu[:, h, :], -1.0 / MSC, None, ALU.mult)\
                            .then_inc(negm_done, 1)
                    if done.exists():
                        norm(done, 2)
                    if nx.exists():
                        dve.wait_ge(negm_done, u * 2 + 1)
                        nc.vector.scalar_tensor_tensor(negm[:, h, 2 * HH:4 * HH], mxu[:, h, :], -1.0 / MSC,
                                                       negm[:, h, 0:2 * HH], ALU.mult, ALU.subtract)\
                            .then_inc(negm_done, 1)
                    x_of, ob_of = un.next(-8), un.next(-6)
                    if un.h == 0 and x_of.exists():
                        dve.wait_ge(o_proj, x_of.b + 1)
                        xb = xres[:, x_of.b, :] if isinstance(x_of.b, int) else \
                            xres[:, bass.ds(x_of.b, 1), :].rearrange("p a e -> p (a e)")
                        nc.vector.scalar_tensor_tensor(xb, psb[OT][:, E:2 * E], s_res[:, :], xb, ALU.mult, ALU.add)\
                            .then_inc(x1_done, 1)
                    if un.h == 0 and ob_of.exists():
                        dve.wait_ge(o_T, ob_of.b + 1)
                        if ob_of.o >= 2:
                            dve.wait_ge(o_proj, ob_of.b)
                        nc.vector.tensor_copy(oT[:, 0].rearrange("p c n -> p (c n)"), psb[OT][:, 0:E]).then_inc(o_hi, 1)
                    if un.next(-1).exists():
                        weights_lo(un.next(-1))
                    if un.h == 0 and ob_of.exists():
                        dve.wait_ge(o_hi, ob_of.b + 1)
                        nc.vector.tensor_tensor(oT[:, 1].rearrange("p c n -> p (c n)"), psb[OT][:, 0:E],
                                                oT[:, 0].rearrange("p c n -> p (c n)"), ALU.subtract).then_inc(o_split, 1)

                units(dve, body)

            @block.scalar
            def _(act):
                act.wait_ge(sel_done, 1)

                def exps(un, n):
                    u, h = un.u, un.h
                    act.wait_ge(scoresT, u * 2 + (n + 1))
                    if n == 0 and un.o >= 2:
                        act.wait_ge(p_split, u - 1)
                    nc.scalar.activation(prob[h][:, n * 512:(n + 1) * 512], psb[ST0 + n][:, :], ACT.Exp,
                                         bias=pbias[:, :], scale=s_attn[:, :]).then_inc(exp_done, 1)

                def body(un):
                    pr = un.next(-1)
                    if pr.exists():
                        exps(pr, 0)
                    if un.exists():
                        u, h = un.u, un.h
                        act.wait_ge(m_T, u + 1)
                        if un.o >= 2:
                            act.wait_ge(scoresT, u * 2 - 2)
                        nc.scalar.activation(mT[0:4 * HH, h, :], psb[MI][0:4 * HH, 0:P // 2].bitcast(F16),
                                             ACT.Copy).then_inc(m_copied, 1)
                    if pr.exists():
                        exps(pr, 1)
                        act.wait_ge(exp_done, pr.u * 2 + 2)
                        if pr.o >= 2:
                            act.wait_ge(pv_done, pr.u - 1)
                        nc.scalar.activation(ph[:, pr.h, 0], prob[pr.h], ACT.Copy).then_inc(p_hi, 1)
                    if un.exists():
                        if un.o >= 2:
                            act.wait_ge(wp_split, un.b * 2 - 1)
                        nc.scalar.activation(WS[:, bass.ds(un.b * (2 * PIECE) + un.h * HPC, HPC)],
                                             WSF[:, bass.ds(un.b * PIECE + (PIECE + un.h * HPC), HPC)], ACT.Copy,
                                             scale=wsc[:, bass.ds(un.b, 1)]).then_inc(wp_hi, 1)

                units(act, body)

            @block.tensor
            def _(pe):
                pe.wait_ge(sel_done, 1)

                def body(un):
                    nx, done = un.next(1), un.next(-2)
                    if nx.exists():
                        pe.wait_ge(ld_s[nx.r], nx.turn * 48 + 48)
                        for hd in range(HH):
                            head = nx.h * HH + hd
                            n = hd // 4
                            if hd % 4 == 0 and nx.o >= 1:
                                pe.wait_ge(max_done, nx.u * 2 + (n - 1))
                            last = nc.tensor.matmul(psb[S0 + n][:, (hd % 4) * P:(hd % 4 + 1) * P],
                                                    QK[nx.r][:, 0, hd, :], QK[nx.r][:, 1, hd, :], start=True, stop=True)
                            if hd % 4 == 3:
                                last.then_inc(scores, 1)
                    if un.exists():
                        u, h = un.u, un.h
                        pe.wait_ge(negm_done, u * 2 + 2)
                        if un.o >= 1:
                            pe.wait_ge(m_copied, u)
                        nc.tensor.transpose(psb[MI][0:4 * HH, 0:P // 2].bitcast(F16), negm[:, h, :], identh[:, :])\
                            .then_inc(m_T, 1)
                    if un.exists():
                        pe.wait_ge(m_copied, u + 1)
                        for hd in range(HH):
                            head = h * HH + hd
                            n = hd // 4
                            if hd % 4 == 0 and un.o >= 1:
                                pe.wait_ge(exp_done, u * 2 + (n - 1))
                            o = psb[ST0 + n][:, (hd % 4) * P:(hd % 4 + 1) * P]
                            nc.tensor.matmul(o, QK[un.r][:, 1, hd, :], QK[un.r][:, 0, hd, :], start=True, stop=False)
                            last = nc.tensor.matmul(o, sel[:, hd, :], mT[:, h, :], start=False, stop=True)
                            if hd % 4 == 3:
                                last.then_inc(scoresT, 1)
                    if done.exists():
                        if done.h == 0:
                            pe.wait_ge(ld_v[done.j], done.turn * 32 + 32)
                        if done.o >= 2:
                            pe.wait_ge(weighed, done.u - 1)
                        pe.wait_ge(p_split, done.u + 1)
                        for hd in range(HH):
                            head = done.h * HH + hd
                            for n, (a, s) in enumerate(((0, 0), (1, 0), (0, 1))):
                                last = nc.tensor.matmul(psb[PO + done.h][:, hd * 2 * VW:(hd + 1) * 2 * VW],
                                                        ph[:, done.h, a, hd * P:(hd + 1) * P],
                                                        VA[done.j][:, s, :, head * VW:(head + 1) * VW],
                                                        start=(n == 0), stop=(n == 2))
                        last.then_inc(pv_done, 1)
                    if un.h == 1:
                        t_of = un.next(-5)
                        if t_of.exists():
                            pe.wait_ge(normed, t_of.b * 2 + 2)
                            if t_of.o >= 2:
                                pe.wait_ge(o_split, t_of.b)
                            for c in range(EC):
                                last = nc.tensor.transpose(psb[OT][:, c * P:(c + 1) * P],
                                                           ob[:, t_of.j, c * P:(c + 1) * P], identf[:, :])
                            last.then_inc(o_T, 1)
                        p_of = un.next(-7)
                        if p_of.exists():
                            pe.wait_ge(o_split, p_of.b + 1)
                            if p_of.o >= 2:
                                pe.wait_ge(x1_done, p_of.b)
                            terms = [(a, s, c) for a, s in ((0, 0), (0, 1), (1, 0)) for c in range(EC)]
                            for n, (a, s, c) in enumerate(terms):
                                last = nc.tensor.matmul(psb[OT][:, E:2 * E], oT[:, s, c], WT[:, a, WO, c, :],
                                                        start=(n == 0), stop=(n == len(terms) - 1))
                            last.then_inc(o_proj, 1)

                units(pe, body)

        region_at[0] = 0
        upper = carve(P, F16)
        ones = carve(P, F16)
        zeros = carve(P, F16)
        iot = carve(LCOL, F16)
        iob = carve(B, F32)
        pval = carve(2, F32)
        iotile = carve(NT, F32)
        routing_at = region_at[0]
        xn = [carve(G4 * E, F32).rearrange("p (b e) -> p b e", b=G4) for _ in range(2)]
        xrow = [carve(G4 * 2 * E, F16).rearrange("p (b s e) -> p b s e", b=G4, s=2) for _ in range(2)]
        xT2 = carve(G4 * 2 * E, F16).rearrange("p (b s c n) -> p b s c n", b=G4, s=2, c=EC)
        lg = carve(2 * G4 * NX, F32).rearrange("p (j b n) -> p j b n", j=2, b=G4)
        mx8 = carve(2 * G4 * 8, F32).rearrange("p (j b n) -> p j b n", j=2, b=G4)
        ix8 = carve(2 * G4 * 8, U32).rearrange("p (j b n) -> p j b n", j=2, b=G4)
        (bn2, mv2, sd2, rstd2, xn_done, xr_hi, xr_split, xr_T, xr_cp, lg_mm, lg_cp, mx_done, ix_done,
         st0, st1, io_set, io_done) = sems("bn2", "mv2", "sd2", "rstd2", "xn_done", "xr_hi", "xr_split", "xr_T", "xr_cp", "lg_mm",
                          "lg_cp", "mx_done", "ix_done", "st0", "st1", "io_set", "io_done")
        st_ = [st0, st1]
        with nc.Block() as block:
            @block.vector
            def _(dve):
                def body(gr):
                    nx, done = gr.next(1), gr.next(-2)
                    j, g = done.par, done.g
                    if nx.exists():
                        for b in range(G4):
                            last = nc.vector.bn_stats(st[:, nx.par, b, :], nx.row(b))
                        last.then_inc(bn2, 1)
                    if done.exists():
                        dve.wait_ge(lg_mm, g + 1)
                        nc.vector.tensor_copy(lg[:, j].rearrange("p b n -> p (b n)"), psb[4 + j][:, 0:G4 * NX])\
                            .then_inc(lg_cp, 1)
                    if nx.exists():
                        dve.wait_ge(bn2, nx.g + 1)
                        dve.sem_inc(passed_dve, 1)
                        for b in range(G4):
                            last = nc.vector.bn_aggr(mv[:, nx.par, b, :], st[:, nx.par, b, :])
                        last.then_inc(mv2, 1)
                    if done.exists():
                        dve.wait_ge(lg_cp, g + 1)
                        dve.sem_inc(passed_dve, 1)
                        for b in range(G4):
                            last = nc.vector.max(mx8[:, j, b, :], lg[:, j, b, :])
                        last.then_inc(mx_done, 1)
                    if nx.exists():
                        dve.wait_ge(sd2, nx.g + 1)
                        nc.vector.reciprocal(rstd[:, nx.par, :], sd[:, nx.par, :]).then_inc(rstd2, 1)
                    if done.exists():
                        dve.wait_ge(mx_done, g + 1)
                        dve.sem_inc(passed_dve, 1)
                        for b in range(G4):
                            last = nc.vector.max_index(ix8[:, j, b, :], mx8[:, j, b, :], lg[:, j, b, :])
                        last.then_inc(ix_done, 1)
                    if nx.exists():
                        dve.wait_ge(rstd2, nx.g + 1)
                        if nx.o >= 2:
                            dve.wait_ge(xr_split, nx.g - 1)
                        for b in range(G4):
                            last = nc.vector.tensor_scalar(xn[nx.par][:, b, :], nx.row(b), mv[:, nx.par, b, 0:1],
                                                           rstd[:, nx.par, b:b + 1], ALU.subtract, ALU.mult)
                        last.then_inc(xn_done, 1)
                    if done.exists():
                        dve.wait_ge(ix_done, g + 1)
                        dve.sem_inc(passed_dve, 1)
                        nc.vector.tensor_copy(MX[:, bass.ds(g * G4, G4), :], mx8[:, j, :, 0:2])
                        nc.vector.tensor_copy(IX[:, bass.ds(g * G4, G4), :], ix8[:, j, :, 0:2])

                groups(dve, body, drain=2)

            @block.gpsimd
            def _(pool):
                nc.gpsimd.iota(iota_i[:, :], [[1, LCOL]], base=0, channel_multiplier=0).then_inc(io_set, 1)
                pool.wait_ge(io_set, 1)
                nc.gpsimd.tensor_copy(iot, iota_i[:, :]).then_inc(io_set, 1)
                nc.gpsimd.tensor_copy(iotile, iota_i[:, 0:NT]).then_inc(io_set, 1)
                pool.wait_ge(io_set, 3)
                nc.gpsimd.iota(iota_i[:, 0:B], [[256, B]], base=0, channel_multiplier=0).then_inc(io_set, 1)
                nc.gpsimd.iota(iota_i[:, B:B + 2], [[1, 2]], base=1, channel_multiplier=2).then_inc(io_set, 1)
                pool.wait_ge(io_set, 5)
                nc.gpsimd.tensor_copy(iob, iota_i[:, 0:B]).then_inc(io_set, 1)
                nc.gpsimd.tensor_copy(pval, iota_i[:, B:B + 2]).then_inc(io_set, 1)
                nc.gpsimd.memset(ones, 1.0).then_inc(io_set, 1)
                nc.gpsimd.memset(zeros, 0.0).then_inc(io_set, 1)
                nc.gpsimd.memset(upper, 1.0).then_inc(io_set, 1)
                pool.wait_ge(io_set, 10)
                nc.gpsimd.affine_select(out=upper, in_=upper, compare_op=ALU.is_ge, fill=0.0, base=-1,
                                        pattern=[[1, P]], channel_multiplier=-1).then_inc(io_done, 1)

                def body(gr):
                    nx = gr.next(1)
                    if nx.exists():
                        pool.wait_ge(xr_hi, nx.g + 1)
                        nc.gpsimd.tensor_tensor(xrow[nx.par][:, :, 1, :], xn[nx.par], xrow[nx.par][:, :, 0, :],
                                                ALU.subtract).then_inc(xr_split, 1)

                groups(pool, body)

            @block.scalar
            def _(act):
                def body(gr):
                    nx, g = gr.next(1), gr.g
                    if nx.exists():
                        act.wait_ge(mv2, nx.g + 1)
                        nc.scalar.activation(sd[:, nx.par, :], mv[:, nx.par, :, 1], ACT.Sqrt, bias=eps1[:, :],
                                             scale=2.0 ** -22).then_inc(sd2, 1)
                        act.wait_ge(xn_done, nx.g + 1)
                        if nx.o >= 2:
                            act.wait_ge(lg_mm, nx.g - 1)
                            act.wait_ge(st_[nx.par], nx.turn * 16)
                        nc.scalar.activation(xrow[nx.par][:, :, 0, :], xn[nx.par], ACT.Copy).then_inc(xr_hi, 1)
                    if gr.exists():
                        act.wait_ge(xr_T, g + 1)
                        if gr.o >= 1:
                            act.wait_ge(lg_mm, g)
                        for n in range(2):
                            last = nc.scalar.activation(xT2[:, 2 * n:2 * n + 2].rearrange("p b s c n -> p (b s c n)"),
                                                        psb[n][:, :].bitcast(F16), ACT.Copy)
                        last.then_inc(xr_cp, 1)

                groups(act, body)

            @block.tensor
            def _(pe):
                def body(gr):
                    if not gr.exists():
                        return
                    g, j = gr.g, gr.par
                    pe.wait_ge(xr_split, g + 1)
                    if gr.o >= 1:
                        pe.wait_ge(xr_cp, g)
                    for b in range(G4):
                        bank = psb[b // 2][:, :].bitcast(F16).rearrange("p (b s c n) -> p b s c n", b=2, s=2, c=EC)
                        for s in range(2):
                            for c in range(EC):
                                last = nc.tensor.transpose(bank[:, b % 2, s, c, :], xrow[j][:, b, s, c * P:(c + 1) * P],
                                                           identh[:, :])
                    last.then_inc(xr_T, 1)
                    pe.wait_ge(xr_cp, g + 1)
                    if gr.o >= 2:
                        pe.wait_ge(lg_cp, g - 1)
                    for b in range(G4):
                        terms = [(a, s, c) for a, s in ((0, 0), (0, 1), (1, 0)) for c in range(EC)]
                        for n, (a, s, c) in enumerate(terms):
                            last = nc.tensor.matmul(psb[4 + j][:, b * NX:(b + 1) * NX], xT2[:, b, s, c, :], gT[:, a, c, :],
                                                    start=(n == 0), stop=(n == len(terms) - 1))
                    last.then_inc(lg_mm, 1)

                groups(pe, body)

            @block.sync
            def _(sp):
                def body(gr):
                    if gr.exists():
                        sp.wait_ge(xr_split, gr.g + 1)
                        sp.dma_start(xs[bass.ds(gr.g * (G4 * S), G4 * S), :].rearrange("(b p) n -> p b n", p=P),
                                     xrow[gr.par].rearrange("p b s e -> p b (s e)")).then_inc(st_[gr.par], 16)

                groups(sp, body)
                for j in range(2):
                    sp.wait_ge(st_[j], 16 * NG // 2)

        region_at[0] = routing_at
        LB = 4
        lsT = carve(2 * LB * LCOL, F16).rearrange("p (s n) -> p s n", s=2 * LB)
        lsR = carve(2 * LB * 2 * P, F16).rearrange("p (a s n) -> p a s n", s=2 * LB, a=2)
        rowhot = carve(2 * LB * P, F16).rearrange("p (s n) -> p s n", s=2 * LB)
        oh = carve(2 * B * NX, F32).rearrange("p (k b n) -> p k b n", k=2, b=B)
        Mh = carve(B * NX, F16)
        cum = carve(B * NX, F32)
        cex = carve(B * NX, F16)
        rsel = carve(2 * B * NX, F32).rearrange("p (k b n) -> p k b n", k=2, b=B)
        rk = carve(2 * B, F32)
        rki = carve(2 * 2 * B, I32).rearrange("p (a n) -> p a n", a=2)
        rr = carve(2 * B, F32).rearrange("p (k b) -> p k b", k=2)
        cc = carve(2 * B, F32).rearrange("p (k b) -> p k b", k=2)
        ew = carve(2 * B, F32).rearrange("p (k b) -> p k b", k=2)
        val = carve(LCOL, F32)
        isneg = carve(LCOL, F32)
        vali = carve(LCOL, I32)
        nti = carve(NX, I32)
        ntf = carve(NX, F32)
        ncum = carve(NX, F32)
        cmp_ = carve(NT * NX, F32).rearrange("p (t n) -> p t n", n=NX)
        cmp2 = carve(NT * NX, F32).rearrange("p (t n) -> p t n", n=NX)
        et = carve(NT, F32)
        jt = carve(NT, F32)
        iota8 = iot[:, 0:NX]
        def batches(eng, body):
            for j in range(LB):
                body(j, j, True)
            with eng.Fori(1, B // LB) as i:
                for j in range(LB):
                    body(i * LB + j, j, False)

        (rchain, c_mm, rank_mm, list_set, list_mm, exped, row_set, row_scaled) = sems(
            "rchain", "c_mm", "rank_mm", "list_set", "list_mm",
            "exped", "row_set", "row_scaled")
        with nc.Block() as block:
            @block.vector
            def _(dve):
                n = [0]

                def link(ins):
                    n[0] += 1
                    ins.then_inc(rchain, 1)
                    dve.wait_ge(rchain, n[0])

                link(nc.vector.tensor_tensor(ew[:, 0, :], MX[:, :, 1], MX[:, :, 0], ALU.subtract))
                dve.wait_ge(io_done, 1)
                for k in range(2):
                    link(nc.vector.tensor_tensor(oh[:, k], iota8.unsqueeze(1).broadcast_to([P, B, NX]),
                                                 IX[:, :, k].unsqueeze(2).broadcast_to([P, B, NX]), ALU.is_equal))
                ohf = [oh[:, k].rearrange("p b n -> p (b n)") for k in range(2)]
                link(nc.vector.tensor_tensor(Mh, ohf[0], ohf[1], ALU.add))
                cumv = cum.rearrange("p (b n) -> p b n", n=NX)
                mv_ = Mh.rearrange("p (b n) -> p b n", n=NX)
                for e in range(NX):
                    last = nc.vector.tensor_tensor_scan(cumv[:, :, e], mv_[:, :, e], mv_[:, :, e], 0.0, ALU.add, ALU.bypass)
                link(last)
                nc.vector.tensor_tensor(cex, cum, Mh, ALU.subtract).then_inc(c_mm, 1)
                dve.wait_ge(exped, 1)
                link(nc.vector.tensor_scalar(ew[:, 0, :], ew[:, 1, :], 1.0, None, ALU.add))
                link(nc.vector.reciprocal(ew[:, 0, :], ew[:, 0, :]))
                link(nc.vector.tensor_scalar(coef[:, :, 0], ew[:, 0, :], s_out[:, :], None, ALU.mult))
                link(nc.vector.tensor_tensor(coef[:, :, 1], coef[:, :, 0], ew[:, 1, :], ALU.mult))
                dve.wait_ge(rank_mm, 1)
                for k in range(2):
                    link(nc.vector.tensor_tensor(rsel[:, k].rearrange("p b n -> p (b n)"), psb[0][:, 0:B * NX], ohf[k], ALU.mult))
                    link(nc.vector.tensor_reduce(rk[:, k * B:(k + 1) * B], rsel[:, k], AX.X, ALU.add))
                link(nc.vector.tensor_copy(rki[:, 0], rk))
                link(nc.vector.tensor_scalar(rki[:, 1], rki[:, 0], 7, None, ALU.logical_shift_right))
                link(nc.vector.tensor_scalar(rki[:, 0], rki[:, 0], P - 1, None, ALU.bitwise_and))
                link(nc.vector.tensor_copy(rr.rearrange("p k b -> p (k b)"), rki[:, 0]))
                link(nc.vector.tensor_copy(cc.rearrange("p k b -> p (k b)"), rki[:, 1]))
                for k in range(2):
                    link(nc.vector.scalar_tensor_tensor(cc[:, k], IX[:, :, k], float(TCOL), cc[:, k], ALU.mult, ALU.add))

                def body(b, j, first):
                    if not first:
                        dve.wait_ge(list_mm, b - (LB - 1))
                    for k in range(2):
                        s = 2 * j + k
                        r = rr[:, k, bass.ds(b, 1)]
                        c = cc[:, k, bass.ds(b, 1)]
                        last = nc.vector.tensor_scalar(rowhot[:, s], iot[:, 0:P], r, None, ALU.is_equal)
                        last.then_inc(row_set, 1)
                        last = nc.vector.tensor_scalar(lsT[:, s], iot, c, None, ALU.is_equal)
                    last.then_inc(list_set, 1)

                batches(dve, body)

                link(nc.vector.tensor_scalar(ntf, psb[1][:, 0:NX], float(SLOTS - 1), None, ALU.add))
                link(nc.vector.tensor_copy(nti, ntf))
                link(nc.vector.tensor_scalar(nti, nti, int(math.log2(SLOTS)), None, ALU.logical_shift_right))
                link(nc.vector.tensor_copy(ntf, nti))
                link(nc.vector.tensor_tensor_scan(ncum, ntf, ntf, 0.0, ALU.add, ALU.bypass))
                link(nc.vector.tensor_tensor(cmp_, ncum.unsqueeze(1).broadcast_to([P, NT, NX]),
                                             iotile.unsqueeze(2).broadcast_to([P, NT, NX]), ALU.is_le))
                link(nc.vector.tensor_tensor(cmp2, cmp_, ntf.unsqueeze(1).broadcast_to([P, NT, NX]), ALU.mult))
                link(nc.vector.tensor_reduce(et, cmp_, AX.X, ALU.add))
                link(nc.vector.tensor_reduce(jt, cmp2, AX.X, ALU.add))
                link(nc.vector.tensor_tensor(jt, iotile, jt, ALU.subtract))
                link(nc.vector.tensor_scalar(jt, jt, float(SLOTS // P), None, ALU.mult))
                link(nc.vector.scalar_tensor_tensor(jt, et, float(TCOL), jt, ALU.mult, ALU.add))
                link(nc.vector.tensor_scalar(jt, jt, float(LCOL), None, ALU.min))
                link(nc.vector.tensor_scalar(et, et, float(NX - 1), None, ALU.min))
                nc.vector.tensor_copy(tmap[0:1, 0, 0:NT], et[0:1, :])
                link(nc.vector.tensor_copy(tmap[0:1, 1, 0:NT], jt[0:1, :]))

                dve.wait_ge(list_mm, B + 1)
                link(nc.vector.tensor_scalar(val, psb[2][:, 0:LCOL], -1.0, None, ALU.add))
                link(nc.vector.tensor_scalar(isneg, val, 0.0, float(4 * T), ALU.is_lt, ALU.mult))
                link(nc.vector.tensor_tensor(listT[:, 0:LCOL, 1], val, isneg, ALU.add))
                link(nc.vector.tensor_scalar(vali, val, 0.0, None, ALU.max))
                link(nc.vector.tensor_scalar(listT[:, 0:LCOL, 0], vali, 1, None, ALU.logical_shift_right))
                nc.vector.memset(listT[:, LCOL:LCOL + 2, 0], 0)
                link(nc.vector.memset(listT[:, LCOL:LCOL + 2, 1], 4 * T))

            @block.scalar
            def _(act):
                act.wait_ge(rchain, 1)
                nc.scalar.activation(ew[:, 1, :], ew[:, 0, :], ACT.Exp, bias=zero1[:, :], scale=s_gate[:, :]).then_inc(exped, 1)

                def body(b, j, first):
                    for k in range(2):
                        s = 2 * j + k
                        act.wait_ge(row_set, b * 2 + (k + 1))
                        if not first and k == 0:
                            act.wait_ge(list_mm, b - (LB - 1))
                        nc.scalar.activation(lsR[:, 0, s], rowhot[:, s], ACT.Copy, scale=pval[:, k:k + 1])
                    nc.scalar.activation(lsR[:, 1, 2 * j:2 * j + 2], rowhot[:, 2 * j:2 * j + 2], ACT.Copy,
                                         scale=iob[:, bass.ds(b, 1)]).then_inc(row_scaled, 1)

                batches(act, body)

            @block.tensor
            def _(pe):
                pe.wait_ge(c_mm, 1)
                nc.tensor.matmul(psb[0][:, 0:B * NX], upper, Mh, start=True, stop=False)
                nc.tensor.matmul(psb[0][:, 0:B * NX], ones, cex, start=False, stop=True)
                nc.tensor.matmul(psb[1][:, 0:NX], ones, cex[:, (B - 1) * NX:B * NX], start=True, stop=False)
                nc.tensor.matmul(psb[1][:, 0:NX], ones, Mh[:, (B - 1) * NX:B * NX], start=False, stop=True)\
                    .then_inc(rank_mm, 1)

                def body(b, j, first):
                    pe.wait_ge(row_scaled, b + 1)
                    pe.wait_ge(list_set, b + 1)
                    for k in range(2):
                        for a in range(2):
                            last = nc.tensor.matmul(psb[2][:, 0:LCOL], lsR[:, a, 2 * j + k], lsT[:, 2 * j + k],
                                                    start=(first and j == 0 and k == 0 and a == 0), stop=False)
                    last.then_inc(list_mm, 1)

                batches(pe, body)
                nc.tensor.matmul(psb[2][:, 0:LCOL], zeros, lsT[:, 0], start=False, stop=True).then_inc(list_mm, 1)

        region_at[0] = 0
        hid = carve(2 * 2 * FC * SLOTS, F16).rearrange("p (u s f n) -> p u s f n", u=2, s=2, f=FC)
        gel = carve(2 * 512, F32).rearrange("p (u n) -> p u n", u=2)
        xT = carve(2 * 4 * SLOTS, F16).rearrange("p (u a n) -> p u a n", u=2, a=4)
        SH = SLOTS // P
        aux_at[0] = 0
        xg = [beside(SH * 2 * E, F16).rearrange("p (h n) -> p h n", h=SH) for _ in range(3)]
        ysb = [beside(SH * E, F32).rearrange("p (h n) -> p h n", h=SH) for _ in range(3)]
        (g_idx, g0, g1, g2, t_T, t_cp, h_mm, gel_done, h_hi, h_split, y_mm, y_cp, sc0, sc1, sc2) = sems(
            "g_idx", "g0", "g1", "g2", "t_T", "t_cp", "h_mm", "gel_done", "h_hi", "h_split", "y_mm", "y_cp",
            "sc0", "sc1", "sc2")
        gsem, ssem = [g0, g1, g2], [sc0, sc1, sc2]
        W2_AT = NX * EC * 2 * PIECE
        FH = PIECE // E
        NQ = FC // 2

        TP = 6
        PEEL = 3
        assert (NT - PEEL) % TP == 0

        class Tile:
            def __init__(self, i, o):
                self.i, self.o = i, o
                self.t = i * TP + o
                self.par, self.buf = o % 2, o % 3
                self.uses = i * (TP // 3) + o // 3

            def next(self, d):
                return Tile(self.i, self.o + d)

        def tiles(eng, body):
            for o in range(PEEL):
                body(Tile(0, o))
            with eng.Fori(0, (NT - PEEL) // TP) as i:
                for o in range(PEEL, PEEL + TP):
                    body(Tile(i, o))

        def at_least(tile, n):
            return tile.o >= n

        with nc.Block() as block:
            @block.gpsimd
            def _(pool):
                def fetch(tile):
                    r = tile.buf
                    col = pool.value_load(tmap[0:1, 1, bass.ds(tile.t, 1)], min_val=0, max_val=LCOL)
                    if at_least(tile, 3):
                        pool.wait_ge(ssem[r], tile.uses * (16 * SH))
                        pool.wait_ge(t_T, tile.t - 2)
                    nc.gpsimd.tensor_copy(gi[:, r, :].rearrange("p (h a) -> p h a", a=2), listT[:, bass.ds(col, SH), :])\
                        .then_inc(g_idx, 1)
                    pool.wait_ge(g_idx, tile.t + 1)
                    pool.sem_inc(passed_pool, 1)
                    for h in range(SH):
                        nc.gpsimd.indirect_dma_start(
                            out=xg[r][:, h, :], out_offset=None, in_=xs[:, :],
                            in_offset=bass.IndirectOffsetOnAxis(ap=gi[:, r, 2 * h:2 * h + 1].bitcast(U32), axis=0))\
                            .then_inc(gsem[r], 16)

                def scatter(tile):
                    r = tile.buf
                    pool.wait_ge(y_cp, tile.t + 1)
                    pool.sem_inc(passed_pool, 1)
                    for h in range(SH):
                        nc.gpsimd.indirect_dma_start(
                            out=ys[:, :],
                            out_offset=bass.IndirectOffsetOnAxis(ap=gi[:, r, 2 * h + 1:2 * h + 2].bitcast(U32), axis=0),
                            in_=ysb[r][:, h, :], in_offset=None, bounds_check=2 * T - 1, oob_is_err=False)\
                            .then_inc(ssem[r], 16)

                def body(tile):
                    fetch(tile)
                    if at_least(tile, 2):
                        scatter(tile.next(-2))

                tiles(pool, body)
                scatter(Tile(0, NT - 2))
                scatter(Tile(0, NT - 1))
                for r in range(3):
                    pool.wait_ge(ssem[r], 16 * SH * (NT // 3))

            @block.tensor
            def _(pe):
                def rows_T(tile):
                    pe.wait_ge(gsem[tile.buf], tile.uses * (16 * SH) + 16 * SH)
                    if at_least(tile, 1):
                        pe.wait_ge(t_cp, tile.t)
                    bank = psb[6][:, :].bitcast(F16).rearrange("p (a n) -> p a n", a=4)
                    for h in range(SH):
                        for a in range(4):
                            last = nc.tensor.transpose(bank[:, a, h * P:(h + 1) * P],
                                                       xg[tile.buf][:, h, a * P:(a + 1) * P], identh[:, :])
                    last.then_inc(t_T, 1)

                def expert(tile):
                    return pe.value_load(tmap[0:1, 0, bass.ds(tile.t, 1)], min_val=0, max_val=NX - 1)

                def hidden(tile, e):
                    pe.wait_ge(t_cp, tile.t + 1)
                    for q in range(NQ):
                        if at_least(tile, 1):
                            pe.wait_ge(gel_done, tile.t * NQ + (q + 1 - NQ))
                        for f in (2 * q, 2 * q + 1):
                            terms = [(a, s, c) for a, s in ((0, 0), (0, 1), (1, 0)) for c in range(EC)]
                            for n, (a, s, c) in enumerate(terms):
                                last = nc.tensor.matmul(psb[q][:, (f % 2) * SLOTS:(f % 2 + 1) * SLOTS],
                                                        WS[:, bass.ds(e * (2 * EC * PIECE) + ((2 * c + a) * PIECE + f * P), P)],
                                                        xT[:, tile.par, 2 * s + c, :],
                                                        start=(n == 0), stop=(n == len(terms) - 1))
                        last.then_inc(h_mm, 1)

                def output(tile, e):
                    if at_least(tile, 2):
                        pe.wait_ge(y_cp, tile.t - 1)
                    for h in range(SH):
                        terms = [(s, a, f) for f in range(FC) for s, a in ((0, 0), (0, 1), (1, 0))]
                        for n, (s, a, f) in enumerate(terms):
                            if h == 0 and n % (3 * FC // NQ) == 0:
                                pe.wait_ge(h_split, tile.t * NQ + (f // 2 + 1))
                            last = nc.tensor.matmul(psb[4 + tile.par][:, h * E:(h + 1) * E],
                                                    hid[:, tile.par, s, f, h * P:(h + 1) * P],
                                                    WS[:, bass.ds(e * (2 * EC * PIECE) + W2_AT + a * PIECE
                                                                  + f // FH * 2 * PIECE + f % FH * E, E)],
                                                    start=(n == 0), stop=(n == len(terms) - 1))
                    last.then_inc(y_mm, 1)

                def body(tile):
                    rows_T(tile)
                    if at_least(tile, 1):
                        before = tile.next(-1)
                        output(before, expert(before))
                    hidden(tile, expert(tile))

                tiles(pe, body)
                output(Tile(0, NT - 1), expert(Tile(0, NT - 1)))

            @block.scalar
            def _(act):
                def body(tile):
                    act.wait_ge(t_T, tile.t + 1)
                    if at_least(tile, 2):
                        act.wait_ge(h_mm, tile.t * NQ - NQ)
                    nc.scalar.activation(xT[:, tile.par].rearrange("p a n -> p (a n)"), psb[6][:, :].bitcast(F16), ACT.Copy)\
                        .then_inc(t_cp, 1)
                    for q in range(NQ):
                        act.wait_ge(h_mm, tile.t * NQ + (q + 1))
                        if at_least(tile, 1) or q >= 2:
                            act.wait_ge(h_split, tile.t * NQ + (q - 1))
                        nc.scalar.activation(gel[:, q % 2], psb[q][:, :], ACT.Gelu, bias=zero1[:, :], scale=s_pre[:, :])\
                            .then_inc(gel_done, 1)

                tiles(act, body)

            @block.vector
            def _(dve):
                def y_copy(tile):
                    dve.wait_ge(y_mm, tile.t + 1)
                    if at_least(tile, 3):
                        dve.wait_ge(ssem[tile.buf], tile.uses * (16 * SH))
                    nc.vector.tensor_copy(ysb[tile.buf].rearrange("p h n -> p (h n)"), psb[4 + tile.par][:, :])\
                        .then_inc(y_cp, 1)

                def body(tile):
                    if at_least(tile, 1):
                        y_copy(tile.next(-1))
                    for q in range(NQ):
                        dve.wait_ge(gel_done, tile.t * NQ + (q + 1))
                        hi = hid[:, tile.par, 0, 2 * q:2 * q + 2, :].rearrange("p f n -> p (f n)")
                        lo = hid[:, tile.par, 1, 2 * q:2 * q + 2, :].rearrange("p f n -> p (f n)")
                        nc.vector.tensor_scalar(hi, gel[:, q % 2], s_hid[:, :], None, ALU.mult).then_inc(h_hi, 1)
                        dve.wait_ge(h_hi, tile.t * NQ + (q + 1))
                        nc.vector.scalar_tensor_tensor(lo, gel[:, q % 2], s_hid[:, :], hi, ALU.mult, ALU.subtract)\
                            .then_inc(h_split, 1)

                tiles(dve, body)
                y_copy(Tile(0, NT - 1))

        ybuf = WSF[:, 0:B * 2 * E].rearrange("p (b k e) -> p b k e", b=B, k=2)
        obuf = WSF[:, B * 2 * E:B * 3 * E].rearrange("p (b e) -> p b e", b=B)
        NC8 = 8
        BB = B // NC8
        ysems = sems(*[f"y_ld{n}" for n in range(NC8)])
        c_one, c_done, out_st = sems("c_one", "c_done", "out_st")
        with nc.Block() as block:
            @block.sync
            def _(sp):
                for n in range(NC8):
                    sp.dma_start(ybuf[:, n * BB:(n + 1) * BB].rearrange("p b k e -> p b (k e)"),
                                 ys.rearrange("(b p k) e -> b p (k e)", p=P, k=2)[n * BB:(n + 1) * BB].rearrange("b p n -> p b n"))\
                        .then_inc(ysems[n], 16)
                for n in range(NC8):
                    sp.wait_ge(c_done, BB * (n + 1))
                    sp.dma_start(out[n * BB:(n + 1) * BB].rearrange("b s e -> s b e"), obuf[:, n * BB:(n + 1) * BB])\
                        .then_inc(out_st, 16)
                sp.wait_ge(out_st, 16 * NC8)

            @block.vector
            def _(dve):
                for n in range(NC8):
                    dve.wait_ge(ysems[n], 16)
                    for b in range(n * BB, (n + 1) * BB):
                        nc.vector.scalar_tensor_tensor(obuf[:, b], ybuf[:, b, 0], coef[:, b, 0:1], xres[:, b], ALU.mult, ALU.add)\
                            .then_inc(c_one, 1)
                    for b in range(n * BB, (n + 1) * BB):
                        dve.wait_ge(c_one, b + 1)
                        nc.vector.scalar_tensor_tensor(obuf[:, b], ybuf[:, b, 1], coef[:, b, 1:2], obuf[:, b], ALU.mult, ALU.add)\
                            .then_inc(c_done, 1)


_INS = ["x", "ctx_1024", "L0_xattn_Wq", "L0_xattn_Wk", "L0_xattn_Wv", "L0_xattn_Wo", "L0_ffn_gate_w", "L0_ffn_w1",
        "L0_ffn_w2"]


def kernel(**inputs):
    import numpy as _np
    import concourse.bacc as _bacc
    from concourse import mybir as _mybir
    from concourse.bass_utils import run_bass_kernel_spmd as _run

    nc = _bacc.Bacc("TRN2", target_bir_lowering=False, num_devices=1, dynamic_dma_scratch_size=4096)
    arrays, args = {}, []
    for name in _INS:
        a = _np.ascontiguousarray(inputs[name])
        arrays[f"in_{name}_dram"] = a
        args.append(nc.dram_tensor(f"in_{name}_dram", a.shape, _mybir.dt.from_np(a.dtype), kind="ExternalInput").ap())
    shape = arrays["in_x_dram"].shape
    out = nc.dram_tensor("out_0_dram", shape, _mybir.dt.from_np(_np.dtype("float32")), kind="ExternalOutput").ap()
    build(nc, *args, out)
    r = _run(nc, [arrays], core_ids=[0])
    return r.results[0]["out_0_dram"]
```
